# Optimizing a Trainium2 kernel written in Bass

```python
import numpy as np
import jax
import jax.numpy as jnp

def _softmax(x, axis=-1):
    return jax.nn.softmax(x, axis=axis)

def _gelu(x):
    return jax.nn.gelu(x, approximate=True)

def _silu(x):
    return jax.nn.silu(x)

def _sigmoid(x):
    return jax.nn.sigmoid(x)

def _layernorm(x, axis=-1, eps=1e-05):
    m = jnp.mean(x, axis=axis, keepdims=True)
    v = jnp.var(x, axis=axis, keepdims=True)
    return (x - m) / jnp.sqrt(v + eps)

def _scatter_add(tgt, idx, src, axis=0):
    return tgt.at[idx].add(src)

def _segment_sum(src, seg, n):
    return jax.ops.segment_sum(src, seg, n)
kernel_name = 'mk_seq_postln_d1_jaxref_r4_31288a'

def setup_inputs(seed: int=0):
    np.random.seed(seed)
    _w = jnp.asarray

    def _L0_attn_setup():
        import math
        import jax, jax.numpy as jnp
        import numpy as np
        B, S, D, H = (2, 512, 256, 16)
        HD = D // H
        LAMBDA_MAX = 0.5
        AMP_EPS = 1e-06

        def _amp_norm(t):
            a = jax.nn.softplus(t)
            return a / jnp.sqrt(jnp.mean(a * a, axis=-1, keepdims=True) + AMP_EPS)
        key = jax.random.key(seed)
        ks = jax.random.split(key, 8)
        x = jax.random.normal(ks[0], (B, S, D), jnp.float32)
        w = lambda k, std: std * jax.random.normal(k, (D, D), jnp.float32)
        return {'x': x, 'Wq': w(ks[1], 0.02), 'Wk': w(ks[2], 0.02), 'Wv': w(ks[3], 0.02), 'Wo': w(ks[4], 0.02), 'Wqp': w(ks[5], 0.005), 'Wkp': w(ks[6], 0.005), 'lambda_raw': jnp.full((H,), float(np.arctanh(0.5)), jnp.float32)}
    _L0_attn_in = _L0_attn_setup()

    def _L0_ffn_setup():
        import jax, jax.numpy as jnp
        import numpy as np
        DIM = 256
        HID = 512
        OUT = 256
        NE = 8
        TOPK = 2

        def _xavier(key, shape):
            fan_in, fan_out = (shape[-2], shape[-1])
            lim = jnp.sqrt(6.0 / (fan_in + fan_out))
            return jax.random.uniform(key, shape, jnp.float32, -lim, lim)
        key = jax.random.key(seed)
        ks = jax.random.split(key, 8)
        X = jax.random.normal(ks[0], (4, 256, DIM), jnp.float32)
        W1 = _xavier(ks[1], (NE, DIM, HID))
        W3 = _xavier(ks[2], (NE, DIM, HID))
        W2 = _xavier(ks[3], (NE, HID, OUT))
        b1 = jnp.zeros((NE, HID), jnp.float32)
        b3 = jnp.zeros((NE, HID), jnp.float32)
        b2 = jnp.zeros((NE, OUT), jnp.float32)
        Wg = _xavier(ks[4], (DIM, NE))
        bg = jnp.zeros((NE,), jnp.float32)
        Wf = _xavier(ks[5], (OUT, OUT))
        bf = jnp.zeros((OUT,), jnp.float32)
        return {'X': X, 'W1': W1, 'b1': b1, 'W3': W3, 'b3': b3, 'W2': W2, 'b2': b2, 'Wg': Wg, 'bg': bg, 'Wf': Wf, 'bf': bf}
    _L0_ffn_in = _L0_ffn_setup()
    _d = {'L0_attn_x': _L0_attn_in['x'], 'L0_attn_Wq': _L0_attn_in['Wq'], 'L0_attn_Wk': _L0_attn_in['Wk'], 'L0_attn_Wv': _L0_attn_in['Wv'], 'L0_attn_Wo': _L0_attn_in['Wo'], 'L0_attn_Wqp': _L0_attn_in['Wqp'], 'L0_attn_Wkp': _L0_attn_in['Wkp'], 'L0_attn_lambda_raw': _L0_attn_in['lambda_raw'], 'L0_ffn_W1': _L0_ffn_in['W1'], 'L0_ffn_b1': _L0_ffn_in['b1'], 'L0_ffn_W3': _L0_ffn_in['W3'], 'L0_ffn_b3': _L0_ffn_in['b3'], 'L0_ffn_W2': _L0_ffn_in['W2'], 'L0_ffn_b2': _L0_ffn_in['b2'], 'L0_ffn_Wg': _L0_ffn_in['Wg'], 'L0_ffn_bg': _L0_ffn_in['bg'], 'L0_ffn_Wf': _L0_ffn_in['Wf'], 'L0_ffn_bf': _L0_ffn_in['bf']}
    _x0 = _d['L0_attn_x']
    _d['L0_attn_x'] = jax.random.normal(jax.random.fold_in(jax.random.key(seed), 1), (2, 2048, 256), dtype=_x0.dtype)
    del _x0
    return _d

def reference(L0_attn_x, L0_attn_Wq, L0_attn_Wk, L0_attn_Wv, L0_attn_Wo, L0_attn_Wqp, L0_attn_Wkp, L0_attn_lambda_raw, L0_ffn_W1, L0_ffn_b1, L0_ffn_W3, L0_ffn_b3, L0_ffn_W2, L0_ffn_b2, L0_ffn_Wg, L0_ffn_bg, L0_ffn_Wf, L0_ffn_bf):

    def _L0_attn_ref(x, Wq, Wk, Wv, Wo, Wqp, Wkp, lambda_raw):
        import math
        import jax, jax.numpy as jnp
        import numpy as np
        B, S, D, H = (2, 512, 256, 16)
        HD = D // H
        LAMBDA_MAX = 0.5
        AMP_EPS = 1e-06

        def _amp_norm(t):
            a = jax.nn.softplus(t)
            return a / jnp.sqrt(jnp.mean(a * a, axis=-1, keepdims=True) + AMP_EPS)
        b, s, d = x.shape
        split = lambda t: t.reshape(b, s, H, HD)
        q = split(x @ Wq)
        k = split(x @ Wk)
        v = split(x @ Wv)
        scale = 1.0 / math.sqrt(HD)
        scores_dot = jnp.einsum('bihd,bjhd->bhij', q, k) * scale
        q_amp = _amp_norm(q)
        k_amp = _amp_norm(k)
        q_phi = math.pi * jnp.tanh(split(x @ Wqp))
        k_phi = math.pi * jnp.tanh(split(x @ Wkp))
        q_cos = q_amp * jnp.cos(q_phi)
        q_sin = q_amp * jnp.sin(q_phi)
        k_cos = k_amp * jnp.cos(k_phi)
        k_sin = k_amp * jnp.sin(k_phi)
        scores_phase = (jnp.einsum('bihd,bjhd->bhij', q_cos, k_cos) + jnp.einsum('bihd,bjhd->bhij', q_sin, k_sin)) * scale
        lam = (LAMBDA_MAX * jnp.tanh(lambda_raw))[None, :, None, None]
        scores = scores_dot + lam * scores_phase
        causal = jnp.tril(jnp.ones((s, s), bool))
        scores = jnp.where(causal[None, None], scores, -jnp.inf)
        attn = jax.nn.softmax(scores, axis=-1)
        out = jnp.einsum('bhij,bjhd->bihd', attn, v).reshape(b, s, d)
        return out @ Wo

    def _L0_ffn_ref(X, W1, b1, W3, b3, W2, b2, Wg, bg, Wf, bf):
        import jax, jax.numpy as jnp
        import numpy as np
        DIM = 256
        HID = 512
        OUT = 256
        NE = 8
        TOPK = 2

        def _xavier(key, shape):
            fan_in, fan_out = (shape[-2], shape[-1])
            lim = jnp.sqrt(6.0 / (fan_in + fan_out))
            return jax.random.uniform(key, shape, jnp.float32, -lim, lim)
        gating = jax.nn.softmax(X @ Wg + bg, axis=-1)
        top_k_indices = jnp.argsort(gating, axis=-1)[..., -TOPK:]
        h1 = jnp.einsum('bsd,edh->bseh', X, W1) + b1
        h3 = jnp.einsum('bsd,edh->bseh', X, W3) + b3
        h = jax.nn.silu(h1 * h3)
        expert_outputs = jnp.einsum('bseh,eho->bseo', h, W2) + b2
        topk_out = jnp.take_along_axis(expert_outputs, top_k_indices[..., None], axis=2)
        topk_w = jnp.take_along_axis(gating, top_k_indices, axis=-1)
        mixed = jnp.sum(topk_w[..., None] * topk_out, axis=2)
        return mixed @ Wf + bf
    x = L0_attn_x
    x = _layernorm(x + _L0_attn_ref(x, L0_attn_Wq, L0_attn_Wk, L0_attn_Wv, L0_attn_Wo, L0_attn_Wqp, L0_attn_Wkp, L0_attn_lambda_raw), axis=-1)
    x = _layernorm(x + _L0_ffn_ref(x, L0_ffn_W1, L0_ffn_b1, L0_ffn_W3, L0_ffn_b3, L0_ffn_W2, L0_ffn_b2, L0_ffn_Wg, L0_ffn_bg, L0_ffn_Wf, L0_ffn_bf), axis=-1)
    return x

_drawn_inputs = setup_inputs


def setup_inputs(seed=0):
    import zlib

    import numpy as np

    out = dict(_drawn_inputs(seed))
    spreads = {'L0_attn_lambda_raw': (0.5493061542510986, 0.6),
     'L0_ffn_b1': (0.0, 0.273),
     'L0_ffn_b3': (0.0, 0.275),
     'L0_ffn_b2': (0.0, 0.1),
     'L0_ffn_bg': (0.0, 0.1),
     'L0_ffn_bf': (0.0, 0.1)}
    factors = {'L0_attn_Wq': 8.0,
     'L0_attn_Wk': 8.0,
     'L0_attn_Wv': 5.633,
     'L0_attn_Wo': 5.587,
     'L0_attn_Wqp': 8.0,
     'L0_attn_Wkp': 8.0}
    for name, (base, spread) in spreads.items():
        noise = np.random.default_rng([zlib.crc32(name.encode()), seed]).standard_normal(out[name].shape)
        drawn = base * np.exp(spread * noise) if base else spread * noise
        out[name] = jnp.asarray(drawn.astype(out[name].dtype))
    for name, factor in factors.items():
        out[name] = (out[name] * factor).astype(out[name].dtype)
    return out
```

```python
from contextlib import ExitStack
import math

import concourse.bass as bass
from concourse import mybir

F32 = mybir.dt.float32
F32R = mybir.dt.float32r
BF16 = mybir.dt.bfloat16
I32 = mybir.dt.int32
U32 = mybir.dt.uint32
ACT = mybir.ActivationFunctionType
ALU = mybir.AluOpType
AX = mybir.AxisListType

P = 128
B, S, D, H = 2, 2048, 256, 16
HD = D // H
T = B * S
DK = D // P
FEAT = 3 * HD
SPLIT = 2 * FEAT
CH = 512
NCH = T // CH
TPC = CH // P
QUAD = 4
NQ = H // QUAD
NQ_BITS = NQ.bit_length() - 1
QC = S // CH
VW = 32
NE, HID, TOPK = 8, 512, 2
NT = T // P
HK = HID // P
SLOT_TILES = T * TOPK // P + NE
SLOTS = SLOT_TILES * P
AMP_EPS = 1e-6
LN_EPS = 1e-5
LAMBDA_MAX = 0.5
SCALE = 1.0 / math.sqrt(HD)
PI_BELOW = 3.1415925
MASKED = -1e30


class Names:

    def __init__(self, nc, stack, stage):
        self.nc, self.stack, self.stage = nc, stack, stage

    def sem(self, name):
        return self.stack.enter_context(self.nc.semaphore(f"{self.stage}_{name}"))

    def sb(self, name, shape, dt=F32):
        return self.stack.enter_context(self.nc.sbuf_tensor(f"{self.stage}_{name}", shape, dt))

    def ps(self, name, shape, dt=F32):
        return self.stack.enter_context(self.nc.psum_tensor(f"{self.stage}_{name}", shape, dt))


def staggered(eng, count, front, back):
    def pair(i):
        front(i + 1, 1)
        back(i, 0)
        front(i + 2, 0)
        back(i + 1, 1)

    front(0, 0)
    pair(0)
    with eng.Fori(1, count // 2 - 1) as j:
        pair(2 * j)
    front(count - 1, 1)
    back(count - 2, 0)
    back(count - 1, 1)


def pipelined(eng, count, stages, body=2):
    deepest = max(lag for _, lag in stages)
    lead = (deepest + 2 * body - 1) // body * body
    loops = max(0, (count - lead) // body)

    def iteration(i, u):
        for f, lag in stages:
            if not isinstance(i, int) or 0 <= i - lag < count:
                f(i - lag, (u - lag) % body)

    for i in range(lead):
        iteration(i, i)
    if loops:
        with eng.Fori(lead // body, lead // body + loops) as j:
            for u in range(body):
                iteration(body * j + u, u)
    for i in range(lead + body * loops, count + deepest):
        iteration(i, i)


def since(i, first):
    return not isinstance(i, int) or i >= first


def at(view, i):
    if isinstance(i, int):
        return view[i]
    rest = " ".join("bcdef"[:len(view.shape) - 2])
    return view[bass.ds(i, 1)].rearrange(f"o a {rest} -> (o a) {rest}")




def identity(pool, tile, begun, ready):
    pool.memset(tile, 0.0).then_inc(begun, 1)
    pool.wait_ge(begun, 1)
    pool.affine_select(out=tile, in_=tile, compare_op=ALU.not_equal, fill=1.0, base=0,
                       pattern=[[-1, P]], channel_multiplier=1).then_inc(ready, 1)


def absolute(dve, out, in_):
    return dve.tensor_scalar(out.bitcast(U32), in_.bitcast(U32), 0x7FFFFFFF, None, ALU.bitwise_and)


def prepare(nc, x, Wq, Wk, Wv, Wqp, Wkp, lambda_raw, q_parts, k_parts, v_rows, sorted_rows):
    with ExitStack() as stack:
        n = Names(nc, stack, "pre")
        ident = n.sb("ident", [P, P])
        heads_mean = n.sb("heads_mean", [P, P])
        weights = n.sb("weights", [P, 5, DK, D])
        lam = n.sb("lam", [P, 2])
        lam_tanh = n.sb("lam_tanh", [P, 2])
        lam_scale = n.sb("lam_scale", [P, 2])
        consts = n.sb("consts", [P, 3])
        half_pi, amp_eps, one = consts[:, 0:1], consts[:, 1:2], consts[:, 2:3]
        zeros = n.sb("zeros", [P, D])
        x_rows = n.sb("x_rows", [P, 2, TPC, D])
        x_t = n.sb("x_t", [P, 2, DK, CH])
        qk = n.sb("qk", [P, 2, 4, CH])
        soft = n.sb("soft", [P, 4, CH])
        amp = n.sb("amp", [P, 2, 4, CH])
        amp_sq = n.sb("amp_sq", [P, 4, CH])
        phase = n.sb("phase", [P, 2, 4, CH])
        waves = n.sb("waves", [P, 2, 4, CH])
        rnorm = n.sb("rnorm", [P, 4, CH])
        high = n.sb("high", [P, 3, 4, CH], F32R)
        low = n.sb("low", [P, 3, 4, CH], F32R)
        v_sb = n.sb("v_sb", [P, 2, TPC, H, VW])
        ps_x = n.ps("ps_x", [P, DK, CH])
        ps_v = n.ps("ps_v", [P, TPC, D])
        ps_p = n.ps("ps_p", [P, 4, CH])

        s_w = n.sem("weights_loaded")
        s_const = n.sem("constants")
        s_const_made = n.sem("constants_begun")
        s_lam = n.sem("lambda_ready")
        s_ones = n.sem("value_ones")
        s_x = [n.sem(f"x_loaded{i}") for i in range(2)]
        s_xp = n.sem("x_transposed")
        s_xt = n.sem("x_t_ready")
        s_pp = n.sem("phase_projected")
        s_tanh = n.sem("phase_ready")
        s_qkp = n.sem("qk_projected")
        s_qk = n.sem("qk_ready")
        s_abs = n.sem("abs_ready")
        s_exp = n.sem("exp_ready")
        s_log = n.sem("log_ready")
        s_amp = n.sem("amp_ready")
        s_scaled = n.sem("q_scaled")
        s_sq = n.sem("amp_squared")
        s_norm = n.sem("norm_summed")
        s_ln = n.sem("norm_log")
        s_rn = n.sem("rnorm_ready")
        s_absp = n.sem("abs_phase")
        s_sin = n.sem("sine_ready")
        s_cos = n.sem("cosine_ready")
        s_an = n.sem("amp_normed")
        s_feat = n.sem("features_ready")
        s_feat_q = n.sem("q_features_ready")
        s_high = n.sem("high_ready")
        s_low = n.sem("low_ready")
        s_vp = n.sem("v_projected")
        s_v = n.sem("v_ready")
        s_out = n.sem("parts_stored")
        s_vout = n.sem("v_stored")
        s_z = n.sem("places_cleared")
        block = stack.enter_context(nc.Block())

        CONSTS = 5
        STORES = 12
        HEADS = P // HD
        rows_in = x.rearrange("b (c t p) d -> (b c) p t d", p=P, t=TPC)
        rows_v = v_rows.rearrange("(c t p) w -> c p t w", p=P, t=TPC)
        cleared = sorted_rows.rearrange("(c a p) d -> c p a d", c=SLOT_TILES // 8, p=P)
        CLEARS = SLOT_TILES // 8

        @block.sync
        def _(sp):
            for w, src in enumerate((Wq, Wk, Wqp, Wkp, Wv)):
                sp.dma_start(weights[:, w], src.rearrange("(k p) n -> p k n", p=P)).then_inc(s_w, 16)
            for c in range(2):
                per_head = lambda_raw[c * HEADS:(c + 1) * HEADS].rearrange("(h o) -> h o", o=1)
                for h in range(HEADS):
                    sp.dma_start(lam[h * HD:(h + 1) * HD, c:c + 1],
                                 per_head[h:h + 1, :].to_broadcast([HD, 1])).then_inc(s_w, 16)

            def front(i, p):
                if since(i, 2):
                    sp.wait_ge(s_xp, i - 1)
                sp.dma_start(x_rows[:, p], at(rows_in, i)).then_inc(s_x[p], 16)

            def back(i, p):
                sp.wait_ge(s_v, i + 1)
                sp.dma_start(at(rows_v, i), v_sb[:, p].rearrange("p t h w -> p t (h w)")).then_inc(s_vout, 16)
                for kind in range(3):
                    for part, (tile, ready) in enumerate(((high, s_high), (low, s_low))):
                        sp.wait_ge(ready, i * 3 + (kind + 1))
                        for c, parts in enumerate((q_parts, k_parts)):
                            to = parts[:, 3 * part + kind].rearrange("n (c r) t -> n r c t", c=2)
                            sp.dma_start(at(to, i), tile[:, kind, 2 * c:2 * c + 2].bitcast(F32)).then_inc(s_out, 16)

            staggered(sp, NCH, front, back)
            sp.wait_ge(s_const, CONSTS)
            for c in range(CLEARS):
                sp.dma_start(cleared[c], zeros[:, :].rearrange("p (o d) -> p o d", o=1).to_broadcast([P, 8, D])).then_inc(s_z, 16)
            sp.wait_ge(s_vout, 16 * NCH)
            sp.wait_ge(s_out, 16 * STORES * NCH)
            sp.wait_ge(s_z, 16 * CLEARS)

        @block.tensor
        def _(pe):
            pe.wait_ge(s_const, CONSTS)
            pe.wait_ge(s_w, 16 * (5 + H))

            def project(pair, p):
                for w in range(2):
                    for c in range(2):
                        for k in range(DK):
                            mm = pe.matmul(ps_p[:, 2 * w + c], weights[:, pair + w, k, c * P:(c + 1) * P],
                                           x_t[:, p, k], start=(k == 0), stop=(k == DK - 1))
                return mm

            def front(i, p):
                pe.wait_ge(s_x[p], 16 * ((i >> 1) + 1))
                if since(i, 1):
                    pe.wait_ge(s_xt, i)
                for t in range(TPC):
                    for k in range(DK):
                        mm = pe.transpose(ps_x[:, k, t * P:(t + 1) * P], x_rows[:, p, t, k * P:(k + 1) * P],
                                          ident[:, :])
                mm.then_inc(s_xp, 1)
                pe.wait_ge(s_xt, i + 1)
                if since(i, 2):
                    pe.wait_ge(s_ln, i - 1)
                if since(i, 1):
                    pe.wait_ge(s_qk, i)
                project(2, p).then_inc(s_pp, 1)
                if since(i, 1):
                    pe.wait_ge(s_v, i)
                for t in range(TPC):
                    for k in range(DK):
                        mm = pe.matmul(ps_v[:, t], x_t[:, p, k, t * P:(t + 1) * P], weights[:, 4, k],
                                       start=(k == 0), stop=(k == DK - 1))
                mm.then_inc(s_vp, 1)
                pe.wait_ge(s_tanh, i + 1)
                project(0, p).then_inc(s_qkp, 1)

            def back(i, p):
                pe.wait_ge(s_sq, i + 1)
                pe.wait_ge(s_qk, min(i + 2, NCH) if isinstance(i, int) else i + 2)
                for c in range(4):
                    mm = pe.matmul(ps_p[:, c], heads_mean[:, :], amp_sq[:, c], start=True, stop=True)
                mm.then_inc(s_norm, 1)
                if isinstance(i, int) and i == NCH - 2:
                    pe.wait_ge(s_ln, i + 1)
            staggered(pe, NCH, front, back)

        @block.scalar
        def _(act):
            act.wait_ge(s_w, 16 * (5 + H))
            act.activation(lam_tanh[:, :], lam[:, :], ACT.Tanh).then_inc(s_lam, 1)
            act.wait_ge(s_const, CONSTS)

            def front(i, p):
                act.wait_ge(s_pp, i + 1)
                if since(i, 2):
                    act.wait_ge(s_cos, i - 1)
                    act.wait_ge(s_absp, i - 1)
                act.activation(phase[:, p], ps_p[:, :], ACT.Tanh).then_inc(s_tanh, 1)
                act.wait_ge(s_abs, i + 1)
                act.activation(soft[:, :], soft[:, :], ACT.Exp, scale=-1.0).then_inc(s_exp, 1)
                act.wait_ge(s_exp, i + 1)
                act.activation(soft[:, :], soft[:, :], ACT.Ln, bias=one).then_inc(s_log, 1)

            def back(i, p):
                act.wait_ge(s_norm, i + 1)
                if since(i, 1):
                    act.wait_ge(s_an, i)
                act.activation(rnorm[:, :], ps_p[:, :], ACT.Ln, bias=amp_eps).then_inc(s_ln, 1)
                act.wait_ge(s_ln, i + 1)
                act.activation(rnorm[:, :], rnorm[:, :], ACT.Exp, scale=-0.5).then_inc(s_rn, 1)
                act.wait_ge(s_tanh, i + 1)
                act.wait_ge(s_absp, i + 1)
                act.activation(waves[:, 0], waves[:, 0], ACT.Sin, bias=half_pi, scale=-PI_BELOW).then_inc(s_cos, 1)
                if since(i, 1):
                    act.wait_ge(s_low, i * 3)
                act.activation(waves[:, 1], phase[:, p], ACT.Sin, scale=PI_BELOW).then_inc(s_sin, 1)
            staggered(act, NCH, front, back)

        @block.vector
        def _(dve):
            dve.memset(v_sb[:, :, :, :, :], 0.0).then_inc(s_ones, 1)
            dve.wait_ge(s_ones, 1)
            for p in range(2):
                dve.memset(v_sb[:, p, :, :, HD:HD + 1], 1.0).then_inc(s_ones, 1)
            dve.wait_ge(s_ones, 3)
            dve.wait_ge(s_lam, 1)
            dve.tensor_scalar(lam_scale[:, :], lam_tanh[:, :], LAMBDA_MAX * SCALE, None, ALU.mult).then_inc(s_lam, 1)
            dve.wait_ge(s_lam, 2)

            def front(i, p):
                dve.wait_ge(s_xp, i + 1)
                if since(i, 2):
                    dve.wait_ge(s_qkp, i - 1)
                dve.tensor_copy(x_t[:, p], ps_x[:, :]).then_inc(s_xt, 1)
                dve.wait_ge(s_vp, i + 1)
                if since(i, 2):
                    dve.wait_ge(s_vout, 16 * (i - 1))
                dve.tensor_copy(v_sb[:, p, :, :, 0:HD].rearrange("p t h d -> p (t h) d"),
                                ps_v[:, :].rearrange("p t (h d) -> p (t h) d", d=HD)).then_inc(s_v, 1)
                dve.wait_ge(s_qkp, i + 1)
                if since(i, 2):
                    dve.wait_ge(s_low, 3 * (i - 1))
                dve.tensor_copy(qk[:, p], ps_p[:, :]).then_inc(s_qk, 1)
                dve.wait_ge(s_qk, i + 1)
                if since(i, 1):
                    dve.wait_ge(s_amp, i)
                absolute(dve, soft[:, :], qk[:, p]).then_inc(s_abs, 1)
                dve.wait_ge(s_log, i + 1)
                if since(i, 2):
                    dve.wait_ge(s_feat, 2 * (i - 1))
                flat = "p c t -> p (c t)"
                dve.scalar_tensor_tensor(amp[:, p].rearrange(flat), qk[:, p].rearrange(flat), 0.0,
                                         soft[:, :].rearrange(flat), ALU.max, ALU.add).then_inc(s_amp, 1)

            def back(i, p):
                dve.wait_ge(s_tanh, i + 1)
                if since(i, 1):
                    dve.wait_ge(s_low, 3 * i)
                absolute(dve, waves[:, 0], phase[:, p]).then_inc(s_absp, 1)
                dve.wait_ge(s_amp, i + 1)
                dve.tensor_scalar(qk[:, p, 0:2], qk[:, p, 0:2], SCALE, None, ALU.mult).then_inc(s_scaled, 1)
                dve.wait_ge(s_scaled, i + 1)
                if since(i, 1):
                    dve.wait_ge(s_out, 16 * STORES * i)
                dve.tensor_copy(high[:, 0], qk[:, p]).then_inc(s_high, 1)
                dve.wait_ge(s_rn, i + 1)
                dve.wait_ge(s_sq, i + 1)
                dve.tensor_tensor(amp[:, p], amp[:, p], rnorm[:, :], ALU.mult).then_inc(s_an, 1)
                dve.wait_ge(s_an, i + 1)
                for f, ready in enumerate((s_cos, s_sin)):
                    dve.wait_ge(ready, i + 1)
                    for c in range(2):
                        dve.scalar_tensor_tensor(waves[:, f, c], amp[:, p, c], lam_scale[:, c:c + 1], waves[:, f, c],
                                                 ALU.mult, ALU.mult).then_inc(s_feat_q, 1)
                    dve.tensor_tensor(waves[:, f, 2:4], amp[:, p, 2:4], waves[:, f, 2:4], ALU.mult).then_inc(s_feat, 1)
                    dve.wait_ge(s_feat_q, 4 * i + 2 * (f + 1))
                    dve.wait_ge(s_feat, 2 * i + (f + 1))
                    dve.tensor_copy(high[:, 1 + f], waves[:, f]).then_inc(s_high, 1)
            staggered(dve, NCH, front, back)

        @block.gpsimd
        def _(pool):
            pool.memset(consts[:, 0:1], math.pi / 2).then_inc(s_const, 1)
            pool.memset(consts[:, 1:2], AMP_EPS).then_inc(s_const, 1)
            pool.memset(consts[:, 2:3], 1.0).then_inc(s_const, 1)
            identity(pool, ident[:, :], s_const_made, s_const)
            pool.memset(heads_mean[:, :], 1.0 / HD).then_inc(s_const_made, 1)
            pool.memset(zeros[:, :], 0.0).then_inc(s_const_made, 1)
            pool.wait_ge(s_const_made, 3)
            blocks = heads_mean[:, :].rearrange("p (g d) -> p g d", d=HD)
            pool.affine_select(out=blocks, in_=blocks, compare_op=ALU.is_ge, fill=0.0, base=0,
                               pattern=[[-HD, HEADS], [0, HD]], channel_multiplier=1).then_inc(s_const_made, 1)
            pool.wait_ge(s_const_made, 4)
            pool.affine_select(out=blocks, in_=blocks, compare_op=ALU.is_ge, fill=0.0, base=HD - 1,
                               pattern=[[HD, HEADS], [0, HD]], channel_multiplier=-1).then_inc(s_const, 1)

            def split(i, kind, whole):
                pool.wait_ge(s_high, i * 3 + (kind + 1))
                pool.tensor_tensor(low[:, kind], whole, high[:, kind].bitcast(F32), ALU.subtract).then_inc(s_low, 1)

            def front(i, p):
                pool.wait_ge(s_amp, i + 1)
                if since(i, 1):
                    pool.wait_ge(s_norm, i)
                pool.tensor_tensor(amp_sq[:, :], amp[:, p], amp[:, p], ALU.mult).then_inc(s_sq, 1)

            def back(i, p):
                if since(i, 1):
                    pool.wait_ge(s_out, 16 * STORES * i)
                split(i, 0, qk[:, p])
                split(i, 1, waves[:, 0])
                split(i, 2, waves[:, 1])
            staggered(pool, NCH, front, back)
BLOCKS = [4 * (c + 1) for c in range(QC)]
FIRST = [sum(BLOCKS[:c]) for c in range(QC)]
STEPS = sum(BLOCKS)
AHEAD = 3
MAXIMA = [QUAD * TPC * (c + 1) for c in range(QC)]
EARLY = sum(MAXIMA[:AHEAD])
PER_QUAD = sum(MAXIMA)


def max_tiles(chunks):
    return [(nxt, c, h, q, k) for nxt, c in chunks for h in range(QUAD) for q in range(TPC) for k in range(c + 1)]


def attend_plan(last):
    tiles = max_tiles([(False, c) for c in range(AHEAD, QC)] + ([] if last else [(True, c) for c in range(AHEAD)]))
    columns = [CH - P * max(0, s - FIRST[c] - TPC * c) for c in range(QC) for s in range(FIRST[c], FIRST[c] + BLOCKS[c])]
    late = 5 * sum(columns[0:BLOCKS[0]])
    total, passed, at_ = 5 * sum(columns) - late, -late, 0
    plan, turns = [], []

    def fill(cols):
        nonlocal passed, at_
        passed += cols
        while at_ < min(len(tiles), PER_QUAD * passed // total + 1):
            plan.append(("max",) + tiles[at_])
            nxt, c, h, q, k = tiles[at_]
            if (h, q, k) == (QUAD - 1, TPC - 1, c):
                turns.append(("turn_max", nxt, c))
            at_ += 1

    for s in range(STEPS):
        for pair in range(2):
            plan.append(("scores", s, pair))
            if pair == 0:
                plan += turns
                turns.clear()
            fill(2 * columns[s])
        if s >= 1:
            plan.append(("values", s - 1))
            fill(columns[s])
            if s in FIRST:
                turns.append(("turn_out", FIRST.index(s) - 1))
        if s == STEPS - 1:
            plan.append(("values", s))
    while at_ < len(tiles):
        fill(total)
    plan += turns
    plan.append(("turn_out", QC - 1))
    return plan


def wait_positive(eng, sem, value):
    if not isinstance(value, int) or value > 0:
        eng.wait_ge(sem, value)


def quads(eng, quad):
    quad(0, False)
    with eng.Fori(1, B * NQ - 1) as g:
        quad(g, False)
    quad(B * NQ - 1, True)


def attend(nc, q_parts, k_parts, v_rows, attn_rows):
    with ExitStack() as stack:
        n = Names(nc, stack, "att")
        ident = n.sb("ident", [P, P])
        ident_b = n.sb("ident_b", [P, P], BF16)
        future = n.sb("future", [P, P], BF16)
        future_t = n.sb("future_t", [P, P], BF16)
        q_same = n.sb("q_same", [SPLIT + 1, QC, QUAD, CH], F32R)
        q_swap = n.sb("q_swap", [SPLIT, QC, QUAD, CH], F32R)
        keys = n.sb("keys", [SPLIT + 1, QUAD, QC, CH], F32R)
        keys_next = n.sb("keys_next", [SPLIT, QUAD, AHEAD, CH], F32R)
        values = n.sb("values", [P, S // P, QUAD * VW])
        probs = n.sb("probs", [P, 4, QUAD, CH])
        maxima = n.sb("maxima", [P, 2, QUAD * TPC, QC])
        neg_max = n.sb("neg_max", [P, 2, QUAD * TPC])
        max_row = n.sb("max_row", [QUAD * TPC, 2, P], F32R)
        out_t = n.sb("out_t", [P, CH])
        inv_sum = n.sb("inv_sum", [P, TPC * QUAD])
        out_rows = n.sb("out_rows", [P, 2, TPC, QUAD * HD])
        ps_s = [n.ps(f"ps_s{i}", [P, 2, CH]) for i in range(2)]
        ps_m = [n.ps(f"ps_m{i}", [P, CH]) for i in range(2)]
        ps_o = n.ps("ps_o", [P, CH])
        ps_t = n.ps("ps_t", [P, CH])

        s_made = n.sem("constants_begun")
        s_const = n.sem("constants")
        s_q = [n.sem(f"q_loaded{c}") for c in range(QC)]
        s_k = [n.sem(f"k_loaded{c}") for c in range(QC)]
        s_kn = [n.sem(f"next_k_loaded{c}") for c in range(AHEAD)]
        s_v = [n.sem(f"v_loaded{c}") for c in range(QC)]
        s_scores = n.sem("scores_ready")
        s_exp = n.sem("probs_ready")
        s_pv = n.sem("values_summed")
        s_mt = n.sem("max_tile_ready")
        s_mr = n.sem("max_tile_read")
        s_neg = n.sem("neg_max_ready")
        s_turn = n.sem("max_turned")
        s_row = n.sem("max_row_ready")
        s_m = [n.sem(f"max_row_placed{c}") for c in range(QC)]
        s_oc = n.sem("out_copied")
        s_ot = n.sem("out_turned")
        s_inv = n.sem("inverse_ready")
        s_or = n.sem("out_rows_ready")
        s_store = [n.sem(f"out_stored{i}") for i in range(2)]
        block = stack.enter_context(nc.Block())

        CONSTS = 5
        Q_LOADS, K_LOADS = 3 * QUAD, QUAD
        heads_q = q_parts.rearrange("n g (h d) t -> n h g d t", d=HD)
        heads_k = k_parts.rearrange("n g (h d) t -> n h g d t", d=HD)
        rows_v = v_rows.rearrange("(n k p) w -> n p k w", k=TPC, p=P)
        rows_o = attn_rows.rearrange("(n k p) w -> n p k w", k=TPC, p=P)

        def place(eng, g):
            chunk, head = (g >> NQ_BITS & (B - 1)) * QC, (g & (NQ - 1)) * QUAD
            return (chunk, head) if isinstance(g, int) else (eng.snap(chunk), eng.snap(head))

        def of_head(view, where, c, h, lo, hi):
            n_, h_ = where[0] + c, where[1] + h
            if isinstance(n_, int):
                return view[n_, h_, lo:hi]
            return view[bass.ds(n_, 1), bass.ds(h_, 1), lo:hi].rearrange("n h g d t -> (n h g) d t")

        def in_rows(view, where, c, width):
            n_, w_ = where[0] + c, where[1] * width
            if isinstance(n_, int):
                return view[n_, :, :, w_:w_ + QUAD * width]
            return view[bass.ds(n_, 1), :, :, bass.ds(w_, QUAD * width)].rearrange("n p k w -> (n p) k w")

        @block.sync
        def _(sp):
            KINDS = 3

            def load_q(where, c):
                for h in range(QUAD):
                    sp.dma_start(q_same[0:SPLIT, c, h].bitcast(F32), of_head(heads_q, where, c, h, 0, 2 * KINDS)).then_inc(s_q[c], 16)
                    sp.dma_start(q_swap[0:FEAT, c, h].bitcast(F32), of_head(heads_q, where, c, h, KINDS, 2 * KINDS)).then_inc(s_q[c], 16)
                    sp.dma_start(q_swap[FEAT:SPLIT, c, h].bitcast(F32), of_head(heads_q, where, c, h, 0, KINDS)).then_inc(s_q[c], 16)

            def load_k(where, c):
                for h in range(QUAD):
                    sp.dma_start(keys[0:SPLIT, h, c].bitcast(F32), of_head(heads_k, where, c, h, 0, 2 * KINDS)).then_inc(s_k[c], 16)

            def load_kn(where, c):
                for h in range(QUAD):
                    sp.dma_start(keys_next[:, h, c].bitcast(F32), of_head(heads_k, where, c, h, 0, 2 * KINDS)).then_inc(s_kn[c], 16)

            def load_v(where, c):
                sp.dma_start(values[:, TPC * c:TPC * c + TPC], in_rows(rows_v, where, c, VW)).then_inc(s_v[c], 16)

            def place_max(g, c, turned):
                sp.wait_ge(s_row, turned)
                sp.dma_start(q_same[SPLIT:SPLIT + 1, c].bitcast(F32), max_row[:, c % 2].bitcast(F32)).then_inc(s_m[c], 16)

            def scored(g, step):
                sp.wait_ge(s_scores, g * (2 * STEPS) + 2 * step)

            for c in range(AHEAD):
                load_kn((0, 0), c)
                load_q((0, 0), c)
            for c in range(QC):
                load_k((0, 0), c)
                load_v((0, 0), c)
            load_q((0, 0), 3)
            place_max(0, 0, 1)
            place_max(0, 1, 2)

            def quad(g, last):
                after = None if last else place(sp, g + 1)
                if not last:
                    sp.wait_ge(s_mt, g * PER_QUAD + EARLY)
                    for c in range(AHEAD):
                        load_kn(after, c)
                place_max(g, 2, g * QC + 3)
                if not last:
                    scored(g, FIRST[1])
                    load_q(after, 0)
                place_max(g, 3, g * QC + 4)
                if not last:
                    scored(g, FIRST[2])
                    load_q(after, 1)
                    place_max(g + 1, 0, g * QC + 5)
                    scored(g, FIRST[3])
                    load_q(after, 2)
                    place_max(g + 1, 1, g * QC + 6)
                    for c in range(QC):
                        scored(g, FIRST[3] + TPC * (c + 1))
                        load_k(after, c)
                        sp.wait_ge(s_pv, g * STEPS + (FIRST[3] + TPC * (c + 1)))
                        load_v(after, c)
                    load_q(after, 3)
            quads(sp, quad)

        @block.tensor
        def _(pe):
            pe.wait_ge(s_const, CONSTS)

            def max_tile(g, nxt, c, h, q, k, before, number):
                if (h, q) == (0, 0):
                    gg = g + 1 if nxt else g
                    if k == 0:
                        pe.wait_ge(s_q[c], 16 * Q_LOADS * (gg + 1))
                    if c < AHEAD:
                        pe.wait_ge(s_kn[k], 16 * K_LOADS * (gg + 1))
                    else:
                        pe.wait_ge(s_k[k], 16 * K_LOADS * (gg + 1))
                wait_positive(pe, s_mr, before + (number - 1))
                width = CH if k < c else P * (q + 1)
                key = keys_next[:, h, k, 0:width] if c < AHEAD else keys[0:SPLIT, h, k, 0:width]
                buf = ps_m[number % 2]
                mm = pe.matmul(buf[:, 0:width], q_same[0:SPLIT, c, h, P * q:P * q + P], key, start=True, stop=(k < c))
                if k == c:
                    mm = pe.matmul(buf[:, P * q:P * q + P], ident_b[:, :], future[:, :], start=False, stop=True)
                mm.then_inc(s_mt, 1)

            def turn_max(c, maxes, outs):
                pe.wait_ge(s_neg, maxes + 1)
                wait_positive(pe, s_row, maxes)
                wait_positive(pe, s_or, outs)
                pe.transpose(ps_t[0:QUAD * TPC, 0:P], neg_max[:, c % 2], ident[:, :]).then_inc(s_turn, 1)

            def scores(g, s, pair):
                c = max(c for c in range(QC) if FIRST[c] <= s)
                k = s - FIRST[c]
                skip = P * max(0, k - TPC * c)
                if k == 0 and pair == 0:
                    pe.wait_ge(s_m[c], 16 * (g + 1))
                    pe.wait_ge(s_q[c], 16 * Q_LOADS * (g + 1))
                if k % TPC == 0 and pair == 0:
                    pe.wait_ge(s_k[k // TPC], 16 * K_LOADS * (g + 1))
                wait_positive(pe, s_exp, g * (2 * STEPS) + (2 * s + pair - 1))
                for e in range(2):
                    h = 2 * pair + e
                    out = ps_s[pair][:, e, skip:CH]
                    kk = slice(P * (k % TPC), P * (k % TPC) + P)
                    pe.matmul(out, keys[0:SPLIT + 1, h, k // TPC, kk], q_same[0:SPLIT + 1, c, h, skip:CH],
                              start=True, stop=False)
                    if k >= TPC * c:
                        pe.matmul(ps_s[pair][:, e, skip:skip + P], ident_b[:, :], future_t[:, :],
                                  start=False, stop=False)
                    mm = pe.matmul(out, keys[0:SPLIT, h, k // TPC, kk], q_swap[0:SPLIT, c, h, skip:CH],
                                   start=False, stop=True)
                mm.then_inc(s_scores, 1)

            def sum_values(g, s):
                c = max(c for c in range(QC) if FIRST[c] <= s)
                k = s - FIRST[c]
                skip = P * max(0, k - TPC * c)
                pe.wait_ge(s_exp, g * (2 * STEPS) + 2 * (s + 1))
                if k % TPC == 0:
                    pe.wait_ge(s_v[k // TPC], 16 * (g + 1))
                if k == 0:
                    wait_positive(pe, s_oc, g * QC + c)
                for h in range(QUAD):
                    mm = pe.matmul(ps_o[VW * h:VW * h + VW, skip:CH], values[:, k, VW * h:VW * h + VW],
                                   probs[:, s % 4, h, skip:CH], start=(k == 0), stop=(k == BLOCKS[c] - 1))
                mm.then_inc(s_pv, 1)

            def turn_out(g, c, maxes):
                pe.wait_ge(s_oc, g * QC + (c + 1))
                pe.wait_ge(s_row, maxes)
                wait_positive(pe, s_or, g * QC + c)
                for q in range(TPC):
                    mm = pe.transpose(ps_t[:, P * q:P * q + P], out_t[:, P * q:P * q + P], ident[:, :])
                mm.then_inc(s_ot, 1)

            for number, (nxt, c, h, q, k) in enumerate(max_tiles([(False, c) for c in range(AHEAD)])):
                max_tile(0, nxt, c, h, q, k, 0, number)
                if c >= 1 and (h, q, k) == (0, 1, 0):
                    turn_max(c - 1, c - 1, 0)
            turn_max(AHEAD - 1, AHEAD - 1, 0)

            def quad(g, last):
                number, maxes, outs = 0, 0, 0
                for event, *what in attend_plan(last):
                    if event == "scores":
                        scores(g, *what)
                    elif event == "values":
                        sum_values(g, what[0])
                    elif event == "max":
                        max_tile(g, *what, g * PER_QUAD + EARLY, number)
                        number += 1
                    elif event == "turn_max":
                        turn_max(what[1], g * QC + (AHEAD + maxes), g * QC + outs)
                        maxes += 1
                    elif event == "turn_out":
                        turn_out(g, what[0], g * QC + (AHEAD + maxes))
                        outs += 1
            quads(pe, quad)

        @block.scalar
        def _(act):
            def quad(g, last):
                for s in range(STEPS):
                    c = max(c for c in range(QC) if FIRST[c] <= s)
                    skip = P * max(0, s - FIRST[c] - TPC * c)
                    wait_positive(act, s_pv, g * STEPS + (s - 3))
                    for pair in range(2):
                        act.wait_ge(s_scores, g * (2 * STEPS) + (2 * s + pair + 1))
                        act.activation(probs[:, s % 4, 2 * pair:2 * pair + 2, skip:CH], ps_s[pair][:, :, skip:CH],
                                       ACT.Exp).then_inc(s_exp, 1)
            quads(act, quad)

        @block.vector
        def _(dve):
            dve.memset(keys[SPLIT:SPLIT + 1, :, :, :].bitcast(F32), 1.0).then_inc(s_const, 1)

            def read_max(nxt, c, h, q, k, before, number):
                dve.wait_ge(s_mt, before + (number + 1))
                width = CH if k < c else P * (q + 1)
                dve.tensor_reduce(maxima[:, c % 2, h * TPC + q, k:k + 1], ps_m[number % 2][:, 0:width], AX.X,
                                  ALU.max).then_inc(s_mr, 1)

            def negate(c, number, turned):
                dve.wait_ge(s_mr, number + 1)
                wait_positive(dve, s_turn, turned)
                dve.tensor_reduce(neg_max[:, c % 2], maxima[:, c % 2, :, 0:c + 1], AX.X, ALU.max,
                                  negate=True).then_inc(s_neg, 1)

            def keep_row(c, turned, placed):
                dve.wait_ge(s_turn, turned)
                if placed is not None:
                    dve.wait_ge(s_m[(c + 2) % QC], placed)
                dve.tensor_copy(max_row[:, c % 2], ps_t[0:QUAD * TPC, 0:P]).then_inc(s_row, 1)

            number = 0
            for nxt, c, h, q, k in max_tiles([(False, c) for c in range(AHEAD)]):
                read_max(nxt, c, h, q, k, 0, number)
                if (h, q, k) == (QUAD - 1, TPC - 1, c):
                    negate(c, number, c - 1)
                number += 1
                if c >= 1 and (h, q, k) == (0, 1, 0):
                    keep_row(c - 1, c, None)
            keep_row(AHEAD - 1, AHEAD, 16)

            def quad(g, last):
                number, negs, maxes = 0, 0, 0
                for event, *what in attend_plan(last):
                    if event == "max":
                        read_max(*what, g * PER_QUAD + EARLY, number)
                        nxt, c, h, q, k = what
                        if (h, q, k) == (QUAD - 1, TPC - 1, c):
                            negate(c, g * PER_QUAD + (EARLY + number), g * QC + (AHEAD + negs - 1))
                            negs += 1
                        number += 1
                    elif event == "turn_max":
                        keep_row(what[1], g * QC + (AHEAD + 1 + maxes), 16 * (g + (1 + (AHEAD - 2 + maxes) // QC)))
                        maxes += 1
                    elif event == "values" and what[0] + 1 in FIRST + [STEPS]:
                        c = (FIRST + [STEPS]).index(what[0] + 1) - 1
                        dve.wait_ge(s_pv, g * STEPS + (what[0] + 1))
                        wait_positive(dve, s_ot, g * QC + c)
                        dve.tensor_copy(out_t[:, :], ps_o[:, :]).then_inc(s_oc, 1)
                    elif event == "turn_out":
                        c = what[0]
                        dve.wait_ge(s_ot, g * QC + (c + 1))
                        turned = ps_t[:, :].rearrange("p (j w) -> p j w", w=VW)
                        wait_positive(dve, s_or, g * QC + c)
                        dve.reciprocal(inv_sum[:, :].rearrange("p (j o) -> p j o", o=1), turned[:, :, HD:HD + 1]).then_inc(s_inv, 1)
                        dve.wait_ge(s_inv, g * QC + (c + 1))
                        wait_positive(dve, s_store[c % 2], 16 * (g * 2 + c // 2))
                        dve.tensor_tensor(out_rows[:, c % 2].rearrange("p q (h d) -> p (q h) d", d=HD), turned[:, :, 0:HD],
                                          inv_sum[:, :].rearrange("p (j o) -> p j o", o=1).to_broadcast([P, TPC * QUAD, HD]),
                                          ALU.mult).then_inc(s_or, 1)
            quads(dve, quad)

        @block.gpsimd
        def _(pool):
            identity(pool, ident[:, :], s_made, s_const)
            pool.memset(ident_b[:, :], 0.0).then_inc(s_made, 1)
            pool.memset(future[:, :], 0.0).then_inc(s_made, 1)
            pool.memset(future_t[:, :], 0.0).then_inc(s_made, 1)
            pool.wait_ge(s_made, 4)
            pool.affine_select(out=future_t[:, :], in_=future_t[:, :], compare_op=ALU.is_ge, fill=MASKED, base=0,
                               pattern=[[1, P]], channel_multiplier=-1).then_inc(s_const, 1)
            pool.affine_select(out=ident_b[:, :], in_=ident_b[:, :], compare_op=ALU.not_equal, fill=1.0, base=0,
                               pattern=[[-1, P]], channel_multiplier=1).then_inc(s_const, 1)
            pool.affine_select(out=future[:, :], in_=future[:, :], compare_op=ALU.is_ge, fill=MASKED, base=0,
                               pattern=[[-1, P]], channel_multiplier=1).then_inc(s_const, 1)

            def store(g, where, c):
                pool.wait_ge(s_or, g * QC + (c + 1))
                pool.dma_start(in_rows(rows_o, where, c, HD), out_rows[:, c % 2]).then_inc(s_store[c % 2], 16)

            with pool.Fori(0, B * NQ) as g:
                where = place(pool, g)
                for c in range(QC):
                    store(g, where, c)
            for i in range(2):
                pool.wait_ge(s_store[i], 16 * B * NQ * QC // 2)
STEP_SHIFTED = 2
STEP_BOTH = STEP_SHIFTED + 4 + 5 * TOPK + (TOPK - 1) + 1
STEP_PLACES = [STEP_BOTH + 10 + 3 * (r + 1) for r in range(TOPK)]


def flat(a):
    return a.rearrange("p t e -> p (t e)")


class Norm:

    def __init__(self, n):
        self.stats = n.sb("stats", [P, TPC, 6])
        self.moments = n.sb("moments", [P, 4, TPC])
        self.mean, self.var, self.m2, self.gap = (self.moments[:, i] for i in range(4))
        self.rstd = n.sb("rstd", [P, TPC])
        self.s_stats = n.sem("stats_ready")
        self.s_step = n.sem("variance_step")
        self.s_var = n.sem("variance_ready")
        self.s_log = n.sem("variance_log")
        self.s_rstd = n.sem("rstd_ready")
        self.s_done = n.sem("rows_normed")

    def statistics(self, dve, i, rows):
        if since(i, 1):
            dve.wait_ge(self.s_done, i * TPC)
        for t in range(TPC):
            dve.bn_stats(self.stats[:, t], rows[:, t]).then_inc(self.s_stats, 1)
        even_mean, even_m2, odd_mean, odd_m2 = (self.stats[:, :, j] for j in (1, 2, 4, 5))
        dve.wait_ge(self.s_stats, i * TPC + TPC)
        dve.tensor_tensor(self.mean, even_mean, odd_mean, ALU.add).then_inc(self.s_step, 1)
        dve.tensor_tensor(self.gap, even_mean, odd_mean, ALU.subtract).then_inc(self.s_step, 1)
        dve.tensor_tensor(self.m2, even_m2, odd_m2, ALU.add).then_inc(self.s_step, 1)
        dve.wait_ge(self.s_step, i * 6 + 3)
        dve.tensor_scalar(self.mean, self.mean, 0.5, None, ALU.mult).then_inc(self.s_step, 1)
        dve.scalar_tensor_tensor(self.gap, self.gap, 0.25, self.gap, ALU.mult, ALU.mult).then_inc(self.s_step, 1)
        dve.tensor_scalar(self.m2, self.m2, 1.0 / D, None, ALU.mult).then_inc(self.s_step, 1)
        dve.wait_ge(self.s_step, i * 6 + 6)
        dve.tensor_tensor(self.var, self.m2, self.gap, ALU.add).then_inc(self.s_var, 1)

    def inverse(self, act, i, eps):
        act.wait_ge(self.s_var, i + 1)
        if since(i, 1):
            act.wait_ge(self.s_done, i * TPC)
        act.activation(self.rstd[:, :], self.var, ACT.Ln, bias=eps).then_inc(self.s_log, 1)
        act.wait_ge(self.s_log, i + 1)
        act.activation(self.rstd[:, :], self.rstd[:, :], ACT.Exp, scale=-0.5).then_inc(self.s_rstd, 1)

    def apply(self, dve, i, out, rows):
        dve.wait_ge(self.s_rstd, i + 1)
        for t in range(TPC):
            dve.tensor_scalar(out[:, t], rows[:, t], self.mean[:, t:t + 1], self.rstd[:, t:t + 1],
                              ALU.subtract, ALU.mult).then_inc(self.s_done, 1)


def turn_rows(pe, out, rows, ident):
    for t in range(TPC):
        for k in range(DK):
            mm = pe.transpose(out[:, k, t * P:(t + 1) * P], rows[:, t, k * P:(k + 1) * P], ident)
    return mm


def multiply_rows(pe, out, turned, weight):
    for t in range(TPC):
        for k in range(DK):
            mm = pe.matmul(out[:, t], turned[:, k, t * P:(t + 1) * P], weight[:, k], start=(k == 0), stop=(k == DK - 1))
    return mm


def route(nc, x, attn_rows, Wo, Wg, bg, W1, W3, W2, keep, sorted_rows):
    x1, places, weight, tile_expert, w1, w3, w2 = keep
    with ExitStack() as stack:
        n = Names(nc, stack, "route")
        ident = n.sb("ident", [P, P])
        before = n.sb("before", [P, P])
        ones = n.sb("ones", [P, P])
        eps = n.sb("eps", [P, 1])
        wo = n.sb("wo", [P, DK, D])
        wg = n.sb("wg", [P, DK, NE])
        bias_g = n.sb("bias_g", [P, NE])
        a_rows = n.sb("a_rows", [P, 2, TPC, D])
        a_t = n.sb("a_t", [P, 2, DK, CH])
        x_rows = n.sb("x_rows", [P, 2, TPC, D])
        res = n.sb("res", [P, TPC, D])
        normed = n.sb("normed", [P, 2, TPC, D])
        x1_t = n.sb("x1_t", [P, DK, CH])
        norm = Norm(n)
        logits = n.sb("logits", [P, NT, NE])
        gates = n.sb("gates", [P, NT, NE])
        rest = n.sb("rest", [P, NT, NE])
        hot = n.sb("hot", [P, TOPK, NT, NE])
        tmp = n.sb("tmp", [P, NT, NE])
        both = n.sb("both", [P, NT, NE])
        col = n.sb("col", [P, NT])
        number = n.sb("number", [P, NE])
        tile_no = n.sb("tile_no", [P, SLOT_TILES])
        counted = n.sb("counted", [P, NT, NE])
        place = n.sb("place", [P, NT, NE])
        tiles_i = n.sb("tiles_i", [P, NE], I32)
        tiles = n.sb("tiles", [P, NE])
        ends = n.sb("ends", [P, NE])
        passed = n.sb("passed", [1, SLOT_TILES, NE])
        owner = n.sb("owner", [1, SLOT_TILES])
        ps_a = n.ps("ps_a", [P, DK, CH])
        ps_y = n.ps("ps_y", [P, TPC, D])
        ps_n = n.ps("ps_n", [P, DK, CH])
        ps_g = n.ps("ps_g", [P, TPC, NE])
        ps_c = n.ps("ps_c", [P, 2, NT * NE])

        s_made = n.sem("constants_begun")
        s_const = n.sem("constants")
        s_w = n.sem("weights_loaded")
        s_expert = n.sem("expert_weights_loaded")
        s_in = [n.sem(f"rows_loaded{i}") for i in range(2)]
        s_ap = n.sem("attention_turned")
        s_at = n.sem("attention_t_ready")
        s_y = n.sem("projected")
        s_res = n.sem("residual_ready")
        s_kept = n.sem("x1_kept")
        s_np = n.sem("x1_turned")
        s_nt = n.sem("x1_t_ready")
        s_g = n.sem("gates_projected")
        s_l = n.sem("logits_ready")
        s_step = n.sem("routing_step")
        s_e = n.sem("gates_exp")
        s_count = n.sem("counts_ready")
        s_scan = n.sem("running_sums")
        s_put = n.sem("rows_put")
        block = stack.enter_context(nc.Block())

        CONSTS = 6
        rows_a = attn_rows.rearrange("(c t p) d -> c p t d", t=TPC, p=P)
        rows_in = x.rearrange("b (c t p) d -> (b c) p t d", p=P, t=TPC)

        @block.sync
        def _(sp):
            sp.dma_start(wo[:, :], Wo.rearrange("(k p) n -> p k n", p=P)).then_inc(s_w, 16)
            sp.dma_start(wg[:, :], Wg.rearrange("(k p) n -> p k n", p=P)).then_inc(s_w, 16)
            sp.dma_start(bias_g[:, :], bg.partition_broadcast(P)).then_inc(s_w, 16)

            def front(i, p):
                if since(i, 2):
                    sp.wait_ge(s_ap, i - 1)
                    sp.wait_ge(s_res, i - 1)
                sp.dma_start(a_rows[:, p], at(rows_a, i)).then_inc(s_in[p], 16)
                sp.dma_start(x_rows[:, p], at(rows_in, i)).then_inc(s_in[p], 16)

            def back(i, p):
                pass
            staggered(sp, NCH, front, back)
            for k in range(DK):
                for dst, src in ((w1, W1), (w3, W3)):
                    sp.dma_start(dst[:, k], src[:, k * P:(k + 1) * P].rearrange("e p h -> p e h")).then_inc(s_expert, 16)
            for k in range(HK):
                sp.dma_start(w2[:, k], W2[:, k * P:(k + 1) * P].rearrange("e p n -> p e n")).then_inc(s_expert, 16)
            sp.wait_ge(s_expert, 16 * (2 * DK + HK))

        @block.tensor
        def _(pe):
            pe.wait_ge(s_const, CONSTS)
            pe.wait_ge(s_w, 16 * 3)

            def front(i, p):
                pe.wait_ge(s_in[p], 32 * ((i >> 1) + 1))
                if since(i, 1):
                    pe.wait_ge(s_at, i)
                turn_rows(pe, ps_a, a_rows[:, p], ident[:, :]).then_inc(s_ap, 1)
                pe.wait_ge(s_at, i + 1)
                if since(i, 1):
                    pe.wait_ge(s_res, i)
                multiply_rows(pe, ps_y, a_t[:, p], wo).then_inc(s_y, 1)

            def back(i, p):
                pe.wait_ge(norm.s_done, i * TPC + TPC)
                if since(i, 1):
                    pe.wait_ge(s_nt, i)
                turn_rows(pe, ps_n, normed[:, p], ident[:, :]).then_inc(s_np, 1)
                pe.wait_ge(s_nt, i + 1)
                if since(i, 1):
                    pe.wait_ge(s_l, i)
                multiply_rows(pe, ps_g, x1_t, wg).then_inc(s_g, 1)
            staggered(pe, NCH, front, back)
            pe.wait_ge(s_step, STEP_BOTH)
            pe.matmul(ps_c[:, 0], before[:, :], both[:, :].rearrange("p t e -> p (t e)"), start=True, stop=True).then_inc(s_count, 1)
            pe.matmul(ps_c[:, 1], ones[:, :], both[:, :].rearrange("p t e -> p (t e)"), start=True, stop=True).then_inc(s_count, 1)

        @block.scalar
        def _(act):
            act.wait_ge(s_const, CONSTS)

            def front(i, p):
                pass

            def back(i, p):
                norm.inverse(act, i, eps[:, 0:1])
                act.wait_ge(norm.s_done, i * TPC + TPC)
                x1_chunk = x1[:, i * TPC:i * TPC + TPC] if isinstance(i, int) else x1[:, bass.ds(i * TPC, TPC)]
                act.copy(x1_chunk, normed[:, p]).then_inc(s_kept, 1)
                act.wait_ge(s_np, i + 1)
                if since(i, 1):
                    act.wait_ge(s_g, i)
                act.copy(x1_t[:, :], ps_n[:, :]).then_inc(s_nt, 1)
            staggered(act, NCH, front, back)
            act.wait_ge(s_step, STEP_SHIFTED)
            act.activation(gates[:, :], gates[:, :], ACT.Exp).then_inc(s_e, 1)

        @block.vector
        def _(dve):
            dve.wait_ge(s_w, 16 * 3)

            def front(i, p):
                dve.wait_ge(s_ap, i + 1)
                if since(i, 2):
                    dve.wait_ge(s_y, i - 1)
                dve.tensor_copy(a_t[:, p], ps_a[:, :]).then_inc(s_at, 1)

            def back(i, p):
                dve.wait_ge(s_y, i + 1)
                if since(i, 1):
                    dve.wait_ge(norm.s_done, i * TPC)
                dve.tensor_tensor(res[:, :], ps_y[:, :], x_rows[:, p], ALU.add).then_inc(s_res, 1)
                dve.wait_ge(s_res, i + 1)
                norm.statistics(dve, i, res)
                if since(i, 2):
                    dve.wait_ge(s_np, i - 1)
                    dve.wait_ge(s_kept, i - 1)
                norm.apply(dve, i, normed[:, p], res)
                dve.wait_ge(s_g, i + 1)
                out = logits[:, i * TPC:i * TPC + TPC] if isinstance(i, int) else logits[:, bass.ds(i * TPC, TPC)]
                dve.tensor_tensor(out, ps_g[:, :], bias_g[:, :].rearrange("p (o e) -> p o e", o=1).to_broadcast([P, TPC, NE]),
                                  ALU.add).then_inc(s_l, 1)
            staggered(dve, NCH, front, back)
            dve.wait_ge(s_const, CONSTS)
            dve.wait_ge(s_l, NCH)

            done = [0]

            def step(instruction):
                done[0] += 1
                instruction.then_inc(s_step, 1)
                dve.wait_ge(s_step, done[0])
            per_row = lambda a: a.rearrange("p (t o) -> p t o", o=1).to_broadcast([P, NT, NE])
            numbers = number[:, :].rearrange("p (o e) -> p o e", o=1).to_broadcast([P, NT, NE])
            step(dve.tensor_reduce(col[:, :], logits[:, :], AX.X, ALU.max))
            step(dve.tensor_tensor(gates[:, :], logits[:, :], per_row(col[:, :]), ALU.subtract))
            assert done[0] == STEP_SHIFTED
            dve.wait_ge(s_e, 1)
            step(dve.tensor_reduce(col[:, :], gates[:, :], AX.X, ALU.add))
            step(dve.reciprocal(col[:, :], col[:, :]))
            step(dve.tensor_tensor(gates[:, :], gates[:, :], per_row(col[:, :]), ALU.mult))
            step(dve.tensor_copy(rest[:, :], gates[:, :]))
            for r in range(TOPK):
                step(dve.tensor_reduce(weight[:, r], rest[:, :], AX.X, ALU.max))
                step(dve.tensor_tensor(tmp[:, :], rest[:, :], per_row(weight[:, r]), ALU.is_equal))
                step(dve.tensor_tensor(tmp[:, :], tmp[:, :], numbers, ALU.mult))
                step(dve.tensor_reduce(col[:, :], tmp[:, :], AX.X, ALU.max))
                step(dve.tensor_tensor(hot[:, r], numbers, per_row(col[:, :]), ALU.is_equal))
                if r + 1 < TOPK:
                    step(dve.scalar_tensor_tensor(flat(rest[:, :]), flat(hot[:, r]), -2.0, flat(rest[:, :]), ALU.mult, ALU.add))
            step(dve.tensor_tensor(both[:, :], hot[:, 0], hot[:, 1], ALU.add))
            assert done[0] == STEP_BOTH
            dve.wait_ge(s_count, 2)
            step(dve.tensor_copy(tmp[:, :], ps_c[:, 1].rearrange("p (t e) -> p t e", e=NE)))
            for e in range(NE):
                dve.tensor_tensor_scan(counted[:, :, e], ones[:, 0:NT], tmp[:, :, e], 0.0, ALU.mult, ALU.add).then_inc(s_scan, 1)
            dve.wait_ge(s_scan, NE)
            step(dve.tensor_scalar(tiles_i[:, :], counted[:, NT - 1], float(P - 1), None, ALU.add))
            step(dve.tensor_scalar(tiles_i[:, :], tiles_i[:, :], P.bit_length() - 1, None, ALU.logical_shift_right))
            step(dve.tensor_copy(tiles[:, :], tiles_i[:, :]))
            step(dve.tensor_tensor_scan(ends[:, :], ones[:, 0:NE], tiles[:, :], 0.0, ALU.mult, ALU.add))
            step(dve.tensor_tensor(tiles[:, :], ends[:, :], tiles[:, :], ALU.subtract))
            step(dve.tensor_tensor(place[:, :], counted[:, :], tmp[:, :], ALU.subtract))
            step(dve.tensor_tensor(place[:, :], place[:, :], ps_c[:, 0].rearrange("p (t e) -> p t e", e=NE), ALU.add))
            step(dve.tensor_scalar(tiles[:, :], tiles[:, :], float(P), None, ALU.mult))
            step(dve.tensor_tensor(place[:, :], place[:, :], tiles[:, :].rearrange("p (o e) -> p o e", o=1).to_broadcast([P, NT, NE]), ALU.add))
            for r in range(TOPK):
                step(dve.tensor_tensor(tmp[:, :], hot[:, r], place[:, :], ALU.mult))
                step(dve.tensor_reduce(col[:, :], tmp[:, :], AX.X, ALU.add))
                step(dve.tensor_copy(places[:, r], col[:, :]))
                assert done[0] == STEP_PLACES[r]
            step(dve.tensor_tensor(passed[:, :], tile_no[0:1, :].rearrange("p (t o) -> p t o", o=1).to_broadcast([1, SLOT_TILES, NE]),
                                   ends[0:1, :].rearrange("p (o e) -> p o e", o=1).to_broadcast([1, SLOT_TILES, NE]), ALU.is_ge))
            step(dve.tensor_reduce(owner[:, :], passed[:, :], AX.X, ALU.add))
            step(dve.tensor_scalar(tile_expert[:, :], owner[:, :], float(NE - 1), None, ALU.min))

        @block.gpsimd
        def _(pool):
            identity(pool, ident[:, :], s_made, s_const)
            pool.memset(eps[:, :], LN_EPS).then_inc(s_const, 1)
            pool.memset(ones[:, :], 1.0).then_inc(s_const, 1)
            pool.memset(before[:, :], 1.0).then_inc(s_made, 1)
            pool.wait_ge(s_made, 2)
            pool.affine_select(out=before[:, :], in_=before[:, :], compare_op=ALU.is_gt, fill=0.0, base=0,
                               pattern=[[1, P]], channel_multiplier=-1).then_inc(s_const, 1)
            pool.iota(number[:, :], [[1, NE]], base=1, channel_multiplier=0, allow_small_or_imprecise_dtypes=True).then_inc(s_const, 1)
            pool.iota(tile_no[:, :], [[1, SLOT_TILES]], base=0, channel_multiplier=0, allow_small_or_imprecise_dtypes=True).then_inc(s_const, 1)
            pool.wait_ge(s_kept, NCH)
            for r in range(TOPK):
                pool.wait_ge(s_step, STEP_PLACES[r])
                for t in range(NT):
                    pool.indirect_dma_start(out=sorted_rows, out_offset=bass.IndirectOffsetOnAxis(ap=places[:, r, t:t + 1], axis=0),
                                            in_=x1[:, t], in_offset=None).then_inc(s_put, 16)
            pool.wait_ge(s_put, 16 * TOPK * NT)


def experts(nc, b1, b3, b2, tile_expert, w1, w3, w2, sorted_rows, expert_rows):
    with ExitStack() as stack:
        n = Names(nc, stack, "exp")
        ident = n.sb("ident", [P, P])
        bias1 = n.sb("bias1", [P, NE, HID])
        bias3 = n.sb("bias3", [P, NE, HID])
        bias2 = n.sb("bias2", [P, NE, D])
        rows = n.sb("rows", [P, 4, D])
        rows_t = n.sb("rows_t", [P, 2, DK, P])
        left = n.sb("left", [P, 2, HID])
        right = n.sb("right", [P, 2, HID])
        product = n.sb("product", [P, 2, HID])
        hidden = n.sb("hidden", [P, 2, HID])
        hidden_t = n.sb("hidden_t", [P, 2, HK, P])
        result = n.sb("result", [P, 4, D])
        ps_x = n.ps("ps_x", [P, DK, P])
        ps_h = [[n.ps(f"ps_h{p}{i}", [P, HID]) for i in range(2)] for p in range(2)]
        ps_t = n.ps("ps_t", [P, HK, P])
        ps_y = [n.ps(f"ps_y{p}", [P, D]) for p in range(2)]

        s_made = n.sem("constants_begun")
        s_const = n.sem("constants")
        s_b = n.sem("biases_loaded")
        s_x = [n.sem(f"rows_loaded{i}") for i in range(4)]
        s_xp = n.sem("rows_turned")
        s_xt = n.sem("rows_t_ready")
        s_h = n.sem("hidden_projected")
        s_lr = n.sem("factors_ready")
        s_prod = n.sem("product_ready")
        s_act = n.sem("hidden_ready")
        s_hp = n.sem("hidden_turned")
        s_ht = n.sem("hidden_t_ready")
        s_y = n.sem("result_projected")
        s_r = n.sem("result_ready")
        s_out = [n.sem(f"result_stored{i}") for i in range(4)]
        block = stack.enter_context(nc.Block())

        rows_in = sorted_rows.rearrange("(s p) d -> s p d", p=P)
        rows_out = expert_rows.rearrange("(s p) d -> s p d", p=P)

        def expert(eng, s):
            cell = tile_expert[0:1, s:s + 1] if isinstance(s, int) else tile_expert[0:1, bass.ds(s, 1)]
            return eng.value_load(cell, min_val=0, max_val=NE - 1)

        def of_expert(tile, e):
            return tile[:, bass.ds(e, 1)].rearrange("p o h -> p (o h)")

        @block.sync
        def _(sp):
            for dst, src in ((bias1, b1), (bias3, b3), (bias2, b2)):
                sp.dma_start(dst[:, :].rearrange("p e h -> p (e h)"), src.rearrange("e h -> (e h)").partition_broadcast(P)).then_inc(s_b, 16)

            def load(s, p):
                if since(s, 4):
                    sp.wait_ge(s_xp, s - 3)
                sp.dma_start(rows[:, p], at(rows_in, s)).then_inc(s_x[p], 16)
            pipelined(sp, SLOT_TILES, [(load, 2)], body=4)

        @block.tensor
        def _(pe):
            pe.wait_ge(s_const, 1)

            def turn_in(s, p):
                pe.wait_ge(s_x[p], 16 * ((s >> 2) + 1))
                if since(s, 1):
                    pe.wait_ge(s_xt, s)
                for k in range(DK):
                    mm = pe.transpose(ps_x[:, k], rows[:, p, k * P:(k + 1) * P], ident[:, :])
                mm.then_inc(s_xp, 1)

            def project(s, p):
                p = p % 2
                e = expert(pe, s)
                pe.wait_ge(s_xt, s + 1)
                if since(s, 2):
                    pe.wait_ge(s_lr, 2 * (s - 1))
                for i, w in enumerate((w1, w3)):
                    for k in range(DK):
                        mm = pe.matmul(ps_h[p][i][:, :], rows_t[:, p, k], of_expert(w[:, k], e), start=(k == 0), stop=(k == DK - 1))
                    mm.then_inc(s_h, 1)

            def turn_hidden(s, p):
                pe.wait_ge(s_act, s + 1)
                if since(s, 1):
                    pe.wait_ge(s_ht, s)
                for k in range(HK):
                    mm = pe.transpose(ps_t[:, k], hidden[:, p % 2, k * P:(k + 1) * P], ident[:, :])
                mm.then_inc(s_hp, 1)

            def project_out(s, p):
                p = p % 2
                e = expert(pe, s)
                pe.wait_ge(s_ht, s + 1)
                if since(s, 2):
                    pe.wait_ge(s_r, s - 1)
                for k in range(HK):
                    mm = pe.matmul(ps_y[p][:, :], hidden_t[:, p, k], of_expert(w2[:, k], e), start=(k == 0), stop=(k == HK - 1))
                mm.then_inc(s_y, 1)
            pipelined(pe, SLOT_TILES, [(project, 1), (turn_in, 0), (project_out, 3), (turn_hidden, 2)], body=4)

        @block.vector
        def _(dve):
            dve.wait_ge(s_b, 48)

            def keep_rows(s, p):
                p = p % 2
                dve.wait_ge(s_xp, s + 1)
                if since(s, 2):
                    dve.wait_ge(s_h, 2 * (s - 1))
                dve.tensor_copy(rows_t[:, p], ps_x[:, :]).then_inc(s_xt, 1)

            def multiply(s, p):
                p = p % 2
                e = expert(dve, s)
                if since(s, 2):
                    dve.wait_ge(s_prod, s - 1)
                dve.wait_ge(s_h, 2 * s + 1)
                dve.tensor_tensor(left[:, p], ps_h[p][0][:, :], of_expert(bias1, e), ALU.add).then_inc(s_lr, 1)
                dve.wait_ge(s_h, 2 * s + 2)
                dve.tensor_tensor(right[:, p], ps_h[p][1][:, :], of_expert(bias3, e), ALU.add).then_inc(s_lr, 1)
                dve.wait_ge(s_lr, 2 * s + 2)
                if since(s, 2):
                    dve.wait_ge(s_act, s - 1)
                dve.tensor_tensor(product[:, p], left[:, p], right[:, p], ALU.mult).then_inc(s_prod, 1)

            def keep_result(s, p):
                e = expert(dve, s)
                dve.wait_ge(s_y, s + 1)
                if since(s, 4):
                    dve.wait_ge(s_out[p], 16 * (s >> 2))
                dve.tensor_tensor(result[:, p], ps_y[p % 2][:, :], of_expert(bias2, e), ALU.add).then_inc(s_r, 1)
            pipelined(dve, SLOT_TILES, [(multiply, 1), (keep_rows, 0), (keep_result, 3)], body=4)

        @block.scalar
        def _(act):
            def activate(s, p):
                p = p % 2
                act.wait_ge(s_prod, s + 1)
                if since(s, 2):
                    act.wait_ge(s_hp, s - 1)
                act.activation(hidden[:, p], product[:, p], ACT.Silu).then_inc(s_act, 1)

            def keep_hidden(s, p):
                p = p % 2
                act.wait_ge(s_hp, s + 1)
                if since(s, 2):
                    act.wait_ge(s_y, s - 1)
                act.copy(hidden_t[:, p], ps_t[:, :]).then_inc(s_ht, 1)
            pipelined(act, SLOT_TILES, [(activate, 1), (keep_hidden, 2)], body=4)

        @block.gpsimd
        def _(pool):
            identity(pool, ident[:, :], s_made, s_const)

            def store(s, p):
                pool.wait_ge(s_r, s + 1)
                pool.dma_start(at(rows_out, s), result[:, p]).then_inc(s_out[p], 16)
            pipelined(pool, SLOT_TILES, [(store, 2)], body=4)
            for p in range(4):
                pool.wait_ge(s_out[p], 16 * SLOT_TILES // 4)


def finish(nc, Wf, bf, x1, places, weight, expert_rows, out):
    with ExitStack() as stack:
        n = Names(nc, stack, "fin")
        ident = n.sb("ident", [P, P])
        eps = n.sb("eps", [P, 1])
        wf = n.sb("wf", [P, DK, D])
        bias = n.sb("bias", [P, D])
        picked = n.sb("picked", [P, 2, TOPK, TPC, D])
        mixed = n.sb("mixed", [P, 2, TPC, D])
        mixed_t = n.sb("mixed_t", [P, 2, DK, CH])
        x1_bias = n.sb("x1_bias", [P, 2, TPC, D])
        res = n.sb("res", [P, TPC, D])
        normed = n.sb("normed", [P, 2, TPC, D])
        norm = Norm(n)
        ps_m = n.ps("ps_m", [P, DK, CH])
        ps_y = n.ps("ps_y", [P, TPC, D])

        s_made = n.sem("constants_begun")
        s_const = n.sem("constants")
        s_w = n.sem("weights_loaded")
        s_pick = [n.sem(f"rows_picked{i}") for i in range(2)]
        s_first = n.sem("first_weighted")
        s_mix = n.sem("rows_mixed")
        s_mp = n.sem("mixed_turned")
        s_mt = n.sem("mixed_t_ready")
        s_y = n.sem("projected")
        s_xb = n.sem("x1_bias_ready")
        s_res = n.sem("residual_ready")
        s_out = [n.sem(f"rows_stored{i}") for i in range(2)]
        block = stack.enter_context(nc.Block())

        rows_out = out.rearrange("b (c t p) d -> (b c) p t d", p=P, t=TPC)

        @block.sync
        def _(sp):
            sp.dma_start(wf[:, :], Wf.rearrange("(k p) n -> p k n", p=P)).then_inc(s_w, 16)
            sp.dma_start(bias[:, :], bf.partition_broadcast(P)).then_inc(s_w, 16)

            def back(i, p):
                sp.wait_ge(norm.s_done, i * TPC + TPC)
                sp.dma_start(at(rows_out, i), normed[:, p]).then_inc(s_out[p], 16)
            staggered(sp, NCH, lambda i, p: None, back)
            for p in range(2):
                sp.wait_ge(s_out[p], 16 * NCH // 2)

        @block.gpsimd
        def _(pool):
            identity(pool, ident[:, :], s_made, s_const)
            pool.memset(eps[:, :], LN_EPS).then_inc(s_const, 1)
            pool.wait_ge(s_w, 32)
            for i in range(NCH):
                p = i % 2
                if i >= 2:
                    pool.wait_ge(s_mix, (i - 1) * TPC)
                for t in range(TPC):
                    for r in range(TOPK):
                        pool.indirect_dma_start(out=picked[:, p, r, t], out_offset=None, in_=expert_rows,
                                                in_offset=bass.IndirectOffsetOnAxis(ap=places[:, r, i * TPC + t:i * TPC + t + 1], axis=0)
                                                ).then_inc(s_pick[p], 16)
                if i >= 2:
                    pool.wait_ge(s_res, i - 1)
                pool.tensor_tensor(x1_bias[:, p], x1[:, i * TPC:(i + 1) * TPC],
                                   bias[:, :].rearrange("p (o d) -> p o d", o=1).to_broadcast([P, TPC, D]), ALU.add).then_inc(s_xb, 1)

        @block.tensor
        def _(pe):
            pe.wait_ge(s_const, 2)
            pe.wait_ge(s_w, 32)

            def front(i, p):
                pe.wait_ge(s_mix, i * TPC + TPC)
                if since(i, 1):
                    pe.wait_ge(s_mt, i)
                turn_rows(pe, ps_m, mixed[:, p], ident[:, :]).then_inc(s_mp, 1)
                pe.wait_ge(s_mt, i + 1)
                if since(i, 1):
                    pe.wait_ge(s_res, i)
                multiply_rows(pe, ps_y, mixed_t[:, p], wf).then_inc(s_y, 1)
            staggered(pe, NCH, front, lambda i, p: None)

        @block.scalar
        def _(act):
            act.wait_ge(s_const, 2)

            def front(i, p):
                act.wait_ge(s_mp, i + 1)
                if since(i, 2):
                    act.wait_ge(s_y, i - 1)
                act.copy(mixed_t[:, p], ps_m[:, :]).then_inc(s_mt, 1)

            def back(i, p):
                norm.inverse(act, i, eps[:, 0:1])
            staggered(act, NCH, front, back)

        @block.vector
        def _(dve):
            def front(i, p):
                dve.wait_ge(s_pick[p], 16 * TPC * TOPK * ((i >> 1) + 1))
                if since(i, 2):
                    dve.wait_ge(s_mp, i - 1)
                gate = lambda r, t: weight[:, r, i * TPC + t:i * TPC + t + 1] if isinstance(i, int) else weight[:, r, bass.ds(i * TPC + t, 1)]
                for t in range(TPC):
                    dve.tensor_scalar(mixed[:, p, t], picked[:, p, 0, t], gate(0, t), None, ALU.mult).then_inc(s_first, 1)
                for t in range(TPC):
                    dve.wait_ge(s_first, i * TPC + (t + 1))
                    dve.scalar_tensor_tensor(mixed[:, p, t], picked[:, p, 1, t], gate(1, t), mixed[:, p, t],
                                             ALU.mult, ALU.add).then_inc(s_mix, 1)

            def back(i, p):
                dve.wait_ge(s_y, i + 1)
                dve.wait_ge(s_xb, i + 1)
                if since(i, 1):
                    dve.wait_ge(norm.s_done, i * TPC)
                dve.tensor_tensor(res[:, :], ps_y[:, :], x1_bias[:, p], ALU.add).then_inc(s_res, 1)
                dve.wait_ge(s_res, i + 1)
                norm.statistics(dve, i, res)
                if since(i, 2):
                    dve.wait_ge(s_out[p], 16 * (i >> 1))
                norm.apply(dve, i, normed[:, p], res)
            staggered(dve, NCH, front, back)


def program(nc, x, Wq, Wk, Wv, Wo, Wqp, Wkp, lambda_raw, W1, b1, W3, b3, W2, b2, Wg, bg, Wf, bf, out):
    scratch = lambda name, shape: nc.dram_tensor(name, shape, F32).ap()
    q_parts = scratch("q_parts", [NCH, 6, D, CH])
    k_parts = scratch("k_parts", [NCH, 6, D, CH])
    v_rows = scratch("v_rows", [T, H * VW])
    attn_rows = scratch("attn_rows", [T, D])
    sorted_rows = scratch("sorted_rows", [SLOTS, D])
    expert_rows = scratch("expert_rows", [SLOTS, D])
    prepare(nc, x, Wq, Wk, Wv, Wqp, Wkp, lambda_raw, q_parts, k_parts, v_rows, sorted_rows)
    attend(nc, q_parts, k_parts, v_rows, attn_rows)
    with ExitStack() as stack:
        n = Names(nc, stack, "keep")
        x1 = n.sb("x1", [P, NT, D])
        places = n.sb("places", [P, TOPK, NT], U32)
        weight = n.sb("weight", [P, TOPK, NT])
        tile_expert = n.sb("tile_expert", [1, SLOT_TILES], I32)
        with ExitStack() as weights:
            m = Names(nc, weights, "keep")
            w1 = m.sb("w1", [P, DK, NE, HID])
            w3 = m.sb("w3", [P, DK, NE, HID])
            w2 = m.sb("w2", [P, HK, NE, D])
            route(nc, x, attn_rows, Wo, Wg, bg, W1, W3, W2, (x1, places, weight, tile_expert, w1, w3, w2), sorted_rows)
            experts(nc, b1, b3, b2, tile_expert, w1, w3, w2, sorted_rows, expert_rows)
        finish(nc, Wf, bf, x1, places, weight, expert_rows, out)


_INS = ['L0_attn_x', 'L0_attn_Wq', 'L0_attn_Wk', 'L0_attn_Wv', 'L0_attn_Wo', 'L0_attn_Wqp', 'L0_attn_Wkp',
        'L0_attn_lambda_raw', 'L0_ffn_W1', 'L0_ffn_b1', 'L0_ffn_W3', 'L0_ffn_b3', 'L0_ffn_W2', 'L0_ffn_b2',
        'L0_ffn_Wg', 'L0_ffn_bg', 'L0_ffn_Wf', 'L0_ffn_bf']


def kernel(**inputs):
    import numpy as _np
    import concourse.bacc as _bacc
    from concourse import mybir as _mybir
    from concourse.bass_utils import run_bass_kernel_spmd as _run

    nc = _bacc.Bacc("TRN2", target_bir_lowering=False, num_devices=1)
    arrays, args = {}, []
    for name in _INS:
        a = _np.ascontiguousarray(inputs[name])
        arrays[f"in_{name}_dram"] = a
        args.append(nc.dram_tensor(f"in_{name}_dram", a.shape, _mybir.dt.from_np(a.dtype), kind="ExternalInput").ap())
    args.append(nc.dram_tensor("out_0_dram", (B, S, D), F32, kind="ExternalOutput").ap())
    program(nc, *args)
    r = _run(nc, [arrays], core_ids=[0])
    return r.results[0]["out_0_dram"]
```

```python
from contextlib import ExitStack
import math

import concourse.bass as bass
from concourse import mybir

F32 = mybir.dt.float32
F32R = mybir.dt.float32r
BF16 = mybir.dt.bfloat16
I32 = mybir.dt.int32
U32 = mybir.dt.uint32
ACT = mybir.ActivationFunctionType
ALU = mybir.AluOpType
AX = mybir.AxisListType

P = 128
B, S, D, H = 2, 2048, 256, 16
HD = D // H
T = B * S
DK = D // P
FEAT = 3 * HD
SPLIT = 2 * FEAT
CH = 512
NCH = T // CH
TPC = CH // P
QUAD = 4
NQ = H // QUAD
NQ_BITS = NQ.bit_length() - 1
QC = S // CH
VW = 32
NE, HID, TOPK = 8, 512, 2
NT = T // P
HK = HID // P
SLOT_TILES = T * TOPK // P + NE
SLOTS = SLOT_TILES * P
AMP_EPS = 1e-6
LN_EPS = 1e-5
LAMBDA_MAX = 0.5
SCALE = 1.0 / math.sqrt(HD)
PI_BELOW = 3.1415925
MASKED = -1e30


class Names:

    def __init__(self, nc, stack, stage):
        self.nc, self.stack, self.stage = nc, stack, stage

    def sem(self, name):
        return self.stack.enter_context(self.nc.semaphore(f"{self.stage}_{name}"))

    def sb(self, name, shape, dt=F32):
        return self.stack.enter_context(self.nc.sbuf_tensor(f"{self.stage}_{name}", shape, dt))

    def ps(self, name, shape, dt=F32):
        return self.stack.enter_context(self.nc.psum_tensor(f"{self.stage}_{name}", shape, dt))


def staggered(eng, count, front, back):
    def pair(i):
        front(i + 1, 1)
        back(i, 0)
        front(i + 2, 0)
        back(i + 1, 1)

    front(0, 0)
    pair(0)
    with eng.Fori(1, count // 2 - 1) as j:
        pair(2 * j)
    front(count - 1, 1)
    back(count - 2, 0)
    back(count - 1, 1)


def pipelined(eng, count, stages, body=2):
    deepest = max(lag for _, lag in stages)
    lead = (deepest + 2 * body - 1) // body * body
    loops = (count - lead) // body
    if loops < 2:
        loops, lead = 0, count

    def iteration(i, u):
        for f, lag in stages:
            if not isinstance(i, int) or 0 <= i - lag < count:
                f(i - lag, (u - lag) % body)

    for i in range(lead):
        iteration(i, i)
    if loops:
        with eng.Fori(lead // body, lead // body + loops) as j:
            for u in range(body):
                iteration(body * j + u, u)
    for i in range(lead + body * loops, count + deepest):
        iteration(i, i)


def since(i, first):
    return not isinstance(i, int) or i >= first


def at(view, i):
    if isinstance(i, int):
        return view[i]
    rest = " ".join("bcdef"[:len(view.shape) - 2])
    return view[bass.ds(i, 1)].rearrange(f"o a {rest} -> (o a) {rest}")




def identity(pool, tile, begun, ready):
    pool.memset(tile, 0.0).then_inc(begun, 1)
    pool.wait_ge(begun, 1)
    pool.affine_select(out=tile, in_=tile, compare_op=ALU.not_equal, fill=1.0, base=0,
                       pattern=[[-1, P]], channel_multiplier=1).then_inc(ready, 1)


def absolute(dve, out, in_):
    return dve.tensor_scalar(out.bitcast(U32), in_.bitcast(U32), 0x7FFFFFFF, None, ALU.bitwise_and)


def prepare(nc, x, Wq, Wk, Wv, Wqp, Wkp, lambda_raw, q_parts, k_parts, v_rows):
    with ExitStack() as stack:
        n = Names(nc, stack, "pre")
        ident = n.sb("ident", [P, P])
        heads_mean = n.sb("heads_mean", [P, P])
        weights = n.sb("weights", [P, 5, DK, D])
        lam = n.sb("lam", [P, 2])
        lam_tanh = n.sb("lam_tanh", [P, 2])
        lam_scale = n.sb("lam_scale", [P, 2])
        consts = n.sb("consts", [P, 3])
        half_pi, amp_eps, one = consts[:, 0:1], consts[:, 1:2], consts[:, 2:3]
        x_rows = n.sb("x_rows", [P, 2, TPC, D])
        x_t = n.sb("x_t", [P, 2, DK, CH])
        qk = n.sb("qk", [P, 2, 4, CH])
        soft = n.sb("soft", [P, 4, CH])
        amp = n.sb("amp", [P, 2, 4, CH])
        amp_sq = n.sb("amp_sq", [P, 4, CH])
        rnorm = n.sb("rnorm", [P, 4, CH])
        normed = n.sb("normed", [P, 4, CH])
        phase = n.sb("phase", [P, 2, 4, CH])
        waves = n.sb("waves", [P, 2, 2, 4, CH])
        high = n.sb("high", [P, 3, 4, CH], F32R)
        low = n.sb("low", [P, 3, 4, CH], F32R)
        v_sb = n.sb("v_sb", [P, TPC, H, VW])
        ps_a = [n.ps(f"ps_a{k}", [P, CH]) for k in range(2)]
        ps_h = n.ps("ps_h", [P, 2, CH])
        ps_q = n.ps("ps_q", [P, 2, CH])
        ps_n = n.ps("ps_n", [P, 2, CH])

        s_w = n.sem("weights_loaded")
        s_const = n.sem("constants")
        s_const_made = n.sem("constants_begun")
        s_lam = n.sem("lambda_ready")
        s_ones = n.sem("value_ones")
        s_x = [n.sem(f"x_loaded{i}") for i in range(2)]
        s_xp = n.sem("x_transposed")
        s_xt = n.sem("x_t_ready")
        s_pp = n.sem("phase_projected")
        s_tanh = n.sem("phase_ready")
        s_qkp = n.sem("qk_projected")
        s_qk = n.sem("qk_ready")
        s_abs = n.sem("abs_ready")
        s_exp = n.sem("exp_ready")
        s_log = n.sem("log_ready")
        s_amp = n.sem("amp_ready")
        s_scaled = n.sem("q_scaled")
        s_sq = n.sem("amp_squared")
        s_norm = n.sem("norm_summed")
        s_ln = n.sem("norm_log")
        s_rn = n.sem("rnorm_ready")
        s_absp = n.sem("abs_phase")
        s_wave = [n.sem("cosine_ready"), n.sem("sine_ready")]
        s_an = n.sem("amp_normed")
        s_feat = n.sem("features_ready")
        s_high = [n.sem(f"high_ready{kind}") for kind in range(3)]
        s_low = [n.sem(f"low_ready{kind}") for kind in range(3)]
        s_vp = n.sem("v_projected")
        s_v = n.sem("v_ready")
        s_high_out = [n.sem(f"high_stored{kind}") for kind in range(3)]
        s_low_out = [n.sem(f"low_stored{kind}") for kind in range(3)]
        s_vout = n.sem("v_stored")
        block = stack.enter_context(nc.Block())

        CONSTS = 5
        Q, K = 0, 1
        STORED = 32
        HEADS = P // HD
        rows_in = x.rearrange("b (c t p) d -> (b c) p t d", p=P, t=TPC)
        rows_v = v_rows.rearrange("(c t p) w -> c p t w", p=P, t=TPC)

        @block.sync
        def _(sp):
            for w, src in enumerate((Wq, Wk, Wqp, Wkp, Wv)):
                sp.dma_start(weights[:, w], src.rearrange("(k p) n -> p k n", p=P)).then_inc(s_w, 16)
            for c in range(2):
                per_head = lambda_raw[c * HEADS:(c + 1) * HEADS].rearrange("(h o) -> h o", o=1)
                for h in range(HEADS):
                    sp.dma_start(lam[h * HD:(h + 1) * HD, c:c + 1],
                                 per_head[h:h + 1, :].to_broadcast([HD, 1])).then_inc(s_w, 16)

            def load(i, p):
                if since(i, 2):
                    sp.wait_ge(s_xp, 2 * (i - 1))
                sp.dma_start(x_rows[:, p], at(rows_in, i)).then_inc(s_x[p], 16)

            def store_v(i, p):
                sp.wait_ge(s_v, 2 * i + 2)
                sp.dma_start(at(rows_v, i), v_sb[:, :].rearrange("p t h w -> p t (h w)")).then_inc(s_vout, 16)

            def store(i, kind, part):
                tile, ready, stored = ((high, s_high, s_high_out), (low, s_low, s_low_out))[part]
                sp.wait_ge(ready[kind], i + 1)
                for side, parts in enumerate((q_parts, k_parts)):
                    to = parts[:, 3 * part + kind].rearrange("n (c r) t -> n r c t", c=2)
                    sp.dma_start(at(to, i), tile[:, kind, 2 * side:2 * side + 2].bitcast(F32)).then_inc(stored[kind], 16)

            pipelined(sp, NCH, [
                (load, 0),
                (lambda i, p: store(i, 0, 0), 2),
                (lambda i, p: store(i, 0, 1), 2),
                (lambda i, p: store(i, 1, 0), 3),
                (store_v, 1),
                (lambda i, p: store(i, 1, 1), 3),
                (lambda i, p: store(i, 2, 0), 3),
                (lambda i, p: store(i, 2, 1), 3)])
            sp.wait_ge(s_vout, 16 * NCH)
            for kind in range(3):
                sp.wait_ge(s_high_out[kind], STORED * NCH)
                sp.wait_ge(s_low_out[kind], STORED * NCH)

        @block.tensor
        def _(pe):
            pe.wait_ge(s_const, CONSTS)
            pe.wait_ge(s_w, 16 * (5 + H))

            def turn(i, p):
                pe.wait_ge(s_x[p], 16 * ((i >> 1) + 1))
                for k in range(DK):
                    if since(i, 1):
                        pe.wait_ge(s_v, 2 * i + (k - 1))
                    for t in range(TPC):
                        mm = pe.transpose(ps_a[k][:, t * P:(t + 1) * P], x_rows[:, p, t, k * P:(k + 1) * P], ident[:, :])
                    mm.then_inc(s_xp, 1)

            def project(weight, out, p):
                for c in range(2):
                    for k in range(DK):
                        mm = pe.matmul(out[:, c], weights[:, weight, k, c * P:(c + 1) * P], x_t[:, p, k],
                                       start=(k == 0), stop=(k == DK - 1))
                return mm

            def project_qk(i, p, side):
                if side == Q:
                    pe.wait_ge(s_xt, 2 * i + 2)
                if side == K or since(i, 1):
                    pe.wait_ge(s_qk, 2 * i + side)
                project(side, ps_q, p).then_inc(s_qkp, 1)

            def project_phase(i, p, side):
                if side == Q and since(i, 2):
                    pe.wait_ge(s_ln, 2 * (i - 1))
                if side == K or since(i, 1):
                    pe.wait_ge(s_tanh, 2 * i + side)
                project(2 + side, ps_h, p).then_inc(s_pp, 1)

            def project_v(i, p):
                for half in range(2):
                    for t in range(2):
                        tokens = slice((2 * half + t) * P, (2 * half + t + 1) * P)
                        for k in range(DK):
                            mm = pe.matmul(ps_a[half][:, t * D:(t + 1) * D], x_t[:, p, k, tokens], weights[:, 4, k],
                                           start=(k == 0), stop=(k == DK - 1))
                    mm.then_inc(s_vp, 1)

            def sum_norm(i, p, side):
                if side == Q:
                    pe.wait_ge(s_sq, i + 1)
                    if since(i, 1):
                        pe.wait_ge(s_ln, 2 * i - 1)
                else:
                    pe.wait_ge(s_tanh, min(2 * i + 4, 2 * NCH) if isinstance(i, int) else 2 * i + 4)
                    if isinstance(i, int) and i == NCH - 1:
                        pe.wait_ge(s_ln, 2 * i)
                for c in range(2):
                    mm = pe.matmul((ps_n, ps_h)[side][:, c], heads_mean[:, :], amp_sq[:, 2 * side + c], start=True, stop=True)
                mm.then_inc(s_norm, 1)

            pipelined(pe, NCH, [
                (lambda i, p: project_qk(i, p, Q), 1),
                (lambda i, p: project_phase(i, p, Q), 1),
                (lambda i, p: project_qk(i, p, K), 1),
                (lambda i, p: project_phase(i, p, K), 1),
                (lambda i, p: sum_norm(i, p, Q), 2),
                (project_v, 1),
                (lambda i, p: sum_norm(i, p, K), 2),
                (turn, 0)])

        @block.scalar
        def _(act):
            act.wait_ge(s_w, 16 * (5 + H))
            act.activation(lam_tanh[:, :], lam[:, :], ACT.Tanh).then_inc(s_lam, 1)
            act.wait_ge(s_const, CONSTS)

            def phases(i, p, side):
                act.wait_ge(s_pp, 2 * i + side + 1)
                if since(i, 2):
                    act.wait_ge(s_wave[1], i - 1)
                    act.wait_ge(s_absp, i - 1)
                act.activation(phase[:, p, 2 * side:2 * side + 2], ps_h[:, :], ACT.Tanh).then_inc(s_tanh, 1)

            def soft_exp(i, p):
                act.wait_ge(s_abs, 2 * i + 2)
                act.activation(soft[:, :], soft[:, :], ACT.Exp, scale=-1.0).then_inc(s_exp, 1)

            def soft_log(i, p):
                act.wait_ge(s_exp, i + 1)
                act.activation(soft[:, :], soft[:, :], ACT.Ln, bias=one).then_inc(s_log, 1)

            def norm_log(i, p, side):
                act.wait_ge(s_norm, 2 * i + side + 1)
                if since(i, 1):
                    act.wait_ge(s_an, i)
                act.activation(rnorm[:, 2 * side:2 * side + 2], (ps_n, ps_h)[side][:, :], ACT.Ln, bias=amp_eps).then_inc(s_ln, 1)

            def norm_exp(i, p):
                act.wait_ge(s_ln, 2 * i + 2)
                act.activation(rnorm[:, :], rnorm[:, :], ACT.Exp, scale=-0.5).then_inc(s_rn, 1)

            def make_waves(i, p):
                act.wait_ge(s_absp, i + 1)
                act.activation(waves[:, p, 0], waves[:, p, 0], ACT.Sin, bias=half_pi, scale=-PI_BELOW).then_inc(s_wave[0], 1)
                act.wait_ge(s_tanh, 2 * i + 2)
                if since(i, 2):
                    act.wait_ge(s_low[2], i - 1)
                act.activation(waves[:, p, 1], phase[:, p], ACT.Sin, scale=PI_BELOW).then_inc(s_wave[1], 1)

            pipelined(act, NCH, [
                (lambda i, p: phases(i, p, Q), 1),
                (norm_exp, 3),
                (soft_exp, 1),
                (lambda i, p: phases(i, p, K), 1),
                (soft_log, 1),
                (lambda i, p: norm_log(i, p, Q), 2),
                (lambda i, p: norm_log(i, p, K), 2),
                (make_waves, 2)])

        @block.vector
        def _(dve):
            dve.memset(v_sb[:, :, :, :], 0.0).then_inc(s_ones, 1)
            dve.wait_ge(s_ones, 1)
            dve.memset(v_sb[:, :, :, HD:HD + 1], 1.0).then_inc(s_ones, 1)
            dve.wait_ge(s_ones, 2)
            dve.wait_ge(s_lam, 1)
            dve.tensor_scalar(lam_scale[:, :], lam_tanh[:, :], LAMBDA_MAX * SCALE, None, ALU.mult).then_inc(s_lam, 1)
            dve.wait_ge(s_lam, 2)

            def keep_x(i, p):
                for k in range(DK):
                    dve.wait_ge(s_xp, 2 * i + k + 1)
                    if since(i, 2):
                        dve.wait_ge(s_vp, 2 * (i - 1))
                        dve.wait_ge(s_pp, 2 * (i - 1))
                    dve.tensor_copy(x_t[:, p, k], ps_a[k][:, :]).then_inc(s_xt, 1)

            def keep_v(i, p):
                for half in range(2):
                    dve.wait_ge(s_vp, 2 * i + half + 1)
                    if since(i, 1):
                        dve.wait_ge(s_vout, 16 * i)
                    dve.tensor_copy(v_sb[:, 2 * half:2 * half + 2, :, 0:HD].rearrange("p t h d -> p (t h) d"),
                                    ps_a[half][:, :].rearrange("p (t d) -> p t d", d=HD)).then_inc(s_v, 1)

            def keep_qk(i, p, side):
                dve.wait_ge(s_qkp, 2 * i + side + 1)
                if since(i, 2):
                    dve.wait_ge(s_low[0], i - 1)
                mine = slice(2 * side, 2 * side + 2)
                dve.tensor_copy(qk[:, p, mine], ps_q[:, :]).then_inc(s_qk, 1)
                dve.wait_ge(s_qk, 2 * i + side + 1)
                if since(i, 1):
                    dve.wait_ge(s_amp, i)
                absolute(dve, soft[:, mine], qk[:, p, mine]).then_inc(s_abs, 1)

            def amplitudes(i, p):
                dve.wait_ge(s_log, i + 1)
                if since(i, 2):
                    dve.wait_ge(s_an, i - 1)
                    dve.wait_ge(s_sq, i - 1)
                flat = "p c t -> p (c t)"
                dve.scalar_tensor_tensor(amp[:, p].rearrange(flat), qk[:, p].rearrange(flat), 0.0,
                                         soft[:, :].rearrange(flat), ALU.max, ALU.add).then_inc(s_amp, 1)

            def abs_phase(i, p):
                dve.wait_ge(s_tanh, 2 * i + 2)
                if since(i, 2):
                    dve.wait_ge(s_low[1], i - 1)
                absolute(dve, waves[:, p, 0], phase[:, p]).then_inc(s_absp, 1)

            def norm_amplitudes(i, p):
                dve.wait_ge(s_rn, i + 1)
                if since(i, 1):
                    dve.wait_ge(s_feat, 6 * i)
                dve.tensor_tensor(normed[:, :], amp[:, p], rnorm[:, :], ALU.mult).then_inc(s_an, 1)

            def take_high(i, kind, whole):
                if since(i, 1):
                    dve.wait_ge(s_low[kind], i)
                    dve.wait_ge(s_high_out[kind], STORED * i)
                dve.tensor_copy(high[:, kind], whole).then_inc(s_high[kind], 1)

            def scale_q(i, p):
                dve.wait_ge(s_amp, i + 1)
                dve.tensor_scalar(qk[:, p, 0:2], qk[:, p, 0:2], SCALE, None, ALU.mult).then_inc(s_scaled, 1)
                dve.wait_ge(s_scaled, i + 1)
                take_high(i, 0, qk[:, p])

            def features(i, p, f):
                dve.wait_ge(s_an, i + 1)
                dve.wait_ge(s_wave[f], i + 1)
                for c in range(2):
                    dve.scalar_tensor_tensor(waves[:, p, f, c], normed[:, c], lam_scale[:, c:c + 1], waves[:, p, f, c],
                                             ALU.mult, ALU.mult).then_inc(s_feat, 1)
                dve.tensor_tensor(waves[:, p, f, 2:4], normed[:, 2:4], waves[:, p, f, 2:4], ALU.mult).then_inc(s_feat, 1)
                dve.wait_ge(s_feat, 6 * i + 3 * (f + 1))
                take_high(i, 1 + f, waves[:, p, f])

            pipelined(dve, NCH, [
                (lambda i, p: keep_qk(i, p, Q), 1),
                (abs_phase, 2),
                (norm_amplitudes, 3),
                (lambda i, p: keep_qk(i, p, K), 1),
                (lambda i, p: features(i, p, 0), 3),
                (keep_v, 1),
                (amplitudes, 1),
                (keep_x, 0),
                (lambda i, p: features(i, p, 1), 3),
                (scale_q, 1)])

        @block.gpsimd
        def _(pool):
            pool.memset(consts[:, 0:1], math.pi / 2).then_inc(s_const, 1)
            pool.memset(consts[:, 1:2], AMP_EPS).then_inc(s_const, 1)
            pool.memset(consts[:, 2:3], 1.0).then_inc(s_const, 1)
            identity(pool, ident[:, :], s_const_made, s_const)
            pool.memset(heads_mean[:, :], 1.0 / HD).then_inc(s_const_made, 1)
            pool.wait_ge(s_const_made, 2)
            blocks = heads_mean[:, :].rearrange("p (g d) -> p g d", d=HD)
            pool.affine_select(out=blocks, in_=blocks, compare_op=ALU.is_ge, fill=0.0, base=0,
                               pattern=[[-HD, HEADS], [0, HD]], channel_multiplier=1).then_inc(s_const_made, 1)
            pool.wait_ge(s_const_made, 3)
            pool.affine_select(out=blocks, in_=blocks, compare_op=ALU.is_ge, fill=0.0, base=HD - 1,
                               pattern=[[HD, HEADS], [0, HD]], channel_multiplier=-1).then_inc(s_const, 1)

            def split(i, kind, whole):
                pool.wait_ge(s_high[kind], i + 1)
                if since(i, 1):
                    pool.wait_ge(s_low_out[kind], STORED * i)
                pool.tensor_tensor(low[:, kind], whole, high[:, kind].bitcast(F32), ALU.subtract).then_inc(s_low[kind], 1)

            def square(i, p):
                pool.wait_ge(s_amp, i + 1)
                if since(i, 1):
                    pool.wait_ge(s_norm, 2 * i)
                pool.tensor_tensor(amp_sq[:, :], amp[:, p], amp[:, p], ALU.mult).then_inc(s_sq, 1)

            pipelined(pool, NCH, [
                (lambda i, p: split(i, 0, qk[:, p]), 2),
                (lambda i, p: split(i, 1, waves[:, p, 0]), 3),
                (square, 1),
                (lambda i, p: split(i, 2, waves[:, p, 1]), 3)])


BLOCKS = [4 * (c + 1) for c in range(QC)]
FIRST = [sum(BLOCKS[:c]) for c in range(QC)]
STEPS = sum(BLOCKS)
AHEAD = 3
MAXIMA = [QUAD * TPC * (c + 1) for c in range(QC)]
EARLY = sum(MAXIMA[:AHEAD])
PER_QUAD = sum(MAXIMA)


def max_tiles(chunks):
    return [(nxt, c, h, q, k) for nxt, c in chunks for h in range(QUAD) for q in range(TPC) for k in range(c + 1)]


def attend_plan(last):
    tiles = max_tiles([(False, c) for c in range(AHEAD, QC)] + ([] if last else [(True, c) for c in range(AHEAD)]))
    columns = [CH - P * max(0, s - FIRST[c] - TPC * c) for c in range(QC) for s in range(FIRST[c], FIRST[c] + BLOCKS[c])]
    late = 5 * sum(columns[0:BLOCKS[0]])
    total, passed, at_ = 5 * sum(columns) - late, -late, 0
    plan, turns = [], []

    def fill(cols):
        nonlocal passed, at_
        passed += cols
        while at_ < min(len(tiles), PER_QUAD * passed // total + 1):
            plan.append(("max",) + tiles[at_])
            nxt, c, h, q, k = tiles[at_]
            if (h, q, k) == (QUAD - 1, TPC - 1, c):
                turns.append(("turn_max", nxt, c))
            at_ += 1

    for s in range(STEPS):
        for pair in range(2):
            plan.append(("scores", s, pair))
            if pair == 0:
                plan += turns
                turns.clear()
            fill(2 * columns[s])
        if s >= 1:
            plan.append(("values", s - 1))
            fill(columns[s])
            if s in FIRST:
                turns.append(("turn_out", FIRST.index(s) - 1))
        if s == STEPS - 1:
            plan.append(("values", s))
    while at_ < len(tiles):
        fill(total)
    plan += turns
    plan.append(("turn_out", QC - 1))
    return plan


def wait_positive(eng, sem, value):
    if not isinstance(value, int) or value > 0:
        eng.wait_ge(sem, value)


def quads(eng, quad):
    quad(0, False)
    with eng.Fori(1, B * NQ - 1) as g:
        quad(g, False)
    quad(B * NQ - 1, True)


def attend(nc, q_parts, k_parts, v_rows, attn_rows, sorted_rows):
    with ExitStack() as stack:
        n = Names(nc, stack, "att")
        ident = n.sb("ident", [P, P])
        zeros = n.sb("zeros", [P, D])
        ident_b = n.sb("ident_b", [P, P], BF16)
        future = n.sb("future", [P, P], BF16)
        future_t = n.sb("future_t", [P, P], BF16)
        q_same = n.sb("q_same", [SPLIT + 1, QC, QUAD, CH], F32R)
        q_swap = n.sb("q_swap", [SPLIT, QC, QUAD, CH], F32R)
        keys = n.sb("keys", [SPLIT + 1, QUAD, QC, CH], F32R)
        keys_next = n.sb("keys_next", [SPLIT, QUAD, AHEAD, CH], F32R)
        values = n.sb("values", [P, S // P, QUAD * VW])
        probs = n.sb("probs", [P, 4, QUAD, CH])
        maxima = n.sb("maxima", [P, 2, QUAD * TPC, QC])
        neg_max = n.sb("neg_max", [P, 2, QUAD * TPC])
        max_row = n.sb("max_row", [QUAD * TPC, 2, P], F32R)
        out_t = n.sb("out_t", [P, CH])
        inv_sum = n.sb("inv_sum", [P, TPC * QUAD])
        out_rows = n.sb("out_rows", [P, 2, TPC, QUAD * HD])
        ps_s = [n.ps(f"ps_s{i}", [P, 2, CH]) for i in range(2)]
        ps_m = [n.ps(f"ps_m{i}", [P, CH]) for i in range(2)]
        ps_o = n.ps("ps_o", [P, CH])
        ps_t = n.ps("ps_t", [P, CH])

        s_made = n.sem("constants_begun")
        s_const = n.sem("constants")
        s_q = [n.sem(f"q_loaded{c}") for c in range(QC)]
        s_k = [n.sem(f"k_loaded{c}") for c in range(QC)]
        s_kn = [n.sem(f"next_k_loaded{c}") for c in range(AHEAD)]
        s_v = [n.sem(f"v_loaded{c}") for c in range(QC)]
        s_scores = n.sem("scores_ready")
        s_exp = n.sem("probs_ready")
        s_pv = n.sem("values_summed")
        s_mt = n.sem("max_tile_ready")
        s_mr = n.sem("max_tile_read")
        s_neg = n.sem("neg_max_ready")
        s_turn = n.sem("max_turned")
        s_row = n.sem("max_row_ready")
        s_m = [n.sem(f"max_row_placed{c}") for c in range(QC)]
        s_oc = n.sem("out_copied")
        s_ot = n.sem("out_turned")
        s_inv = n.sem("inverse_ready")
        s_or = n.sem("out_rows_ready")
        s_store = [n.sem(f"out_stored{i}") for i in range(2)]
        s_clear = n.sem("places_cleared")
        block = stack.enter_context(nc.Block())

        CONSTS = 5
        cleared = sorted_rows.rearrange("(c a p) d -> c p a d", c=SLOT_TILES // 8, p=P)
        CLEARS = SLOT_TILES // 8
        Q_LOADS, K_LOADS = 3 * QUAD, QUAD
        heads_q = q_parts.rearrange("n g (h d) t -> n h g d t", d=HD)
        heads_k = k_parts.rearrange("n g (h d) t -> n h g d t", d=HD)
        rows_v = v_rows.rearrange("(n k p) w -> n p k w", k=TPC, p=P)
        rows_o = attn_rows.rearrange("(n k p) w -> n p k w", k=TPC, p=P)

        def place(eng, g):
            chunk, head = (g >> NQ_BITS & (B - 1)) * QC, (g & (NQ - 1)) * QUAD
            return (chunk, head) if isinstance(g, int) else (eng.snap(chunk), eng.snap(head))

        def of_head(view, where, c, h, lo, hi):
            n_, h_ = where[0] + c, where[1] + h
            if isinstance(n_, int):
                return view[n_, h_, lo:hi]
            return view[bass.ds(n_, 1), bass.ds(h_, 1), lo:hi].rearrange("n h g d t -> (n h g) d t")

        def in_rows(view, where, c, width):
            n_, w_ = where[0] + c, where[1] * width
            if isinstance(n_, int):
                return view[n_, :, :, w_:w_ + QUAD * width]
            return view[bass.ds(n_, 1), :, :, bass.ds(w_, QUAD * width)].rearrange("n p k w -> (n p) k w")

        @block.sync
        def _(sp):
            KINDS = 3

            def load_q(where, c):
                for h in range(QUAD):
                    sp.dma_start(q_same[0:SPLIT, c, h].bitcast(F32), of_head(heads_q, where, c, h, 0, 2 * KINDS)).then_inc(s_q[c], 16)
                    sp.dma_start(q_swap[0:FEAT, c, h].bitcast(F32), of_head(heads_q, where, c, h, KINDS, 2 * KINDS)).then_inc(s_q[c], 16)
                    sp.dma_start(q_swap[FEAT:SPLIT, c, h].bitcast(F32), of_head(heads_q, where, c, h, 0, KINDS)).then_inc(s_q[c], 16)

            def load_k(where, c):
                for h in range(QUAD):
                    sp.dma_start(keys[0:SPLIT, h, c].bitcast(F32), of_head(heads_k, where, c, h, 0, 2 * KINDS)).then_inc(s_k[c], 16)

            def load_kn(where, c):
                for h in range(QUAD):
                    sp.dma_start(keys_next[:, h, c].bitcast(F32), of_head(heads_k, where, c, h, 0, 2 * KINDS)).then_inc(s_kn[c], 16)

            def load_v(where, c):
                sp.dma_start(values[:, TPC * c:TPC * c + TPC], in_rows(rows_v, where, c, VW)).then_inc(s_v[c], 16)

            def place_max(g, c, turned):
                sp.wait_ge(s_row, turned)
                sp.dma_start(q_same[SPLIT:SPLIT + 1, c].bitcast(F32), max_row[:, c % 2].bitcast(F32)).then_inc(s_m[c], 16)

            def scored(g, step):
                sp.wait_ge(s_scores, g * (2 * STEPS) + 2 * step)

            for c in range(AHEAD):
                load_kn((0, 0), c)
                load_q((0, 0), c)
            for c in range(QC):
                load_k((0, 0), c)
                load_v((0, 0), c)
            load_q((0, 0), 3)
            place_max(0, 0, 1)
            place_max(0, 1, 2)

            def quad(g, last):
                after = None if last else place(sp, g + 1)
                if not last:
                    sp.wait_ge(s_mt, g * PER_QUAD + EARLY)
                    for c in range(AHEAD):
                        load_kn(after, c)
                place_max(g, 2, g * QC + 3)
                if not last:
                    scored(g, FIRST[1])
                    load_q(after, 0)
                place_max(g, 3, g * QC + 4)
                if not last:
                    scored(g, FIRST[2])
                    load_q(after, 1)
                    place_max(g + 1, 0, g * QC + 5)
                    scored(g, FIRST[3])
                    load_q(after, 2)
                    place_max(g + 1, 1, g * QC + 6)
                    for c in range(QC):
                        scored(g, FIRST[3] + TPC * (c + 1))
                        load_k(after, c)
                        sp.wait_ge(s_pv, g * STEPS + (FIRST[3] + TPC * (c + 1)))
                        load_v(after, c)
                    load_q(after, 3)
            quads(sp, quad)

        @block.tensor
        def _(pe):
            pe.wait_ge(s_const, CONSTS)

            def max_tile(g, nxt, c, h, q, k, before, number):
                if (h, q) == (0, 0):
                    gg = g + 1 if nxt else g
                    if k == 0:
                        pe.wait_ge(s_q[c], 16 * Q_LOADS * (gg + 1))
                    if c < AHEAD:
                        pe.wait_ge(s_kn[k], 16 * K_LOADS * (gg + 1))
                    else:
                        pe.wait_ge(s_k[k], 16 * K_LOADS * (gg + 1))
                wait_positive(pe, s_mr, before + (number - 1))
                width = CH if k < c else P * (q + 1)
                key = keys_next[:, h, k, 0:width] if c < AHEAD else keys[0:SPLIT, h, k, 0:width]
                buf = ps_m[number % 2]
                mm = pe.matmul(buf[:, 0:width], q_same[0:SPLIT, c, h, P * q:P * q + P], key, start=True, stop=(k < c))
                if k == c:
                    mm = pe.matmul(buf[:, P * q:P * q + P], ident_b[:, :], future[:, :], start=False, stop=True)
                mm.then_inc(s_mt, 1)

            def turn_max(c, maxes, outs):
                pe.wait_ge(s_neg, maxes + 1)
                wait_positive(pe, s_row, maxes)
                wait_positive(pe, s_or, outs)
                pe.transpose(ps_t[0:QUAD * TPC, 0:P], neg_max[:, c % 2], ident[:, :]).then_inc(s_turn, 1)

            def scores(g, s, pair):
                c = max(c for c in range(QC) if FIRST[c] <= s)
                k = s - FIRST[c]
                skip = P * max(0, k - TPC * c)
                if k == 0 and pair == 0:
                    pe.wait_ge(s_m[c], 16 * (g + 1))
                    pe.wait_ge(s_q[c], 16 * Q_LOADS * (g + 1))
                if k % TPC == 0 and pair == 0:
                    pe.wait_ge(s_k[k // TPC], 16 * K_LOADS * (g + 1))
                wait_positive(pe, s_exp, g * (2 * STEPS) + (2 * s + pair - 1))
                for e in range(2):
                    h = 2 * pair + e
                    out = ps_s[pair][:, e, skip:CH]
                    kk = slice(P * (k % TPC), P * (k % TPC) + P)
                    pe.matmul(out, keys[0:SPLIT + 1, h, k // TPC, kk], q_same[0:SPLIT + 1, c, h, skip:CH],
                              start=True, stop=False)
                    if k >= TPC * c:
                        pe.matmul(ps_s[pair][:, e, skip:skip + P], ident_b[:, :], future_t[:, :],
                                  start=False, stop=False)
                    mm = pe.matmul(out, keys[0:SPLIT, h, k // TPC, kk], q_swap[0:SPLIT, c, h, skip:CH],
                                   start=False, stop=True)
                mm.then_inc(s_scores, 1)

            def sum_values(g, s):
                c = max(c for c in range(QC) if FIRST[c] <= s)
                k = s - FIRST[c]
                skip = P * max(0, k - TPC * c)
                pe.wait_ge(s_exp, g * (2 * STEPS) + 2 * (s + 1))
                if k % TPC == 0:
                    pe.wait_ge(s_v[k // TPC], 16 * (g + 1))
                if k == 0:
                    wait_positive(pe, s_oc, g * QC + c)
                for h in range(QUAD):
                    mm = pe.matmul(ps_o[VW * h:VW * h + VW, skip:CH], values[:, k, VW * h:VW * h + VW],
                                   probs[:, s % 4, h, skip:CH], start=(k == 0), stop=(k == BLOCKS[c] - 1))
                mm.then_inc(s_pv, 1)

            def turn_out(g, c, maxes):
                pe.wait_ge(s_oc, g * QC + (c + 1))
                pe.wait_ge(s_row, maxes)
                wait_positive(pe, s_or, g * QC + c)
                for q in range(TPC):
                    mm = pe.transpose(ps_t[:, P * q:P * q + P], out_t[:, P * q:P * q + P], ident[:, :])
                mm.then_inc(s_ot, 1)

            for number, (nxt, c, h, q, k) in enumerate(max_tiles([(False, c) for c in range(AHEAD)])):
                max_tile(0, nxt, c, h, q, k, 0, number)
                if c >= 1 and (h, q, k) == (0, 1, 0):
                    turn_max(c - 1, c - 1, 0)
            turn_max(AHEAD - 1, AHEAD - 1, 0)

            def quad(g, last):
                number, maxes, outs = 0, 0, 0
                for event, *what in attend_plan(last):
                    if event == "scores":
                        scores(g, *what)
                    elif event == "values":
                        sum_values(g, what[0])
                    elif event == "max":
                        max_tile(g, *what, g * PER_QUAD + EARLY, number)
                        number += 1
                    elif event == "turn_max":
                        turn_max(what[1], g * QC + (AHEAD + maxes), g * QC + outs)
                        maxes += 1
                    elif event == "turn_out":
                        turn_out(g, what[0], g * QC + (AHEAD + maxes))
                        outs += 1
            quads(pe, quad)

        @block.scalar
        def _(act):
            def quad(g, last):
                for s in range(STEPS):
                    c = max(c for c in range(QC) if FIRST[c] <= s)
                    skip = P * max(0, s - FIRST[c] - TPC * c)
                    wait_positive(act, s_pv, g * STEPS + (s - 3))
                    for pair in range(2):
                        act.wait_ge(s_scores, g * (2 * STEPS) + (2 * s + pair + 1))
                        act.activation(probs[:, s % 4, 2 * pair:2 * pair + 2, skip:CH], ps_s[pair][:, :, skip:CH],
                                       ACT.Exp).then_inc(s_exp, 1)
            quads(act, quad)

        @block.vector
        def _(dve):
            dve.memset(keys[SPLIT:SPLIT + 1, :, :, :].bitcast(F32), 1.0).then_inc(s_const, 1)

            def read_max(nxt, c, h, q, k, before, number):
                dve.wait_ge(s_mt, before + (number + 1))
                width = CH if k < c else P * (q + 1)
                dve.tensor_reduce(maxima[:, c % 2, h * TPC + q, k:k + 1], ps_m[number % 2][:, 0:width], AX.X,
                                  ALU.max).then_inc(s_mr, 1)

            def negate(c, number, turned):
                dve.wait_ge(s_mr, number + 1)
                wait_positive(dve, s_turn, turned)
                dve.tensor_reduce(neg_max[:, c % 2], maxima[:, c % 2, :, 0:c + 1], AX.X, ALU.max,
                                  negate=True).then_inc(s_neg, 1)

            def keep_row(c, turned, placed):
                dve.wait_ge(s_turn, turned)
                if placed is not None:
                    dve.wait_ge(s_m[(c + 2) % QC], placed)
                dve.tensor_copy(max_row[:, c % 2], ps_t[0:QUAD * TPC, 0:P]).then_inc(s_row, 1)

            number = 0
            for nxt, c, h, q, k in max_tiles([(False, c) for c in range(AHEAD)]):
                read_max(nxt, c, h, q, k, 0, number)
                if (h, q, k) == (QUAD - 1, TPC - 1, c):
                    negate(c, number, c - 1)
                number += 1
                if c >= 1 and (h, q, k) == (0, 1, 0):
                    keep_row(c - 1, c, None)
            keep_row(AHEAD - 1, AHEAD, 16)

            def quad(g, last):
                number, negs, maxes = 0, 0, 0
                for event, *what in attend_plan(last):
                    if event == "max":
                        read_max(*what, g * PER_QUAD + EARLY, number)
                        nxt, c, h, q, k = what
                        if (h, q, k) == (QUAD - 1, TPC - 1, c):
                            negate(c, g * PER_QUAD + (EARLY + number), g * QC + (AHEAD + negs - 1))
                            negs += 1
                        number += 1
                    elif event == "turn_max":
                        keep_row(what[1], g * QC + (AHEAD + 1 + maxes), 16 * (g + (1 + (AHEAD - 2 + maxes) // QC)))
                        maxes += 1
                    elif event == "values" and what[0] + 1 in FIRST + [STEPS]:
                        c = (FIRST + [STEPS]).index(what[0] + 1) - 1
                        dve.wait_ge(s_pv, g * STEPS + (what[0] + 1))
                        wait_positive(dve, s_ot, g * QC + c)
                        dve.tensor_copy(out_t[:, :], ps_o[:, :]).then_inc(s_oc, 1)
                    elif event == "turn_out":
                        c = what[0]
                        dve.wait_ge(s_ot, g * QC + (c + 1))
                        turned = ps_t[:, :].rearrange("p (j w) -> p j w", w=VW)
                        wait_positive(dve, s_or, g * QC + c)
                        dve.reciprocal(inv_sum[:, :].rearrange("p (j o) -> p j o", o=1), turned[:, :, HD:HD + 1]).then_inc(s_inv, 1)
                        dve.wait_ge(s_inv, g * QC + (c + 1))
                        wait_positive(dve, s_store[c % 2], 16 * (g * 2 + c // 2))
                        dve.tensor_tensor(out_rows[:, c % 2].rearrange("p q (h d) -> p (q h) d", d=HD), turned[:, :, 0:HD],
                                          inv_sum[:, :].rearrange("p (j o) -> p j o", o=1).to_broadcast([P, TPC * QUAD, HD]),
                                          ALU.mult).then_inc(s_or, 1)
            quads(dve, quad)

        @block.gpsimd
        def _(pool):
            identity(pool, ident[:, :], s_made, s_const)
            pool.memset(ident_b[:, :], 0.0).then_inc(s_made, 1)
            pool.memset(future[:, :], 0.0).then_inc(s_made, 1)
            pool.memset(future_t[:, :], 0.0).then_inc(s_made, 1)
            pool.wait_ge(s_made, 4)
            pool.affine_select(out=future_t[:, :], in_=future_t[:, :], compare_op=ALU.is_ge, fill=MASKED, base=0,
                               pattern=[[1, P]], channel_multiplier=-1).then_inc(s_const, 1)
            pool.affine_select(out=ident_b[:, :], in_=ident_b[:, :], compare_op=ALU.not_equal, fill=1.0, base=0,
                               pattern=[[-1, P]], channel_multiplier=1).then_inc(s_const, 1)
            pool.affine_select(out=future[:, :], in_=future[:, :], compare_op=ALU.is_ge, fill=MASKED, base=0,
                               pattern=[[-1, P]], channel_multiplier=1).then_inc(s_const, 1)

            pool.memset(zeros[:, :], 0.0).then_inc(s_made, 1)
            pool.wait_ge(s_made, 5)
            for c in range(CLEARS):
                pool.dma_start(cleared[c], zeros[:, :].rearrange("p (o d) -> p o d", o=1).to_broadcast([P, 8, D])).then_inc(s_clear, 16)

            def store(g, where, c):
                pool.wait_ge(s_or, g * QC + (c + 1))
                pool.dma_start(in_rows(rows_o, where, c, HD), out_rows[:, c % 2]).then_inc(s_store[c % 2], 16)

            with pool.Fori(0, B * NQ) as g:
                where = place(pool, g)
                for c in range(QC):
                    store(g, where, c)
            for i in range(2):
                pool.wait_ge(s_store[i], 16 * B * NQ * QC // 2)
            pool.wait_ge(s_clear, 16 * CLEARS)
STEP_SHIFTED = 2
STEP_BOTH = STEP_SHIFTED + 4 + 5 * TOPK + (TOPK - 1) + 1
STEP_PLACES = [STEP_BOTH + 10 + 3 * (r + 1) for r in range(TOPK)]


def flat(a):
    return a.rearrange("p t e -> p (t e)")


class Norm:

    def __init__(self, n):
        self.stats = n.sb("stats", [P, TPC, 6])
        self.moments = n.sb("moments", [P, 4, TPC])
        self.mean, self.var, self.m2, self.gap = (self.moments[:, i] for i in range(4))
        self.rstd = n.sb("rstd", [P, TPC])
        self.s_stats = n.sem("stats_ready")
        self.s_step = n.sem("variance_step")
        self.s_var = n.sem("variance_ready")
        self.s_log = n.sem("variance_log")
        self.s_rstd = n.sem("rstd_ready")
        self.s_done = n.sem("rows_normed")

    def statistics(self, dve, i, rows):
        if since(i, 1):
            dve.wait_ge(self.s_done, i * TPC)
        for t in range(TPC):
            dve.bn_stats(self.stats[:, t], rows[:, t]).then_inc(self.s_stats, 1)
        even_mean, even_m2, odd_mean, odd_m2 = (self.stats[:, :, j] for j in (1, 2, 4, 5))
        dve.wait_ge(self.s_stats, i * TPC + TPC)
        dve.tensor_tensor(self.mean, even_mean, odd_mean, ALU.add).then_inc(self.s_step, 1)
        dve.tensor_tensor(self.gap, even_mean, odd_mean, ALU.subtract).then_inc(self.s_step, 1)
        dve.tensor_tensor(self.m2, even_m2, odd_m2, ALU.add).then_inc(self.s_step, 1)
        dve.wait_ge(self.s_step, i * 6 + 3)
        dve.tensor_scalar(self.mean, self.mean, 0.5, None, ALU.mult).then_inc(self.s_step, 1)
        dve.scalar_tensor_tensor(self.gap, self.gap, 0.25, self.gap, ALU.mult, ALU.mult).then_inc(self.s_step, 1)
        dve.tensor_scalar(self.m2, self.m2, 1.0 / D, None, ALU.mult).then_inc(self.s_step, 1)
        dve.wait_ge(self.s_step, i * 6 + 6)
        dve.tensor_tensor(self.var, self.m2, self.gap, ALU.add).then_inc(self.s_var, 1)

    def inverse(self, act, i, eps):
        act.wait_ge(self.s_var, i + 1)
        if since(i, 1):
            act.wait_ge(self.s_done, i * TPC)
        act.activation(self.rstd[:, :], self.var, ACT.Ln, bias=eps).then_inc(self.s_log, 1)
        act.wait_ge(self.s_log, i + 1)
        act.activation(self.rstd[:, :], self.rstd[:, :], ACT.Exp, scale=-0.5).then_inc(self.s_rstd, 1)

    def apply(self, dve, i, out, rows):
        dve.wait_ge(self.s_rstd, i + 1)
        for t in range(TPC):
            dve.tensor_scalar(out[:, t], rows[:, t], self.mean[:, t:t + 1], self.rstd[:, t:t + 1],
                              ALU.subtract, ALU.mult).then_inc(self.s_done, 1)


def turn_rows(pe, out, rows, ident):
    for t in range(TPC):
        for k in range(DK):
            mm = pe.transpose(out[:, k, t * P:(t + 1) * P], rows[:, t, k * P:(k + 1) * P], ident)
    return mm


def multiply_rows(pe, out, turned, weight):
    for t in range(TPC):
        for k in range(DK):
            mm = pe.matmul(out[:, t], turned[:, k, t * P:(t + 1) * P], weight[:, k], start=(k == 0), stop=(k == DK - 1))
    return mm


def route(nc, x, attn_rows, Wo, Wg, bg, W1, W3, W2, keep, sorted_rows):
    x1, places, weight, tile_expert, w1, w3, w2 = keep
    with ExitStack() as stack:
        n = Names(nc, stack, "route")
        ident = n.sb("ident", [P, P])
        before = n.sb("before", [P, P])
        ones = n.sb("ones", [P, P])
        eps = n.sb("eps", [P, 1])
        wo = n.sb("wo", [P, DK, D])
        wg = n.sb("wg", [P, DK, NE])
        bias_g = n.sb("bias_g", [P, NE])
        a_rows = n.sb("a_rows", [P, 2, TPC, D])
        a_t = n.sb("a_t", [P, 2, DK, CH])
        x_rows = n.sb("x_rows", [P, 2, TPC, D])
        res = n.sb("res", [P, TPC, D])
        normed = n.sb("normed", [P, 2, TPC, D])
        x1_t = n.sb("x1_t", [P, DK, CH])
        norm = Norm(n)
        logits = n.sb("logits", [P, NT, NE])
        gates = n.sb("gates", [P, NT, NE])
        rest = n.sb("rest", [P, NT, NE])
        hot = n.sb("hot", [P, TOPK, NT, NE])
        tmp = n.sb("tmp", [P, NT, NE])
        both = n.sb("both", [P, NT, NE])
        col = n.sb("col", [P, NT])
        number = n.sb("number", [P, NE])
        tile_no = n.sb("tile_no", [P, SLOT_TILES])
        counted = n.sb("counted", [P, NT, NE])
        place = n.sb("place", [P, NT, NE])
        tiles_i = n.sb("tiles_i", [P, NE], I32)
        tiles = n.sb("tiles", [P, NE])
        ends = n.sb("ends", [P, NE])
        passed = n.sb("passed", [1, SLOT_TILES, NE])
        owner = n.sb("owner", [1, SLOT_TILES])
        ps_a = n.ps("ps_a", [P, DK, CH])
        ps_y = n.ps("ps_y", [P, TPC, D])
        ps_n = n.ps("ps_n", [P, DK, CH])
        ps_g = n.ps("ps_g", [P, TPC, NE])
        ps_c = n.ps("ps_c", [P, 2, NT * NE])

        s_made = n.sem("constants_begun")
        s_const = n.sem("constants")
        s_w = n.sem("weights_loaded")
        s_expert = n.sem("expert_weights_loaded")
        s_in = [n.sem(f"rows_loaded{i}") for i in range(2)]
        s_ap = n.sem("attention_turned")
        s_at = n.sem("attention_t_ready")
        s_y = n.sem("projected")
        s_res = n.sem("residual_ready")
        s_kept = n.sem("x1_kept")
        s_np = n.sem("x1_turned")
        s_nt = n.sem("x1_t_ready")
        s_g = n.sem("gates_projected")
        s_l = n.sem("logits_ready")
        s_step = n.sem("routing_step")
        s_e = n.sem("gates_exp")
        s_count = n.sem("counts_ready")
        s_scan = n.sem("running_sums")
        s_put = n.sem("rows_put")
        block = stack.enter_context(nc.Block())

        CONSTS = 6
        rows_a = attn_rows.rearrange("(c t p) d -> c p t d", t=TPC, p=P)
        rows_in = x.rearrange("b (c t p) d -> (b c) p t d", p=P, t=TPC)

        @block.sync
        def _(sp):
            sp.dma_start(wo[:, :], Wo.rearrange("(k p) n -> p k n", p=P)).then_inc(s_w, 16)
            sp.dma_start(wg[:, :], Wg.rearrange("(k p) n -> p k n", p=P)).then_inc(s_w, 16)
            sp.dma_start(bias_g[:, :], bg.partition_broadcast(P)).then_inc(s_w, 16)

            def front(i, p):
                if since(i, 2):
                    sp.wait_ge(s_ap, i - 1)
                    sp.wait_ge(s_res, i - 1)
                sp.dma_start(a_rows[:, p], at(rows_a, i)).then_inc(s_in[p], 16)
                sp.dma_start(x_rows[:, p], at(rows_in, i)).then_inc(s_in[p], 16)

            def back(i, p):
                pass
            staggered(sp, NCH, front, back)
            for k in range(DK):
                for dst, src in ((w1, W1), (w3, W3)):
                    sp.dma_start(dst[:, k], src[:, k * P:(k + 1) * P].rearrange("e p h -> p e h")).then_inc(s_expert, 16)
            for k in range(HK):
                sp.dma_start(w2[:, k], W2[:, k * P:(k + 1) * P].rearrange("e p n -> p e n")).then_inc(s_expert, 16)
            sp.wait_ge(s_expert, 16 * (2 * DK + HK))

        @block.tensor
        def _(pe):
            pe.wait_ge(s_const, CONSTS)
            pe.wait_ge(s_w, 16 * 3)

            def front(i, p):
                pe.wait_ge(s_in[p], 32 * ((i >> 1) + 1))
                if since(i, 1):
                    pe.wait_ge(s_at, i)
                turn_rows(pe, ps_a, a_rows[:, p], ident[:, :]).then_inc(s_ap, 1)
                pe.wait_ge(s_at, i + 1)
                if since(i, 1):
                    pe.wait_ge(s_res, i)
                multiply_rows(pe, ps_y, a_t[:, p], wo).then_inc(s_y, 1)

            def back(i, p):
                pe.wait_ge(norm.s_done, i * TPC + TPC)
                if since(i, 1):
                    pe.wait_ge(s_nt, i)
                turn_rows(pe, ps_n, normed[:, p], ident[:, :]).then_inc(s_np, 1)
                pe.wait_ge(s_nt, i + 1)
                if since(i, 1):
                    pe.wait_ge(s_l, i)
                multiply_rows(pe, ps_g, x1_t, wg).then_inc(s_g, 1)
            staggered(pe, NCH, front, back)
            pe.wait_ge(s_step, STEP_BOTH)
            pe.matmul(ps_c[:, 0], before[:, :], both[:, :].rearrange("p t e -> p (t e)"), start=True, stop=True).then_inc(s_count, 1)
            pe.matmul(ps_c[:, 1], ones[:, :], both[:, :].rearrange("p t e -> p (t e)"), start=True, stop=True).then_inc(s_count, 1)

        @block.scalar
        def _(act):
            act.wait_ge(s_const, CONSTS)

            def front(i, p):
                pass

            def back(i, p):
                norm.inverse(act, i, eps[:, 0:1])
                act.wait_ge(norm.s_done, i * TPC + TPC)
                x1_chunk = x1[:, i * TPC:i * TPC + TPC] if isinstance(i, int) else x1[:, bass.ds(i * TPC, TPC)]
                act.copy(x1_chunk, normed[:, p]).then_inc(s_kept, 1)
                act.wait_ge(s_np, i + 1)
                if since(i, 1):
                    act.wait_ge(s_g, i)
                act.copy(x1_t[:, :], ps_n[:, :]).then_inc(s_nt, 1)
            staggered(act, NCH, front, back)
            act.wait_ge(s_step, STEP_SHIFTED)
            act.activation(gates[:, :], gates[:, :], ACT.Exp).then_inc(s_e, 1)

        @block.vector
        def _(dve):
            dve.wait_ge(s_w, 16 * 3)

            def front(i, p):
                dve.wait_ge(s_ap, i + 1)
                if since(i, 2):
                    dve.wait_ge(s_y, i - 1)
                dve.tensor_copy(a_t[:, p], ps_a[:, :]).then_inc(s_at, 1)

            def back(i, p):
                dve.wait_ge(s_y, i + 1)
                if since(i, 1):
                    dve.wait_ge(norm.s_done, i * TPC)
                dve.tensor_tensor(res[:, :], ps_y[:, :], x_rows[:, p], ALU.add).then_inc(s_res, 1)
                dve.wait_ge(s_res, i + 1)
                norm.statistics(dve, i, res)
                if since(i, 2):
                    dve.wait_ge(s_np, i - 1)
                    dve.wait_ge(s_kept, i - 1)
                norm.apply(dve, i, normed[:, p], res)
                dve.wait_ge(s_g, i + 1)
                out = logits[:, i * TPC:i * TPC + TPC] if isinstance(i, int) else logits[:, bass.ds(i * TPC, TPC)]
                dve.tensor_tensor(out, ps_g[:, :], bias_g[:, :].rearrange("p (o e) -> p o e", o=1).to_broadcast([P, TPC, NE]),
                                  ALU.add).then_inc(s_l, 1)
            staggered(dve, NCH, front, back)
            dve.wait_ge(s_const, CONSTS)
            dve.wait_ge(s_l, NCH)

            done = [0]

            def step(instruction):
                done[0] += 1
                instruction.then_inc(s_step, 1)
                dve.wait_ge(s_step, done[0])
            per_row = lambda a: a.rearrange("p (t o) -> p t o", o=1).to_broadcast([P, NT, NE])
            numbers = number[:, :].rearrange("p (o e) -> p o e", o=1).to_broadcast([P, NT, NE])
            step(dve.tensor_reduce(col[:, :], logits[:, :], AX.X, ALU.max))
            step(dve.tensor_tensor(gates[:, :], logits[:, :], per_row(col[:, :]), ALU.subtract))
            assert done[0] == STEP_SHIFTED
            dve.wait_ge(s_e, 1)
            step(dve.tensor_reduce(col[:, :], gates[:, :], AX.X, ALU.add))
            step(dve.reciprocal(col[:, :], col[:, :]))
            step(dve.tensor_tensor(gates[:, :], gates[:, :], per_row(col[:, :]), ALU.mult))
            step(dve.tensor_copy(rest[:, :], gates[:, :]))
            for r in range(TOPK):
                step(dve.tensor_reduce(weight[:, r], rest[:, :], AX.X, ALU.max))
                step(dve.tensor_tensor(tmp[:, :], rest[:, :], per_row(weight[:, r]), ALU.is_equal))
                step(dve.tensor_tensor(tmp[:, :], tmp[:, :], numbers, ALU.mult))
                step(dve.tensor_reduce(col[:, :], tmp[:, :], AX.X, ALU.max))
                step(dve.tensor_tensor(hot[:, r], numbers, per_row(col[:, :]), ALU.is_equal))
                if r + 1 < TOPK:
                    step(dve.scalar_tensor_tensor(flat(rest[:, :]), flat(hot[:, r]), -2.0, flat(rest[:, :]), ALU.mult, ALU.add))
            step(dve.tensor_tensor(both[:, :], hot[:, 0], hot[:, 1], ALU.add))
            assert done[0] == STEP_BOTH
            dve.wait_ge(s_count, 2)
            step(dve.tensor_copy(tmp[:, :], ps_c[:, 1].rearrange("p (t e) -> p t e", e=NE)))
            for e in range(NE):
                dve.tensor_tensor_scan(counted[:, :, e], ones[:, 0:NT], tmp[:, :, e], 0.0, ALU.mult, ALU.add).then_inc(s_scan, 1)
            dve.wait_ge(s_scan, NE)
            step(dve.tensor_scalar(tiles_i[:, :], counted[:, NT - 1], float(P - 1), None, ALU.add))
            step(dve.tensor_scalar(tiles_i[:, :], tiles_i[:, :], P.bit_length() - 1, None, ALU.logical_shift_right))
            step(dve.tensor_copy(tiles[:, :], tiles_i[:, :]))
            step(dve.tensor_tensor_scan(ends[:, :], ones[:, 0:NE], tiles[:, :], 0.0, ALU.mult, ALU.add))
            step(dve.tensor_tensor(tiles[:, :], ends[:, :], tiles[:, :], ALU.subtract))
            step(dve.tensor_tensor(place[:, :], counted[:, :], tmp[:, :], ALU.subtract))
            step(dve.tensor_tensor(place[:, :], place[:, :], ps_c[:, 0].rearrange("p (t e) -> p t e", e=NE), ALU.add))
            step(dve.tensor_scalar(tiles[:, :], tiles[:, :], float(P), None, ALU.mult))
            step(dve.tensor_tensor(place[:, :], place[:, :], tiles[:, :].rearrange("p (o e) -> p o e", o=1).to_broadcast([P, NT, NE]), ALU.add))
            for r in range(TOPK):
                step(dve.tensor_tensor(tmp[:, :], hot[:, r], place[:, :], ALU.mult))
                step(dve.tensor_reduce(col[:, :], tmp[:, :], AX.X, ALU.add))
                step(dve.tensor_copy(places[:, r], col[:, :]))
                assert done[0] == STEP_PLACES[r]
            step(dve.tensor_tensor(passed[:, :], tile_no[0:1, :].rearrange("p (t o) -> p t o", o=1).to_broadcast([1, SLOT_TILES, NE]),
                                   ends[0:1, :].rearrange("p (o e) -> p o e", o=1).to_broadcast([1, SLOT_TILES, NE]), ALU.is_ge))
            step(dve.tensor_reduce(owner[:, :], passed[:, :], AX.X, ALU.add))
            step(dve.tensor_scalar(tile_expert[:, :], owner[:, :], float(NE - 1), None, ALU.min))

        @block.gpsimd
        def _(pool):
            identity(pool, ident[:, :], s_made, s_const)
            pool.memset(eps[:, :], LN_EPS).then_inc(s_const, 1)
            pool.memset(ones[:, :], 1.0).then_inc(s_const, 1)
            pool.memset(before[:, :], 1.0).then_inc(s_made, 1)
            pool.wait_ge(s_made, 2)
            pool.affine_select(out=before[:, :], in_=before[:, :], compare_op=ALU.is_gt, fill=0.0, base=0,
                               pattern=[[1, P]], channel_multiplier=-1).then_inc(s_const, 1)
            pool.iota(number[:, :], [[1, NE]], base=1, channel_multiplier=0, allow_small_or_imprecise_dtypes=True).then_inc(s_const, 1)
            pool.iota(tile_no[:, :], [[1, SLOT_TILES]], base=0, channel_multiplier=0, allow_small_or_imprecise_dtypes=True).then_inc(s_const, 1)
            pool.wait_ge(s_kept, NCH)
            for r in range(TOPK):
                pool.wait_ge(s_step, STEP_PLACES[r])
                for t in range(NT):
                    pool.indirect_dma_start(out=sorted_rows, out_offset=bass.IndirectOffsetOnAxis(ap=places[:, r, t:t + 1], axis=0),
                                            in_=x1[:, t], in_offset=None).then_inc(s_put, 16)
            pool.wait_ge(s_put, 16 * TOPK * NT)


def experts(nc, b1, b3, b2, tile_expert, w1, w3, w2, sorted_rows, expert_rows):
    with ExitStack() as stack:
        n = Names(nc, stack, "exp")
        ident = n.sb("ident", [P, P])
        bias1 = n.sb("bias1", [P, NE, HID])
        bias3 = n.sb("bias3", [P, NE, HID])
        bias2 = n.sb("bias2", [P, NE, D])
        rows = n.sb("rows", [P, 4, D])
        rows_t = n.sb("rows_t", [P, 2, DK, P])
        left = n.sb("left", [P, 2, HID])
        right = n.sb("right", [P, 2, HID])
        product = n.sb("product", [P, 2, HID])
        hidden = n.sb("hidden", [P, 2, HID])
        hidden_t = n.sb("hidden_t", [P, 2, HK, P])
        result = n.sb("result", [P, 4, D])
        ps_x = n.ps("ps_x", [P, DK, P])
        ps_h = [[n.ps(f"ps_h{p}{i}", [P, HID]) for i in range(2)] for p in range(2)]
        ps_t = n.ps("ps_t", [P, HK, P])
        ps_y = [n.ps(f"ps_y{p}", [P, D]) for p in range(2)]

        s_made = n.sem("constants_begun")
        s_const = n.sem("constants")
        s_b = n.sem("biases_loaded")
        s_x = [n.sem(f"rows_loaded{i}") for i in range(4)]
        s_xp = n.sem("rows_turned")
        s_xt = n.sem("rows_t_ready")
        s_h = n.sem("hidden_projected")
        s_lr = n.sem("factors_ready")
        s_prod = n.sem("product_ready")
        s_act = n.sem("hidden_ready")
        s_hp = n.sem("hidden_turned")
        s_ht = n.sem("hidden_t_ready")
        s_y = n.sem("result_projected")
        s_r = n.sem("result_ready")
        s_out = [n.sem(f"result_stored{i}") for i in range(4)]
        block = stack.enter_context(nc.Block())

        rows_in = sorted_rows.rearrange("(s p) d -> s p d", p=P)
        rows_out = expert_rows.rearrange("(s p) d -> s p d", p=P)

        def expert(eng, s):
            cell = tile_expert[0:1, s:s + 1] if isinstance(s, int) else tile_expert[0:1, bass.ds(s, 1)]
            return eng.value_load(cell, min_val=0, max_val=NE - 1)

        def of_expert(tile, e):
            return tile[:, bass.ds(e, 1)].rearrange("p o h -> p (o h)")

        @block.sync
        def _(sp):
            for dst, src in ((bias1, b1), (bias3, b3), (bias2, b2)):
                sp.dma_start(dst[:, :].rearrange("p e h -> p (e h)"), src.rearrange("e h -> (e h)").partition_broadcast(P)).then_inc(s_b, 16)

            def load(s, p):
                if since(s, 4):
                    sp.wait_ge(s_xp, s - 3)
                sp.dma_start(rows[:, p], at(rows_in, s)).then_inc(s_x[p], 16)
            pipelined(sp, SLOT_TILES, [(load, 2)], body=4)

        @block.tensor
        def _(pe):
            pe.wait_ge(s_const, 1)

            def turn_in(s, p):
                pe.wait_ge(s_x[p], 16 * ((s >> 2) + 1))
                if since(s, 1):
                    pe.wait_ge(s_xt, s)
                for k in range(DK):
                    mm = pe.transpose(ps_x[:, k], rows[:, p, k * P:(k + 1) * P], ident[:, :])
                mm.then_inc(s_xp, 1)

            def project(s, p):
                p = p % 2
                e = expert(pe, s)
                pe.wait_ge(s_xt, s + 1)
                if since(s, 2):
                    pe.wait_ge(s_lr, 2 * (s - 1))
                for i, w in enumerate((w1, w3)):
                    for k in range(DK):
                        mm = pe.matmul(ps_h[p][i][:, :], rows_t[:, p, k], of_expert(w[:, k], e), start=(k == 0), stop=(k == DK - 1))
                    mm.then_inc(s_h, 1)

            def turn_hidden(s, p):
                pe.wait_ge(s_act, s + 1)
                if since(s, 1):
                    pe.wait_ge(s_ht, s)
                for k in range(HK):
                    mm = pe.transpose(ps_t[:, k], hidden[:, p % 2, k * P:(k + 1) * P], ident[:, :])
                mm.then_inc(s_hp, 1)

            def project_out(s, p):
                p = p % 2
                e = expert(pe, s)
                pe.wait_ge(s_ht, s + 1)
                if since(s, 2):
                    pe.wait_ge(s_r, s - 1)
                for k in range(HK):
                    mm = pe.matmul(ps_y[p][:, :], hidden_t[:, p, k], of_expert(w2[:, k], e), start=(k == 0), stop=(k == HK - 1))
                mm.then_inc(s_y, 1)
            pipelined(pe, SLOT_TILES, [(project, 1), (turn_in, 0), (project_out, 3), (turn_hidden, 2)], body=4)

        @block.vector
        def _(dve):
            dve.wait_ge(s_b, 48)

            def keep_rows(s, p):
                p = p % 2
                dve.wait_ge(s_xp, s + 1)
                if since(s, 2):
                    dve.wait_ge(s_h, 2 * (s - 1))
                dve.tensor_copy(rows_t[:, p], ps_x[:, :]).then_inc(s_xt, 1)

            def multiply(s, p):
                p = p % 2
                e = expert(dve, s)
                if since(s, 2):
                    dve.wait_ge(s_prod, s - 1)
                dve.wait_ge(s_h, 2 * s + 1)
                dve.tensor_tensor(left[:, p], ps_h[p][0][:, :], of_expert(bias1, e), ALU.add).then_inc(s_lr, 1)
                dve.wait_ge(s_h, 2 * s + 2)
                dve.tensor_tensor(right[:, p], ps_h[p][1][:, :], of_expert(bias3, e), ALU.add).then_inc(s_lr, 1)
                dve.wait_ge(s_lr, 2 * s + 2)
                if since(s, 2):
                    dve.wait_ge(s_act, s - 1)
                dve.tensor_tensor(product[:, p], left[:, p], right[:, p], ALU.mult).then_inc(s_prod, 1)

            def keep_result(s, p):
                e = expert(dve, s)
                dve.wait_ge(s_y, s + 1)
                if since(s, 4):
                    dve.wait_ge(s_out[p], 16 * (s >> 2))
                dve.tensor_tensor(result[:, p], ps_y[p % 2][:, :], of_expert(bias2, e), ALU.add).then_inc(s_r, 1)
            pipelined(dve, SLOT_TILES, [(multiply, 1), (keep_rows, 0), (keep_result, 3)], body=4)

        @block.scalar
        def _(act):
            def activate(s, p):
                p = p % 2
                act.wait_ge(s_prod, s + 1)
                if since(s, 2):
                    act.wait_ge(s_hp, s - 1)
                act.activation(hidden[:, p], product[:, p], ACT.Silu).then_inc(s_act, 1)

            def keep_hidden(s, p):
                p = p % 2
                act.wait_ge(s_hp, s + 1)
                if since(s, 2):
                    act.wait_ge(s_y, s - 1)
                act.copy(hidden_t[:, p], ps_t[:, :]).then_inc(s_ht, 1)
            pipelined(act, SLOT_TILES, [(activate, 1), (keep_hidden, 2)], body=4)

        @block.gpsimd
        def _(pool):
            identity(pool, ident[:, :], s_made, s_const)

            def store(s, p):
                pool.wait_ge(s_r, s + 1)
                pool.dma_start(at(rows_out, s), result[:, p]).then_inc(s_out[p], 16)
            pipelined(pool, SLOT_TILES, [(store, 2)], body=4)
            for p in range(4):
                pool.wait_ge(s_out[p], 16 * SLOT_TILES // 4)


def finish(nc, Wf, bf, x1, places, weight, expert_rows, out):
    with ExitStack() as stack:
        n = Names(nc, stack, "fin")
        ident = n.sb("ident", [P, P])
        eps = n.sb("eps", [P, 1])
        wf = n.sb("wf", [P, DK, D])
        bias = n.sb("bias", [P, D])
        picked = n.sb("picked", [P, 2, TOPK, TPC, D])
        mixed = n.sb("mixed", [P, 2, TPC, D])
        mixed_t = n.sb("mixed_t", [P, 2, DK, CH])
        x1_bias = n.sb("x1_bias", [P, 2, TPC, D])
        res = n.sb("res", [P, TPC, D])
        normed = n.sb("normed", [P, 2, TPC, D])
        norm = Norm(n)
        ps_m = n.ps("ps_m", [P, DK, CH])
        ps_y = n.ps("ps_y", [P, TPC, D])

        s_made = n.sem("constants_begun")
        s_const = n.sem("constants")
        s_w = n.sem("weights_loaded")
        s_pick = [n.sem(f"rows_picked{i}") for i in range(2)]
        s_first = n.sem("first_weighted")
        s_mix = n.sem("rows_mixed")
        s_mp = n.sem("mixed_turned")
        s_mt = n.sem("mixed_t_ready")
        s_y = n.sem("projected")
        s_xb = n.sem("x1_bias_ready")
        s_res = n.sem("residual_ready")
        s_out = [n.sem(f"rows_stored{i}") for i in range(2)]
        block = stack.enter_context(nc.Block())

        rows_out = out.rearrange("b (c t p) d -> (b c) p t d", p=P, t=TPC)

        @block.sync
        def _(sp):
            sp.dma_start(wf[:, :], Wf.rearrange("(k p) n -> p k n", p=P)).then_inc(s_w, 16)
            sp.dma_start(bias[:, :], bf.partition_broadcast(P)).then_inc(s_w, 16)

            def back(i, p):
                sp.wait_ge(norm.s_done, i * TPC + TPC)
                sp.dma_start(at(rows_out, i), normed[:, p]).then_inc(s_out[p], 16)
            staggered(sp, NCH, lambda i, p: None, back)
            for p in range(2):
                sp.wait_ge(s_out[p], 16 * NCH // 2)

        @block.gpsimd
        def _(pool):
            identity(pool, ident[:, :], s_made, s_const)
            pool.memset(eps[:, :], LN_EPS).then_inc(s_const, 1)
            pool.wait_ge(s_w, 32)
            for i in range(NCH):
                p = i % 2
                if i >= 2:
                    pool.wait_ge(s_mix, (i - 1) * TPC)
                for t in range(TPC):
                    for r in range(TOPK):
                        pool.indirect_dma_start(out=picked[:, p, r, t], out_offset=None, in_=expert_rows,
                                                in_offset=bass.IndirectOffsetOnAxis(ap=places[:, r, i * TPC + t:i * TPC + t + 1], axis=0)
                                                ).then_inc(s_pick[p], 16)
                if i >= 2:
                    pool.wait_ge(s_res, i - 1)
                pool.tensor_tensor(x1_bias[:, p], x1[:, i * TPC:(i + 1) * TPC],
                                   bias[:, :].rearrange("p (o d) -> p o d", o=1).to_broadcast([P, TPC, D]), ALU.add).then_inc(s_xb, 1)

        @block.tensor
        def _(pe):
            pe.wait_ge(s_const, 2)
            pe.wait_ge(s_w, 32)

            def front(i, p):
                pe.wait_ge(s_mix, i * TPC + TPC)
                if since(i, 1):
                    pe.wait_ge(s_mt, i)
                turn_rows(pe, ps_m, mixed[:, p], ident[:, :]).then_inc(s_mp, 1)
                pe.wait_ge(s_mt, i + 1)
                if since(i, 1):
                    pe.wait_ge(s_res, i)
                multiply_rows(pe, ps_y, mixed_t[:, p], wf).then_inc(s_y, 1)
            staggered(pe, NCH, front, lambda i, p: None)

        @block.scalar
        def _(act):
            act.wait_ge(s_const, 2)

            def front(i, p):
                act.wait_ge(s_mp, i + 1)
                if since(i, 2):
                    act.wait_ge(s_y, i - 1)
                act.copy(mixed_t[:, p], ps_m[:, :]).then_inc(s_mt, 1)

            def back(i, p):
                norm.inverse(act, i, eps[:, 0:1])
            staggered(act, NCH, front, back)

        @block.vector
        def _(dve):
            def front(i, p):
                dve.wait_ge(s_pick[p], 16 * TPC * TOPK * ((i >> 1) + 1))
                if since(i, 2):
                    dve.wait_ge(s_mp, i - 1)
                gate = lambda r, t: weight[:, r, i * TPC + t:i * TPC + t + 1] if isinstance(i, int) else weight[:, r, bass.ds(i * TPC + t, 1)]
                for t in range(TPC):
                    dve.tensor_scalar(mixed[:, p, t], picked[:, p, 0, t], gate(0, t), None, ALU.mult).then_inc(s_first, 1)
                for t in range(TPC):
                    dve.wait_ge(s_first, i * TPC + (t + 1))
                    dve.scalar_tensor_tensor(mixed[:, p, t], picked[:, p, 1, t], gate(1, t), mixed[:, p, t],
                                             ALU.mult, ALU.add).then_inc(s_mix, 1)

            def back(i, p):
                dve.wait_ge(s_y, i + 1)
                dve.wait_ge(s_xb, i + 1)
                if since(i, 1):
                    dve.wait_ge(norm.s_done, i * TPC)
                dve.tensor_tensor(res[:, :], ps_y[:, :], x1_bias[:, p], ALU.add).then_inc(s_res, 1)
                dve.wait_ge(s_res, i + 1)
                norm.statistics(dve, i, res)
                if since(i, 2):
                    dve.wait_ge(s_out[p], 16 * (i >> 1))
                norm.apply(dve, i, normed[:, p], res)
            staggered(dve, NCH, front, back)


def program(nc, x, Wq, Wk, Wv, Wo, Wqp, Wkp, lambda_raw, W1, b1, W3, b3, W2, b2, Wg, bg, Wf, bf, out):
    scratch = lambda name, shape: nc.dram_tensor(name, shape, F32).ap()
    q_parts = scratch("q_parts", [NCH, 6, D, CH])
    k_parts = scratch("k_parts", [NCH, 6, D, CH])
    v_rows = scratch("v_rows", [T, H * VW])
    attn_rows = scratch("attn_rows", [T, D])
    sorted_rows = scratch("sorted_rows", [SLOTS, D])
    expert_rows = scratch("expert_rows", [SLOTS, D])
    prepare(nc, x, Wq, Wk, Wv, Wqp, Wkp, lambda_raw, q_parts, k_parts, v_rows)
    attend(nc, q_parts, k_parts, v_rows, attn_rows, sorted_rows)
    with ExitStack() as stack:
        n = Names(nc, stack, "keep")
        x1 = n.sb("x1", [P, NT, D])
        places = n.sb("places", [P, TOPK, NT], U32)
        weight = n.sb("weight", [P, TOPK, NT])
        tile_expert = n.sb("tile_expert", [1, SLOT_TILES], I32)
        with ExitStack() as weights:
            m = Names(nc, weights, "keep")
            w1 = m.sb("w1", [P, DK, NE, HID])
            w3 = m.sb("w3", [P, DK, NE, HID])
            w2 = m.sb("w2", [P, HK, NE, D])
            route(nc, x, attn_rows, Wo, Wg, bg, W1, W3, W2, (x1, places, weight, tile_expert, w1, w3, w2), sorted_rows)
            experts(nc, b1, b3, b2, tile_expert, w1, w3, w2, sorted_rows, expert_rows)
        finish(nc, Wf, bf, x1, places, weight, expert_rows, out)


_INS = ['L0_attn_x', 'L0_attn_Wq', 'L0_attn_Wk', 'L0_attn_Wv', 'L0_attn_Wo', 'L0_attn_Wqp', 'L0_attn_Wkp',
        'L0_attn_lambda_raw', 'L0_ffn_W1', 'L0_ffn_b1', 'L0_ffn_W3', 'L0_ffn_b3', 'L0_ffn_W2', 'L0_ffn_b2',
        'L0_ffn_Wg', 'L0_ffn_bg', 'L0_ffn_Wf', 'L0_ffn_bf']


def kernel(**inputs):
    import numpy as _np
    import concourse.bacc as _bacc
    from concourse import mybir as _mybir
    from concourse.bass_utils import run_bass_kernel_spmd as _run

    nc = _bacc.Bacc("TRN2", target_bir_lowering=False, num_devices=1)
    arrays, args = {}, []
    for name in _INS:
        a = _np.ascontiguousarray(inputs[name])
        arrays[f"in_{name}_dram"] = a
        args.append(nc.dram_tensor(f"in_{name}_dram", a.shape, _mybir.dt.from_np(a.dtype), kind="ExternalInput").ap())
    args.append(nc.dram_tensor("out_0_dram", (B, S, D), F32, kind="ExternalOutput").ap())
    program(nc, *args)
    r = _run(nc, [arrays], core_ids=[0])
    return r.results[0]["out_0_dram"]
```

```python
from contextlib import ExitStack
import math

import numpy as np
import concourse.bass as bass
from concourse import mybir

F32 = mybir.dt.float32
F32R = mybir.dt.float32r
BF16 = mybir.dt.bfloat16
I32 = mybir.dt.int32
U32 = mybir.dt.uint32
ACT = mybir.ActivationFunctionType
ALU = mybir.AluOpType
AX = mybir.AxisListType

P = 128
B, S, D, H = 2, 2048, 256, 16
HD = D // H
T = B * S
DK = D // P
FEAT = 3 * HD
SPLIT = 2 * FEAT
CH = 512
NCH = T // CH
TPC = CH // P
QUAD = 4
NQ = H // QUAD
NQ_BITS = NQ.bit_length() - 1
QC = S // CH
VW = 32
NE, HID, TOPK = 8, 512, 2
NT = T // P
HK = HID // P
SLOT_TILES = T * TOPK // P + NE
ROW, TOKEN, FIRST_EXPERT = D + 2, D, D + 1
NO_TOKEN = 1e6
REGION_TILES = NT + 1
AMP_EPS = 1e-6
LN_EPS = 1e-5
LAMBDA_MAX = 0.5
SCALE = 1.0 / math.sqrt(HD)
PI_BELOW = 3.1415925
MASKED = -1e30
NO_LIMIT = 3e38


class Names:

    def __init__(self, nc, stack, stage):
        self.nc, self.stack, self.stage = nc, stack, stage

    def sem(self, name):
        return self.stack.enter_context(self.nc.semaphore(f"{self.stage}_{name}"))

    def sb(self, name, shape, dt=F32):
        return self.stack.enter_context(self.nc.sbuf_tensor(f"{self.stage}_{name}", shape, dt))

    def ps(self, name, shape, dt=F32):
        return self.stack.enter_context(self.nc.psum_tensor(f"{self.stage}_{name}", shape, dt))


def pipelined(eng, count, stages, body=2):
    deepest = max(lag for _, lag in stages)
    lead = (deepest + 2 * body - 1) // body * body
    loops = (count - lead) // body
    if loops < 2:
        loops, lead = 0, count

    def iteration(i, u):
        for f, lag in stages:
            if not isinstance(i, int) or 0 <= i - lag < count:
                f(i - lag, (u - lag) % body)

    for i in range(lead):
        iteration(i, i)
    if loops:
        with eng.Fori(lead // body, lead // body + loops) as j:
            for u in range(body):
                iteration(body * j + u, u)
    for i in range(lead + body * loops, count + deepest):
        iteration(i, i)


def since(i, first):
    return not isinstance(i, int) or i >= first


def at(view, i):
    if isinstance(i, int):
        return view[i]
    rest = " ".join("bcdef"[:len(view.shape) - 2])
    return view[bass.ds(i, 1)].rearrange(f"o a {rest} -> (o a) {rest}")




def identity(pool, tile, begun, ready):
    pool.memset(tile, 0.0).then_inc(begun, 1)
    pool.wait_ge(begun, 1)
    pool.affine_select(out=tile, in_=tile, compare_op=ALU.not_equal, fill=1.0, base=0,
                       pattern=[[-1, P]], channel_multiplier=1).then_inc(ready, 1)


def absolute(dve, out, in_):
    return dve.tensor_scalar(out.bitcast(U32), in_.bitcast(U32), 0x7FFFFFFF, None, ALU.bitwise_and)


def prepare(nc, x, Wq, Wk, Wv, Wqp, Wkp, lambda_raw, q_parts, k_parts, v_rows):
    with ExitStack() as stack:
        n = Names(nc, stack, "pre")
        ident = n.sb("ident", [P, P])
        heads_mean = n.sb("heads_mean", [P, P])
        same_head = n.sb("same_head", [P, P // HD])
        raw_weights = n.sb("raw_weights", [P, 4, DK, D])
        weights = n.sb("weights", [P, 4, DK, D])
        weight_v = n.sb("weight_v", [P, DK, D])
        lam = n.sb("lam", [P, 2])
        lam_tanh = n.sb("lam_tanh", [P, 2])
        lam_scale = n.sb("lam_scale", [P, 2])
        consts = n.sb("consts", [P, 3])
        half_pi, amp_eps, one = consts[:, 0:1], consts[:, 1:2], consts[:, 2:3]
        x_rows = n.sb("x_rows", [P, 2, TPC, D])
        x_t = n.sb("x_t", [P, 2, DK, CH])
        qk = n.sb("qk", [P, 2, 4, CH])
        soft = n.sb("soft", [P, 4, CH])
        amp = n.sb("amp", [P, 2, 4, CH])
        amp_sq = n.sb("amp_sq", [P, 4, CH])
        rnorm = n.sb("rnorm", [P, 4, CH])
        normed = n.sb("normed", [P, 4, CH])
        phase = n.sb("phase", [P, 2, 4, CH])
        waves = n.sb("waves", [P, 2, 2, 4, CH])
        high = n.sb("high", [P, 3, 4, CH], F32R)
        low = n.sb("low", [P, 3, 4, CH], F32R)
        v_sb = n.sb("v_sb", [P, TPC, H, VW])
        ps_a = [n.ps(f"ps_a{k}", [P, CH]) for k in range(2)]
        ps_h = n.ps("ps_h", [P, 2, CH])
        ps_q = n.ps("ps_q", [P, 2, CH])
        ps_n = n.ps("ps_n", [P, 2, CH])

        s_w = n.sem("weights_loaded")
        s_const = n.sem("constants")
        s_const_made = n.sem("constants_begun")
        s_lam = n.sem("lambda_ready")
        s_ordered = n.sem("weights_ordered")
        s_heads = n.sem("heads_matched")
        s_ones = n.sem("value_ones")
        s_x = [n.sem(f"x_loaded{i}") for i in range(2)]
        s_xp = n.sem("x_transposed")
        s_xt = n.sem("x_t_ready")
        s_pp = n.sem("phase_projected")
        s_tanh = n.sem("phase_ready")
        s_qkp = n.sem("qk_projected")
        s_qk = n.sem("qk_ready")
        s_abs = n.sem("abs_ready")
        s_exp = n.sem("exp_ready")
        s_log = n.sem("log_ready")
        s_amp = n.sem("amp_ready")
        s_scaled = n.sem("q_scaled")
        s_sq = n.sem("amp_squared")
        s_norm = n.sem("norm_summed")
        s_ln = n.sem("norm_log")
        s_rn = n.sem("rnorm_ready")
        s_absp = n.sem("abs_phase")
        s_wave = [n.sem("cosine_ready"), n.sem("sine_ready")]
        s_an = n.sem("amp_normed")
        s_feat = n.sem("features_ready")
        s_high = [n.sem(f"high_ready{kind}") for kind in range(3)]
        s_low = [n.sem(f"low_ready{kind}") for kind in range(3)]
        s_vp = n.sem("v_projected")
        s_v = n.sem("v_ready")
        s_high_out = [n.sem(f"high_stored{kind}") for kind in range(3)]
        s_low_out = [n.sem(f"low_stored{kind}") for kind in range(3)]
        s_vout = n.sem("v_stored")
        block = stack.enter_context(nc.Block())

        CONSTS = 4
        WEIGHT_LOADS = 16 * (5 + NQ)
        Q, K = 0, 1
        STORED = 32
        QUADS = P // (QUAD * HD)
        rows_in = x.rearrange("b (c t p) d -> (b c) p t d", p=P, t=TPC)
        rows_v = v_rows.rearrange("(c t p) w -> c p t w", p=P, t=TPC)

        @block.sync
        def _(sp):
            sp.dma_start(x_rows[:, 0], rows_in[0]).then_inc(s_x[0], 16)
            for w, src in enumerate((Wq, Wk, Wqp, Wkp)):
                sp.dma_start(raw_weights[:, w], src.rearrange("(k p) n -> p k n", p=P)).then_inc(s_w, 16)
            sp.dma_start(weight_v[:, :], Wv.rearrange("(k p) n -> p k n", p=P)).then_inc(s_w, 16)
            for quad in range(NQ):
                rows = slice(quad % QUADS * QUAD * HD, (quad % QUADS + 1) * QUAD * HD)
                sp.dma_start(lam[rows, quad // QUADS:quad // QUADS + 1],
                             lambda_raw[quad * QUAD:(quad + 1) * QUAD].rearrange("(o h) -> o h", o=1).to_broadcast([HD, QUAD])).then_inc(s_w, 16)

            def load(i, p):
                if since(i, 2):
                    sp.wait_ge(s_xp, 2 * (i - 1))
                if since(i, 1):
                    sp.dma_start(x_rows[:, p], at(rows_in, i)).then_inc(s_x[p], 16)

            def store_v(i, p):
                sp.wait_ge(s_v, 2 * i + 2)
                sp.dma_start(at(rows_v, i), v_sb[:, :].rearrange("p t h w -> p t (h w)")).then_inc(s_vout, 16)

            def store(i, kind, part):
                tile, ready, stored = ((high, s_high, s_high_out), (low, s_low, s_low_out))[part]
                sp.wait_ge(ready[kind], i + 1)
                for side, parts in enumerate((q_parts, k_parts)):
                    to = parts[:, 3 * part + kind].rearrange("n (c q) d h t -> n (q d h) c t", q=QUADS)
                    sp.dma_start(at(to, i), tile[:, kind, 2 * side:2 * side + 2].bitcast(F32)).then_inc(stored[kind], 16)

            pipelined(sp, NCH, [
                (load, 0),
                (lambda i, p: store(i, 0, 0), 2),
                (lambda i, p: store(i, 0, 1), 2),
                (lambda i, p: store(i, 1, 0), 3),
                (store_v, 1),
                (lambda i, p: store(i, 1, 1), 3),
                (lambda i, p: store(i, 2, 0), 3),
                (lambda i, p: store(i, 2, 1), 3)])
            sp.wait_ge(s_vout, 16 * NCH)
            for kind in range(3):
                sp.wait_ge(s_high_out[kind], STORED * NCH)
                sp.wait_ge(s_low_out[kind], STORED * NCH)

        @block.tensor
        def _(pe):
            pe.wait_ge(s_const, CONSTS)
            pe.wait_ge(s_w, WEIGHT_LOADS)

            def turn(i, p):
                pe.wait_ge(s_x[p], 16 * ((i >> 1) + 1))
                for k in range(DK):
                    if since(i, 1):
                        pe.wait_ge(s_v, 2 * i + (k - 1))
                    for t in range(TPC):
                        mm = pe.transpose(ps_a[k][:, t * P:(t + 1) * P], x_rows[:, p, t, k * P:(k + 1) * P], ident[:, :])
                    mm.then_inc(s_xp, 1)

            def project(weight, out, p):
                for c in range(2):
                    for k in range(DK):
                        mm = pe.matmul(out[:, c], weights[:, weight, k, c * P:(c + 1) * P], x_t[:, p, k],
                                       start=(k == 0), stop=(k == DK - 1))
                return mm

            def project_qk(i, p, side):
                if side == Q:
                    pe.wait_ge(s_xt, 2 * i + 2)
                    if isinstance(i, int) and i == 0:
                        pe.wait_ge(s_ordered, 1)
                if side == K or since(i, 1):
                    pe.wait_ge(s_qk, 2 * i + side)
                project(side, ps_q, p).then_inc(s_qkp, 1)

            def project_phase(i, p, side):
                if side == Q and since(i, 2):
                    pe.wait_ge(s_ln, 2 * (i - 1))
                if side == K or since(i, 1):
                    pe.wait_ge(s_tanh, 2 * i + side)
                project(2 + side, ps_h, p).then_inc(s_pp, 1)

            def project_v(i, p):
                for half in range(2):
                    for t in range(2):
                        tokens = slice((2 * half + t) * P, (2 * half + t + 1) * P)
                        for k in range(DK):
                            mm = pe.matmul(ps_a[half][:, t * D:(t + 1) * D], x_t[:, p, k, tokens], weight_v[:, k],
                                           start=(k == 0), stop=(k == DK - 1))
                    mm.then_inc(s_vp, 1)

            def sum_norm(i, p, side):
                if side == Q:
                    pe.wait_ge(s_sq, i + 1)
                    if isinstance(i, int) and i == 0:
                        pe.wait_ge(s_heads, 2)
                    if since(i, 1):
                        pe.wait_ge(s_ln, 2 * i - 1)
                else:
                    pe.wait_ge(s_tanh, min(2 * i + 4, 2 * NCH) if isinstance(i, int) else 2 * i + 4)
                    if isinstance(i, int) and i == NCH - 1:
                        pe.wait_ge(s_ln, 2 * i)
                for c in range(2):
                    mm = pe.matmul((ps_n, ps_h)[side][:, c], heads_mean[:, :], amp_sq[:, 2 * side + c], start=True, stop=True)
                mm.then_inc(s_norm, 1)

            pipelined(pe, NCH, [
                (lambda i, p: project_qk(i, p, Q), 1),
                (lambda i, p: project_phase(i, p, Q), 1),
                (lambda i, p: project_qk(i, p, K), 1),
                (lambda i, p: project_phase(i, p, K), 1),
                (lambda i, p: sum_norm(i, p, Q), 2),
                (project_v, 1),
                (lambda i, p: sum_norm(i, p, K), 2),
                (turn, 0)])

        @block.scalar
        def _(act):
            act.wait_ge(s_w, WEIGHT_LOADS)
            act.activation(lam_tanh[:, :], lam[:, :], ACT.Tanh).then_inc(s_lam, 1)
            act.wait_ge(s_const, CONSTS)

            def phases(i, p, side):
                act.wait_ge(s_pp, 2 * i + side + 1)
                if since(i, 2):
                    act.wait_ge(s_wave[1], i - 1)
                    act.wait_ge(s_absp, i - 1)
                act.activation(phase[:, p, 2 * side:2 * side + 2], ps_h[:, :], ACT.Tanh).then_inc(s_tanh, 1)

            def soft_exp(i, p):
                act.wait_ge(s_abs, 2 * i + 2)
                act.activation(soft[:, :], soft[:, :], ACT.Exp, scale=-1.0).then_inc(s_exp, 1)

            def soft_log(i, p):
                act.wait_ge(s_exp, i + 1)
                act.activation(soft[:, :], soft[:, :], ACT.Ln, bias=one).then_inc(s_log, 1)

            def norm_log(i, p, side):
                act.wait_ge(s_norm, 2 * i + side + 1)
                if since(i, 1):
                    act.wait_ge(s_an, i)
                act.activation(rnorm[:, 2 * side:2 * side + 2], (ps_n, ps_h)[side][:, :], ACT.Ln, bias=amp_eps).then_inc(s_ln, 1)

            def norm_exp(i, p):
                act.wait_ge(s_ln, 2 * i + 2)
                act.activation(rnorm[:, :], rnorm[:, :], ACT.Exp, scale=-0.5).then_inc(s_rn, 1)

            def make_waves(i, p):
                act.wait_ge(s_absp, i + 1)
                act.activation(waves[:, p, 0], waves[:, p, 0], ACT.Sin, bias=half_pi, scale=-PI_BELOW).then_inc(s_wave[0], 1)
                act.wait_ge(s_tanh, 2 * i + 2)
                if since(i, 2):
                    act.wait_ge(s_low[2], i - 1)
                act.activation(waves[:, p, 1], phase[:, p], ACT.Sin, scale=PI_BELOW).then_inc(s_wave[1], 1)

            pipelined(act, NCH, [
                (lambda i, p: phases(i, p, Q), 1),
                (lambda i, p: norm_exp(i, p) if i < NCH - 1 else None, 3),
                (soft_exp, 1),
                (lambda i, p: phases(i, p, K), 1),
                (soft_log, 1),
                (lambda i, p: norm_log(i, p, Q), 2),
                (lambda i, p: norm_log(i, p, K), 2),
                (lambda i, p: norm_exp(i, p) if i == NCH - 1 else None, 2),
                (make_waves, 2)])

        @block.vector
        def _(dve):
            dve.wait_ge(s_w, WEIGHT_LOADS)
            dve.tensor_copy(weights[:, :].rearrange("p w k (c d h) -> p (w k c) d h", d=HD, h=QUAD),
                            raw_weights[:, :].rearrange("p w k (c h d) -> p (w k c) d h", d=HD, h=QUAD)).then_inc(s_ordered, 1)
            dve.wait_ge(s_const, CONSTS)
            dve.tensor_reduce(same_head[:, :].rearrange("p (q h) -> p q h", h=QUAD),
                              ident[:, :].rearrange("p (q d h) -> p q h d", d=HD, h=QUAD), AX.X, ALU.add).then_inc(s_heads, 1)
            dve.wait_ge(s_heads, 1)
            dve.tensor_scalar(heads_mean[:, :].rearrange("p (q d h) -> p q d h", d=HD, h=QUAD),
                              same_head[:, :].rearrange("p (q o h) -> p q o h", o=1, h=QUAD).to_broadcast([P, QUADS, HD, QUAD]),
                              1.0 / HD, None, ALU.mult).then_inc(s_heads, 1)
            dve.memset(v_sb[:, :, :, :], 0.0).then_inc(s_ones, 1)
            dve.wait_ge(s_ones, 1)
            dve.memset(v_sb[:, :, :, HD:HD + 1], 1.0).then_inc(s_ones, 1)
            dve.wait_ge(s_ones, 2)
            dve.wait_ge(s_lam, 1)
            dve.tensor_scalar(lam_scale[:, :], lam_tanh[:, :], LAMBDA_MAX * SCALE, None, ALU.mult).then_inc(s_lam, 1)
            dve.wait_ge(s_lam, 2)

            def keep_x(i, p):
                for k in range(DK):
                    dve.wait_ge(s_xp, 2 * i + k + 1)
                    if since(i, 2):
                        dve.wait_ge(s_vp, 2 * (i - 1))
                        dve.wait_ge(s_pp, 2 * (i - 1))
                    dve.tensor_copy(x_t[:, p, k], ps_a[k][:, :]).then_inc(s_xt, 1)

            def keep_v(i, p):
                for half in range(2):
                    dve.wait_ge(s_vp, 2 * i + half + 1)
                    if since(i, 1):
                        dve.wait_ge(s_vout, 16 * i)
                    dve.tensor_copy(v_sb[:, 2 * half:2 * half + 2, :, 0:HD].rearrange("p t h d -> p (t h) d"),
                                    ps_a[half][:, :].rearrange("p (t d) -> p t d", d=HD)).then_inc(s_v, 1)

            def keep_qk(i, p, side):
                dve.wait_ge(s_qkp, 2 * i + side + 1)
                if since(i, 2):
                    dve.wait_ge(s_low[0], i - 1)
                mine = slice(2 * side, 2 * side + 2)
                dve.tensor_copy(qk[:, p, mine], ps_q[:, :]).then_inc(s_qk, 1)
                dve.wait_ge(s_qk, 2 * i + side + 1)
                if since(i, 1):
                    dve.wait_ge(s_amp, i)
                absolute(dve, soft[:, mine], qk[:, p, mine]).then_inc(s_abs, 1)

            def amplitudes(i, p):
                dve.wait_ge(s_log, i + 1)
                if since(i, 2):
                    dve.wait_ge(s_an, i - 1)
                    dve.wait_ge(s_sq, i - 1)
                flat = "p c t -> p (c t)"
                dve.scalar_tensor_tensor(amp[:, p].rearrange(flat), qk[:, p].rearrange(flat), 0.0,
                                         soft[:, :].rearrange(flat), ALU.max, ALU.add).then_inc(s_amp, 1)

            def abs_phase(i, p):
                dve.wait_ge(s_tanh, 2 * i + 2)
                if since(i, 2):
                    dve.wait_ge(s_low[1], i - 1)
                absolute(dve, waves[:, p, 0], phase[:, p]).then_inc(s_absp, 1)

            def norm_amplitudes(i, p):
                dve.wait_ge(s_rn, i + 1)
                if since(i, 1):
                    dve.wait_ge(s_feat, 6 * i)
                dve.tensor_tensor(normed[:, :], amp[:, p], rnorm[:, :], ALU.mult).then_inc(s_an, 1)

            def take_high(i, kind, whole):
                if since(i, 1):
                    dve.wait_ge(s_low[kind], i)
                    dve.wait_ge(s_high_out[kind], STORED * i)
                dve.tensor_copy(high[:, kind], whole).then_inc(s_high[kind], 1)

            def scale_q(i, p):
                dve.wait_ge(s_amp, i + 1)
                dve.tensor_scalar(qk[:, p, 0:2], qk[:, p, 0:2], SCALE, None, ALU.mult).then_inc(s_scaled, 1)
                dve.wait_ge(s_scaled, i + 1)
                take_high(i, 0, qk[:, p])

            def features(i, p, f):
                dve.wait_ge(s_an, i + 1)
                dve.wait_ge(s_wave[f], i + 1)
                for c in range(2):
                    dve.scalar_tensor_tensor(waves[:, p, f, c], normed[:, c], lam_scale[:, c:c + 1], waves[:, p, f, c],
                                             ALU.mult, ALU.mult).then_inc(s_feat, 1)
                dve.tensor_tensor(waves[:, p, f, 2:4], normed[:, 2:4], waves[:, p, f, 2:4], ALU.mult).then_inc(s_feat, 1)
                dve.wait_ge(s_feat, 6 * i + 3 * (f + 1))
                take_high(i, 1 + f, waves[:, p, f])

            pipelined(dve, NCH, [
                (lambda i, p: keep_qk(i, p, Q), 1),
                (abs_phase, 2),
                (norm_amplitudes, 3),
                (lambda i, p: keep_qk(i, p, K), 1),
                (lambda i, p: features(i, p, 0), 3),
                (keep_v, 1),
                (amplitudes, 1),
                (keep_x, 0),
                (lambda i, p: features(i, p, 1), 3),
                (scale_q, 1)])
            dve.wait_ge(s_low_out[2], STORED * (NCH - 1))
            dve.wait_ge(s_high[2], NCH)
            dve.tensor_tensor(low[:, 2], waves[:, (NCH - 1) % 2, 1], high[:, 2].bitcast(F32), ALU.subtract).then_inc(s_low[2], 1)

        @block.gpsimd
        def _(pool):
            pool.memset(consts[:, 0:1], math.pi / 2).then_inc(s_const, 1)
            pool.memset(consts[:, 1:2], AMP_EPS).then_inc(s_const, 1)
            pool.memset(consts[:, 2:3], 1.0).then_inc(s_const, 1)
            identity(pool, ident[:, :], s_const_made, s_const)

            def split(i, kind, whole):
                pool.wait_ge(s_high[kind], i + 1)
                if since(i, 1):
                    pool.wait_ge(s_low_out[kind], STORED * i)
                pool.tensor_tensor(low[:, kind], whole, high[:, kind].bitcast(F32), ALU.subtract).then_inc(s_low[kind], 1)

            def square(i, p):
                pool.wait_ge(s_amp, i + 1)
                if since(i, 1):
                    pool.wait_ge(s_norm, 2 * i)
                pool.tensor_tensor(amp_sq[:, :], amp[:, p], amp[:, p], ALU.mult).then_inc(s_sq, 1)

            pipelined(pool, NCH, [
                (lambda i, p: split(i, 0, qk[:, p]), 2),
                (lambda i, p: split(i, 1, waves[:, p, 0]), 3),
                (square, 1),
                (lambda i, p: split(i, 2, waves[:, p, 1]) if i < NCH - 1 else None, 3)])


BLOCKS = [4 * (c + 1) for c in range(QC)]
FIRST = [sum(BLOCKS[:c]) for c in range(QC)]
STEPS = sum(BLOCKS)
LATER = 1
AHEAD = 3
MAXIMA = [QUAD * TPC * (c + 1) for c in range(QC)]
LEFT = 14
EARLY = sum(MAXIMA[:AHEAD])
PER_QUAD = sum(MAXIMA)


def max_tiles(chunks):
    return [(nxt, c, h, q, k) for nxt, c in chunks for h in range(QUAD) for q in range(TPC) for k in range(c + 1)]


def ahead(g):
    return 1 if isinstance(g, int) and g == 0 else AHEAD - 1


def attend_plan(g, last):
    first = isinstance(g, int) and g == 0
    tiles = max_tiles([(False, c) for c in range(ahead(g), QC)])[0 if first else MAXIMA[AHEAD - 1] - LEFT:]
    if not last:
        tiles += max_tiles([(True, c) for c in range(AHEAD)])[:-LEFT]
    columns = [CH - P * max(0, s - FIRST[c] - TPC * c) for c in range(QC) for s in range(FIRST[c], FIRST[c] + BLOCKS[c])]
    if first:
        stops = [0] + [sum(columns[:FIRST[c] - 2]) for c in range(1, QC)] + [sum(columns)]
        due = [0] + [sum(MAXIMA[1:c + 1]) for c in range(1, QC)] + [len(tiles)]
    else:
        stops, due = [0, sum(columns[:BLOCKS[0]]), sum(columns)], [0, LEFT, PER_QUAD]
    passed, at_ = 0, 0
    plan, turns = [], []

    def fill(cols):
        nonlocal passed, at_
        passed += cols / 5
        while at_ < min(len(tiles), math.ceil(np.interp(passed, stops, due))):
            plan.append(("max",) + tiles[at_])
            nxt, c, h, q, k = tiles[at_]
            if (h, q, k) == (QUAD - 1, TPC - 1, c):
                turns.append(("turn_max", nxt, c))
            at_ += 1

    for s in range(STEPS):
        for pair in range(2):
            plan.append(("scores", s, pair))
            if pair == 0:
                plan += turns
                turns.clear()
            fill(2 * columns[s])
        if s >= LATER:
            plan.append(("values", s - LATER))
            fill(columns[s])
            if s - LATER + 1 in FIRST:
                turns.append(("turn_out", FIRST.index(s - LATER + 1) - 1))
    plan += [("values", s) for s in range(STEPS - LATER, STEPS)]
    fill(sum(columns))
    plan += turns
    plan.append(("turn_out", QC - 1))
    return plan


def tiles_before(g):
    return MAXIMA[0] if isinstance(g, int) and g == 0 else g * PER_QUAD + (EARLY - LEFT)


SLOTS_PS = 3


def turned_slots(g, last):
    in_slots = lambda g, last: [event[0] for event in attend_plan(g, last) if event[0] in ("max", "turn_max", "turn_out")]
    kinds = in_slots(g, last)
    counts = {"max": tiles_before(g), "turn_max": g * QC + ahead(g), "turn_out": g * QC}
    opening = ["max"] * MAXIMA[0] + ["turn_max"]
    if isinstance(g, int) and g == 0:
        before = opening
        buffer = len(before) % SLOTS_PS
    else:
        before = in_slots(1, False)
        assert before[-SLOTS_PS:] == in_slots(0, False)[-SLOTS_PS:]
        assert len(before) % SLOTS_PS == 0 and len(opening + in_slots(0, False)) % SLOTS_PS == 0
        buffer = 0
    freed = []
    for i in range(SLOTS_PS):
        kind = before[-SLOTS_PS + i]
        freed.append((kind, counts[kind] - before[len(before) - SLOTS_PS + i + 1:].count(kind)))
    slots = []
    for kind in kinds:
        slots.append((buffer, *freed.pop(0)))
        counts[kind] = counts[kind] + 1
        freed.append((kind, counts[kind]))
        buffer = (buffer + 1) % SLOTS_PS
    return slots


def wait_positive(eng, sem, value):
    if not isinstance(value, int) or value > 0:
        eng.wait_ge(sem, value)


def quads(eng, quad):
    quad(0, False)
    with eng.Fori(1, B * NQ - 1) as g:
        quad(g, False)
    quad(B * NQ - 1, True)


def attend(nc, q_parts, k_parts, v_rows, attn_rows):
    with ExitStack() as stack:
        n = Names(nc, stack, "att")
        ident = n.sb("ident", [P, P])
        ident_b = n.sb("ident_b", [P, P], BF16)
        future = n.sb("future", [P, P], BF16)
        limit = n.sb("limit", [P, P])
        q_same = n.sb("q_same", [SPLIT + 1, QC, QUAD, CH], F32R)
        q_swap = n.sb("q_swap", [SPLIT, QC, QUAD, CH], F32R)
        keys = n.sb("keys", [SPLIT + 1, QC, QUAD, CH], F32R)
        keys_next = n.sb("keys_next", [SPLIT, AHEAD, QUAD, CH], F32R)
        values = n.sb("values", [P, S // P, QUAD * VW])
        probs = n.sb("probs", [P, 4, QUAD, CH])
        maxima = n.sb("maxima", [P, 2, QUAD * TPC, QC])
        neg_max = n.sb("neg_max", [P, 2, QUAD * TPC])
        max_row = n.sb("max_row", [QUAD * TPC, 2, P], F32R)
        out_t = n.sb("out_t", [P, CH])
        inv_sum = n.sb("inv_sum", [P, TPC * QUAD])
        out_rows = n.sb("out_rows", [P, 2, TPC, QUAD * HD])
        ps_s = [n.ps(f"ps_s{i}", [P, 2, CH]) for i in range(2)]
        ps_m = [n.ps(f"ps_m{i}", [P, CH]) for i in range(SLOTS_PS)]
        ps_o = n.ps("ps_o", [P, CH])

        s_made = n.sem("constants_begun")
        s_const = n.sem("constants")
        s_one = n.sem("ones_under_keys")
        s_q = [n.sem(f"q_loaded{c}") for c in range(QC)]
        s_swap = [n.sem(f"swapped_q_loaded{c}") for c in range(QC)]
        s_k = [n.sem(f"k_loaded{c}") for c in range(QC)]
        s_kn = [n.sem(f"next_k_loaded{c}") for c in range(AHEAD)]
        s_v = [n.sem(f"v_loaded{c}") for c in range(QC)]
        s_scores = n.sem("scores_ready")
        s_exp = n.sem("probs_ready")
        s_masked = n.sem("scores_masked")
        s_pv = n.sem("values_summed")
        s_mt = n.sem("max_tile_ready")
        s_mr = n.sem("max_tile_read")
        s_neg = n.sem("neg_max_ready")
        s_turn = n.sem("max_turned")
        read = {"max": s_mr}
        s_row = n.sem("max_row_ready")
        s_m = [n.sem(f"max_row_placed{c}") for c in range(QC)]
        s_oc = n.sem("out_copied")
        s_ot = n.sem("out_turned")
        s_inv = n.sem("inverse_ready")
        s_or = n.sem("out_rows_ready")
        read.update(turn_max=s_row, turn_out=s_or)
        s_store = [n.sem(f"out_stored{i}") for i in range(2)]
        block = stack.enter_context(nc.Block())

        CONSTS = 4
        quads_q = q_parts.rearrange("n g u d h t -> n u g d (h t)")
        quads_k = k_parts.rearrange("n g u d h t -> n u g d (h t)")
        rows_v = v_rows.rearrange("(n k p) w -> n p k w", k=TPC, p=P)
        rows_o = attn_rows.rearrange("(n k p) w -> n p k w", k=TPC, p=P)

        def place(eng, g):
            chunk, mine = (g >> NQ_BITS & (B - 1)) * QC, g & (NQ - 1)
            return (chunk, mine) if isinstance(g, int) else (eng.snap(chunk), eng.snap(mine))

        def of_quad(view, where, c, lo, hi):
            n_, u_ = where[0] + c, where[1]
            if isinstance(n_, int):
                return view[n_, u_, lo:hi]
            return view[bass.ds(n_, 1), bass.ds(u_, 1), lo:hi].rearrange("n u g d t -> (n u g) d t")

        def in_rows(view, where, c, width):
            n_, w_ = where[0] + c, where[1] * (QUAD * width)
            if isinstance(n_, int):
                return view[n_, :, :, w_:w_ + QUAD * width]
            return view[bass.ds(n_, 1), :, :, bass.ds(w_, QUAD * width)].rearrange("n p k w -> (n p) k w")

        @block.sync
        def _(sp):
            KINDS = FEAT // HD

            def load_q(where, c):
                rows = "r h t -> r (h t)"
                sp.dma_start(q_same[0:SPLIT, c].rearrange(rows).bitcast(F32), of_quad(quads_q, where, c, 0, 2 * KINDS)).then_inc(s_q[c], 16)

            def load_swap(where, c):
                rows = "r h t -> r (h t)"
                sp.dma_start(q_swap[0:FEAT, c].rearrange(rows).bitcast(F32), of_quad(quads_q, where, c, KINDS, 2 * KINDS)).then_inc(s_swap[c], 16)
                sp.dma_start(q_swap[FEAT:SPLIT, c].rearrange(rows).bitcast(F32), of_quad(quads_q, where, c, 0, KINDS)).then_inc(s_swap[c], 16)

            def load_k(where, c):
                sp.dma_start(keys[0:SPLIT, c].rearrange("r h t -> r (h t)").bitcast(F32), of_quad(quads_k, where, c, 0, 2 * KINDS)).then_inc(s_k[c], 16)

            def load_kn(where, c):
                sp.dma_start(keys_next[:, c].rearrange("r h t -> r (h t)").bitcast(F32), of_quad(quads_k, where, c, 0, 2 * KINDS)).then_inc(s_kn[c], 16)

            def load_v(where, c):
                sp.dma_start(values[:, TPC * c:TPC * c + TPC], in_rows(rows_v, where, c, VW)).then_inc(s_v[c], 16)

            def place_max(g, c, turned):
                sp.wait_ge(s_row, turned)
                sp.dma_start(q_same[SPLIT:SPLIT + 1, c].bitcast(F32), max_row[:, c % 2].bitcast(F32)).then_inc(s_m[c], 16)

            def scored(g, step):
                sp.wait_ge(s_scores, g * (2 * STEPS) + 2 * step)

            for c in range(2):
                load_kn((0, 0), c)
                load_q((0, 0), c)
            load_k((0, 0), 0)
            load_swap((0, 0), 0)
            load_v((0, 0), 0)
            place_max(0, 0, 1)
            load_kn((0, 0), 2)
            load_q((0, 0), 2)
            load_k((0, 0), 1)
            load_swap((0, 0), 1)
            load_v((0, 0), 1)
            place_max(0, 1, 2)
            load_q((0, 0), 3)
            for c in range(2, QC):
                load_k((0, 0), c)
                load_swap((0, 0), c)
                load_v((0, 0), c)

            def quad(g, last):
                after = None if last else place(sp, g + 1)
                place_max(g, 2, g * QC + 3)
                if not last:
                    sp.wait_ge(s_mt, g * PER_QUAD + EARLY)
                    for c in range(AHEAD):
                        load_kn(after, c)
                if not last:
                    scored(g, FIRST[1])
                    load_q(after, 0)
                    load_swap(after, 0)
                place_max(g, 3, g * QC + 4)
                if not last:
                    scored(g, FIRST[2])
                    load_q(after, 1)
                    load_swap(after, 1)
                    place_max(g + 1, 0, g * QC + 5)
                    scored(g, FIRST[3])
                    load_q(after, 2)
                    load_swap(after, 2)
                    place_max(g + 1, 1, g * QC + 6)
                    for c in range(QC):
                        scored(g, FIRST[3] + TPC * (c + 1))
                        load_k(after, c)
                        sp.wait_ge(s_pv, g * STEPS + (FIRST[3] + TPC * (c + 1)))
                        load_v(after, c)
                    load_q(after, 3)
                    load_swap(after, 3)
            quads(sp, quad)

        @block.tensor
        def _(pe):
            pe.wait_ge(s_const, CONSTS)

            def take(slot):
                buffer, kind, count = slot
                if kind is not None:
                    pe.wait_ge(read[kind], count)
                return ps_m[buffer]

            def max_tile(g, nxt, c, h, q, k, slot):
                if (h, q) == (0, 0):
                    gg = g + 1 if nxt else g
                    if k == 0:
                        pe.wait_ge(s_q[c], 16 * (gg + 1))
                    if c < AHEAD:
                        pe.wait_ge(s_kn[k], 16 * (gg + 1))
                    else:
                        pe.wait_ge(s_k[k], 16 * (gg + 1))
                buf = take(slot)
                width = CH if k < c else P * (q + 1)
                key = keys_next[:, k, h, 0:width] if c < AHEAD else keys[0:SPLIT, k, h, 0:width]
                mm = pe.matmul(buf[:, 0:width], q_same[0:SPLIT, c, h, P * q:P * q + P], key, start=True, stop=(k < c))
                if k == c:
                    mm = pe.matmul(buf[:, P * q:P * q + P], ident_b[:, :], future[:, :], start=False, stop=True)
                mm.then_inc(s_mt, 1)

            def turn_max(c, maxes, slot):
                pe.wait_ge(s_neg, maxes + 1)
                pe.transpose(take(slot)[0:QUAD * TPC, 0:P], neg_max[:, c % 2], ident[:, :]).then_inc(s_turn, 1)

            def scores(g, s, pair):
                c = max(c for c in range(QC) if FIRST[c] <= s)
                k = s - FIRST[c]
                skip = P * max(0, k - TPC * c)
                if isinstance(g, int) and (g, s, pair) == (0, 0, 0):
                    pe.wait_ge(s_one, 1)
                if k == 0 and pair == 0:
                    pe.wait_ge(s_m[c], 16 * (g + 1))
                    pe.wait_ge(s_q[c], 16 * (g + 1))
                    pe.wait_ge(s_swap[c], 32 * (g + 1))
                if k % TPC == 0 and pair == 0:
                    pe.wait_ge(s_k[k // TPC], 16 * (g + 1))
                wait_positive(pe, s_exp, g * (2 * STEPS) + (2 * s + pair - 1))
                for e in range(2):
                    h = 2 * pair + e
                    out = ps_s[pair][:, e, skip:CH]
                    kk = slice(P * (k % TPC), P * (k % TPC) + P)
                    pe.matmul(out, keys[0:SPLIT + 1, k // TPC, h, kk], q_same[0:SPLIT + 1, c, h, skip:CH],
                              start=True, stop=False)
                    mm = pe.matmul(out, keys[0:SPLIT, k // TPC, h, kk], q_swap[0:SPLIT, c, h, skip:CH],
                                   start=False, stop=True)
                mm.then_inc(s_scores, 1)

            def sum_values(g, s):
                c = max(c for c in range(QC) if FIRST[c] <= s)
                k = s - FIRST[c]
                skip = P * max(0, k - TPC * c)
                pe.wait_ge(s_exp, g * (2 * STEPS) + 2 * (s + 1))
                if k % TPC == 0:
                    pe.wait_ge(s_v[k // TPC], 16 * (g + 1))
                if k == 0:
                    wait_positive(pe, s_oc, g * QC + c)
                for h in range(QUAD):
                    mm = pe.matmul(ps_o[VW * h:VW * h + VW, skip:CH], values[:, k, VW * h:VW * h + VW],
                                   probs[:, s % 4, h, skip:CH], start=(k == 0), stop=(k == BLOCKS[c] - 1))
                mm.then_inc(s_pv, 1)

            def turn_out(g, c, slot):
                pe.wait_ge(s_oc, g * QC + (c + 1))
                out = take(slot)
                for q in range(TPC):
                    mm = pe.transpose(out[:, P * q:P * q + P], out_t[:, P * q:P * q + P], ident[:, :])
                mm.then_inc(s_ot, 1)

            for number, tile in enumerate(max_tiles([(False, 0)])):
                free = number - SLOTS_PS + 1
                max_tile(0, *tile, (number % SLOTS_PS, "max" if free > 0 else None, free))
            turn_max(0, 0, (MAXIMA[0] % SLOTS_PS, "max", MAXIMA[0] - SLOTS_PS + 1))

            def quad(g, last):
                maxes, slots = 0, turned_slots(g, last)
                for event, *what in attend_plan(g, last):
                    if event == "scores":
                        scores(g, *what)
                    elif event == "values":
                        sum_values(g, what[0])
                    elif event == "max":
                        max_tile(g, *what, slots.pop(0))
                    elif event == "turn_max":
                        turn_max(what[1], g * QC + (ahead(g) + maxes), slots.pop(0))
                        maxes += 1
                    elif event == "turn_out":
                        turn_out(g, what[0], slots.pop(0))
            quads(pe, quad)

        @block.scalar
        def _(act):
            def quad(g, last):
                for s in range(STEPS):
                    c = max(c for c in range(QC) if FIRST[c] <= s)
                    skip = P * max(0, s - FIRST[c] - TPC * c)
                    wait_positive(act, s_pv, g * STEPS + (s - 3))
                    own = s - FIRST[c] - TPC * c
                    for pair in range(2):
                        if own >= 0:
                            act.wait_ge(s_masked, g * (2 * QC * TPC) + (2 * (TPC * c + own) + pair + 1))
                        else:
                            act.wait_ge(s_scores, g * (2 * STEPS) + (2 * s + pair + 1))
                        act.activation(probs[:, s % 4, 2 * pair:2 * pair + 2, skip:CH], ps_s[pair][:, :, skip:CH],
                                       ACT.Exp).then_inc(s_exp, 1)
            quads(act, quad)

        @block.vector
        def _(dve):
            dve.wait_ge(s_const, CONSTS)

            def read_max(nxt, c, h, q, k, before, number, buf):
                dve.wait_ge(s_mt, before + (number + 1))
                width = CH if k < c else P * (q + 1)
                dve.tensor_reduce(maxima[:, c % 2, h * TPC + q, k:k + 1], buf[:, 0:width], AX.X,
                                  ALU.max).then_inc(s_mr, 1)

            def negate(c, number):
                dve.wait_ge(s_mr, number + 1)
                dve.tensor_reduce(neg_max[:, c % 2], maxima[:, c % 2, :, 0:c + 1], AX.X, ALU.max,
                                  negate=True).then_inc(s_neg, 1)

            def mask(g, s, pair):
                c = max(c for c in range(QC) if FIRST[c] <= s)
                own = s - FIRST[c] - TPC * c
                if own >= 0:
                    dve.wait_ge(s_scores, g * (2 * STEPS) + (2 * s + pair + 1))
                    block = ps_s[pair][:, :, P * own:P * own + P]
                    dve.tensor_tensor(block, block, limit[:, :].rearrange("p (o q) -> p o q", o=1).to_broadcast([P, 2, P]),
                                      ALU.min).then_inc(s_masked, 1)

            def keep_row(c, turned, placed, buf):
                dve.wait_ge(s_turn, turned)
                wait_positive(dve, s_m[(c + 2) % QC], placed)
                dve.tensor_copy(max_row[:, c % 2], buf[0:QUAD * TPC, 0:P]).then_inc(s_row, 1)

            for number, tile in enumerate(max_tiles([(False, 0)])):
                read_max(*tile, 0, number, ps_m[number % SLOTS_PS])
            negate(0, number)
            keep_row(0, 1, 0, ps_m[MAXIMA[0] % SLOTS_PS])

            def quad(g, last):
                number, maxes, slots = 0, 0, turned_slots(g, last)
                for event, *what in attend_plan(g, last):
                    if event == "max":
                        read_max(*what, tiles_before(g), number, ps_m[slots.pop(0)[0]])
                        nxt, c, h, q, k = what
                        if (h, q, k) == (QUAD - 1, TPC - 1, c):
                            negate(c, tiles_before(g) + number)
                        number += 1
                    elif event == "turn_max":
                        keep_row(what[1], g * QC + (ahead(g) + 1 + maxes), 16 * (g + (1 + (ahead(g) - 2 + maxes) // QC)),
                                 ps_m[slots.pop(0)[0]])
                        maxes += 1
                    elif event == "scores":
                        mask(g, *what)
                    elif event == "values" and what[0] + 1 in FIRST + [STEPS]:
                        c = (FIRST + [STEPS]).index(what[0] + 1) - 1
                        dve.wait_ge(s_pv, g * STEPS + (what[0] + 1))
                        dve.tensor_copy(out_t[:, :], ps_o[:, :]).then_inc(s_oc, 1)
                    elif event == "turn_out":
                        c = what[0]
                        dve.wait_ge(s_ot, g * QC + (c + 1))
                        turned = ps_m[slots.pop(0)[0]][:, :].rearrange("p (j w) -> p j w", w=VW)
                        wait_positive(dve, s_or, g * QC + c)
                        dve.reciprocal(inv_sum[:, :].rearrange("p (j o) -> p j o", o=1), turned[:, :, HD:HD + 1]).then_inc(s_inv, 1)
                        dve.wait_ge(s_inv, g * QC + (c + 1))
                        wait_positive(dve, s_store[c % 2], 16 * (g * 2 + c // 2))
                        dve.tensor_tensor(out_rows[:, c % 2].rearrange("p q (h d) -> p (q h) d", d=HD), turned[:, :, 0:HD],
                                          inv_sum[:, :].rearrange("p (j o) -> p j o", o=1).to_broadcast([P, TPC * QUAD, HD]),
                                          ALU.mult).then_inc(s_or, 1)
            quads(dve, quad)

        @block.gpsimd
        def _(pool):
            identity(pool, ident[:, :], s_made, s_const)
            pool.memset(ident_b[:, :], 0.0).then_inc(s_made, 1)
            pool.memset(future[:, :], 0.0).then_inc(s_made, 1)
            pool.memset(limit[:, :], NO_LIMIT).then_inc(s_made, 1)
            pool.wait_ge(s_made, 4)
            pool.affine_select(out=limit[:, :], in_=limit[:, :], compare_op=ALU.is_ge, fill=MASKED, base=0,
                               pattern=[[1, P]], channel_multiplier=-1).then_inc(s_const, 1)
            pool.affine_select(out=ident_b[:, :], in_=ident_b[:, :], compare_op=ALU.not_equal, fill=1.0, base=0,
                               pattern=[[-1, P]], channel_multiplier=1).then_inc(s_const, 1)
            pool.affine_select(out=future[:, :], in_=future[:, :], compare_op=ALU.is_ge, fill=MASKED, base=0,
                               pattern=[[-1, P]], channel_multiplier=1).then_inc(s_const, 1)


            pool.wait_ge(s_const, CONSTS)
            pool.memset(keys[SPLIT:SPLIT + 1, :, :, :].bitcast(F32), 1.0).then_inc(s_one, 1)

            def store(g, where, c):
                pool.wait_ge(s_or, g * QC + (c + 1))
                pool.dma_start(in_rows(rows_o, where, c, HD), out_rows[:, c % 2]).then_inc(s_store[c % 2], 16)

            with pool.Fori(0, B * NQ) as g:
                where = place(pool, g)
                for c in range(QC):
                    store(g, where, c)
            for i in range(2):
                pool.wait_ge(s_store[i], 16 * B * NQ * QC // 2)
def flat(a):
    return a.rearrange("p t e -> p (t e)")


class Norm:

    def __init__(self, n):
        self.stats = n.sb("stats", [P, TPC, 6])
        self.moments = n.sb("moments", [P, 4, TPC])
        self.mean, self.var, self.m2, self.gap = (self.moments[:, i] for i in range(4))
        self.rstd = n.sb("rstd", [P, TPC])
        self.s_stats = n.sem("stats_ready")
        self.s_step = n.sem("variance_step")
        self.s_var = n.sem("variance_ready")
        self.s_std = n.sem("std_ready")
        self.s_rstd = n.sem("rstd_ready")
        self.s_done = n.sem("rows_normed")

    def statistics(self, dve, i, rows):
        if since(i, 1):
            dve.wait_ge(self.s_done, i * TPC)
        for t in range(TPC):
            dve.bn_stats(self.stats[:, t], rows[:, t]).then_inc(self.s_stats, 1)
        even_mean, even_m2, odd_mean, odd_m2 = (self.stats[:, :, j] for j in (1, 2, 4, 5))
        dve.wait_ge(self.s_stats, i * TPC + TPC)
        dve.tensor_tensor(self.mean, even_mean, odd_mean, ALU.add).then_inc(self.s_step, 1)
        dve.tensor_tensor(self.gap, even_mean, odd_mean, ALU.subtract).then_inc(self.s_step, 1)
        dve.tensor_tensor(self.m2, even_m2, odd_m2, ALU.add).then_inc(self.s_step, 1)
        dve.wait_ge(self.s_step, i * 6 + 3)
        dve.tensor_scalar(self.mean, self.mean, 0.5, None, ALU.mult).then_inc(self.s_step, 1)
        dve.scalar_tensor_tensor(self.gap, self.gap, 0.25, self.gap, ALU.mult, ALU.mult).then_inc(self.s_step, 1)
        dve.tensor_scalar(self.m2, self.m2, 1.0 / D, None, ALU.mult).then_inc(self.s_step, 1)
        dve.wait_ge(self.s_step, i * 6 + 6)
        dve.tensor_tensor(self.var, self.m2, self.gap, ALU.add).then_inc(self.s_var, 1)

    def root(self, act, i, eps):
        act.wait_ge(self.s_var, i + 1)
        if since(i, 1):
            act.wait_ge(self.s_done, i * TPC)
        act.activation(self.rstd[:, :], self.var, ACT.Sqrt, bias=eps).then_inc(self.s_std, 1)

    def apply(self, dve, i, out, rows):
        dve.wait_ge(self.s_std, i + 1)
        dve.reciprocal(self.rstd[:, :], self.rstd[:, :]).then_inc(self.s_rstd, 1)
        dve.wait_ge(self.s_rstd, i + 1)
        for t in range(TPC):
            dve.tensor_scalar(out(t), rows[:, t], self.mean[:, t:t + 1], self.rstd[:, t:t + 1],
                              ALU.subtract, ALU.mult).then_inc(self.s_done, 1)


def turn_rows(pe, out, rows, ident):
    for t in range(TPC):
        for k in range(DK):
            mm = pe.transpose(out[:, k, t * P:(t + 1) * P], rows[:, t, k * P:(k + 1) * P], ident)
    return mm


def multiply_rows(pe, out, turned, weight):
    for t in range(TPC):
        for k in range(DK):
            mm = pe.matmul(out[:, t], turned[:, k, t * P:(t + 1) * P], weight[:, k],
                           start=(k == 0), stop=(k == DK - 1))
    return mm


def route(nc, x, attn_rows, Wo, Wg, bg, W1, W3, W2, b1, b3, b2, keep, sorted_rows):
    x1, weight, tile_expert, tile_in, tile_number, w1, w3, w2, bias1, bias3, bias2 = keep
    with ExitStack() as stack:
        n = Names(nc, stack, "route")
        ident = n.sb("ident", [P, P])
        before = n.sb("before", [P, P], BF16)
        ones = n.sb("ones", [P, P], BF16)
        eps = n.sb("eps", [P, 1])
        zeros = n.sb("zeros", [P, ROW])
        wo = n.sb("wo", [P, DK, D])
        wg = n.sb("wg", [P, DK, NE])
        bias_g = n.sb("bias_g", [P, NE])
        a_rows = n.sb("a_rows", [P, 2, TPC, D])
        a_t = n.sb("a_t", [P, DK, CH])
        x_rows = n.sb("x_rows", [P, 2, TPC, D])
        res = n.sb("res", [P, TPC, D])
        x1_t = n.sb("x1_t", [P, DK, CH])
        norm = Norm(n)
        gates = n.sb("gates", [P, TPC, NE])
        rest = n.sb("rest", [P, TPC, NE])
        top = n.sb("top", [P, TPC])
        same = n.sb("same", [P, TPC, NE])
        col = n.sb("col", [P, TPC])
        hot = n.sb("hot", [P, 2, TOPK, TPC, NE])
        chosen_place = n.sb("chosen_place", [P, TOPK, TPC])
        places = n.sb("places", [P, TOPK, NT], U32)
        both = n.sb("both", [P, 2, TPC, NE], BF16)
        place = n.sb("place", [P, TPC, NE])
        picked = n.sb("picked", [P, TOPK, TPC, NE])
        number = n.sb("number", [P, NE])
        starts = n.sb("starts", [P, NE])
        reached = n.sb("reached", [P, NE])
        pad_places = n.sb("pad_places", [1, NE], I32)
        count = n.sb("count", [P, NE])
        token = n.sb("token", [P, NT])
        tiles_i = n.sb("tiles_i", [P, NE], I32)
        tiles = n.sb("tiles", [P, NE])
        ends = n.sb("ends", [P, NE])
        ones_f = n.sb("ones_f", [P, NE])
        tile_no = n.sb("tile_no", [P, SLOT_TILES])
        owner = n.sb("owner", [P, SLOT_TILES])
        moved = n.sb("moved", [P, SLOT_TILES])
        passed = x1_t[:, :].rearrange("p k c -> p (k c)")[:, 0:SLOT_TILES * NE].rearrange("p (t e) -> p t e", e=NE)
        ps_a = n.ps("ps_a", [P, DK, CH])
        ps_y = n.ps("ps_y", [P, TPC, D])
        ps_n = n.ps("ps_n", [P, DK, CH])
        ps_g = n.ps("ps_g", [P, TPC, NE])
        ps_c = n.ps("ps_c", [P, TPC + 1, NE])

        s_made = n.sem("constants_begun")
        s_const = n.sem("constants")
        s_w = n.sem("weights_loaded")
        s_expert = n.sem("expert_weights_loaded")
        s_in = [n.sem(f"rows_loaded{i}") for i in range(2)]
        s_ap = n.sem("attention_turned")
        s_at = n.sem("attention_t_ready")
        s_y = n.sem("projected")
        s_res = n.sem("residual_ready")
        s_np = n.sem("x1_turned")
        s_nt = n.sem("x1_t_ready")
        s_g = n.sem("gates_projected")
        s_step = n.sem("routing_step")
        s_shift = n.sem("logits_shifted")
        s_e = n.sem("gates_exp")
        s_hot = n.sem("experts_chosen")
        s_count = n.sem("counts_ready")
        s_place = n.sem("places_ready")
        s_token = n.sem("tokens_placed")
        s_pad = n.sem("pad_places_ready")
        s_put = n.sem("rows_put")
        block = stack.enter_context(nc.Block())

        CONSTS = 13
        rows_a = attn_rows.rearrange("(c t p) d -> c p t d", t=TPC, p=P)
        rows_in = x.rearrange("b (c t p) d -> (b c) p t d", p=P, t=TPC)

        @block.sync
        def _(sp):
            sp.dma_start(wo[:, :], Wo.rearrange("(k p) n -> p k n", p=P)).then_inc(s_w, 16)
            sp.dma_start(wg[:, :], Wg.rearrange("(k p) n -> p k n", p=P)).then_inc(s_w, 16)
            sp.dma_start(bias_g[:, :], bg.partition_broadcast(P)).then_inc(s_w, 16)
            later = [(dst[:, k], src[:, k * P:(k + 1) * P].rearrange("e p h -> p e h"))
                     for dst, src, tiles_k in ((w1, W1, DK), (w3, W3, DK), (w2, W2, HK)) for k in range(tiles_k)]
            later += [(dst[:, :].rearrange("p e h -> p (e h)"), src.rearrange("e h -> (e h)").partition_broadcast(P))
                      for dst, src in ((bias1, b1), (bias3, b3), (bias2, b2))]
            loads = len(later)

            for i in range(NCH):
                p = i % 2
                if i >= 2:
                    sp.wait_ge(s_ap, i - 1)
                    sp.wait_ge(s_res, i - 1)
                sp.dma_start(a_rows[:, p], rows_a[i]).then_inc(s_in[p], 16)
                sp.dma_start(x_rows[:, p], rows_in[i]).then_inc(s_in[p], 16)
                while i >= 1 and len(later) > loads * (NCH - 1 - i) // (NCH - 1):
                    sp.dma_start(*later.pop(0)).then_inc(s_expert, 16)
            sp.wait_ge(s_pad, 1)
            sp.wait_ge(s_const, CONSTS)
            for e in range(NE):
                first = sp.value_load(pad_places[0:1, e:e + 1], min_val=e * REGION_TILES * P, max_val=(e * REGION_TILES + NT) * P)
                sp.dma_start(sorted_rows[bass.ds(first, P)], zeros[:, :]).then_inc(s_expert, 16)
            sp.wait_ge(s_expert, 16 * (loads + NE))

        @block.tensor
        def _(pe):
            pe.wait_ge(s_const, CONSTS)
            pe.wait_ge(s_w, 16 * 3)

            def turn_attention(i, p):
                pe.wait_ge(s_in[p], 32 * ((i >> 1) + 1))
                if since(i, 1):
                    pe.wait_ge(s_at, i)
                turn_rows(pe, ps_a, a_rows[:, p], ident[:, :]).then_inc(s_ap, 1)

            def project(i, p):
                pe.wait_ge(s_at, i + 1)
                if since(i, 1):
                    pe.wait_ge(s_res, i)
                multiply_rows(pe, ps_y, a_t, wo).then_inc(s_y, 1)

            def turn_x1(i, p):
                pe.wait_ge(norm.s_done, i * TPC + TPC)
                if since(i, 1):
                    pe.wait_ge(s_nt, i)
                turn_rows(pe, ps_n, x1[:, i * TPC:i * TPC + TPC, 0:D], ident[:, :]).then_inc(s_np, 1)

            def project_gates(i, p):
                pe.wait_ge(s_nt, i + 1)
                if since(i, 1):
                    pe.wait_ge(s_shift, i)
                multiply_rows(pe, ps_g, x1_t, wg).then_inc(s_g, 1)

            def count_before(i, p):
                pe.wait_ge(s_hot, i + 1)
                if since(i, 1):
                    pe.wait_ge(s_place, i)
                for t in range(TPC + 1):
                    if t < TPC:
                        mm = pe.matmul(ps_c[:, t], before[:, :], both[:, p, t], start=True, stop=(t == 0))
                    for u in range(t):
                        mm = pe.matmul(ps_c[:, t], ones[:, :], both[:, p, u], start=(t == TPC and u == 0), stop=(u == t - 1))
                mm.then_inc(s_count, 1)
            pipelined(pe, NCH, [(project, 1), (project_gates, 3), (turn_attention, 0), (count_before, 4), (turn_x1, 2)])

        @block.scalar
        def _(act):
            act.wait_ge(s_const, CONSTS)

            def keep_attention(i, p):
                act.wait_ge(s_ap, i + 1)
                if since(i, 1):
                    act.wait_ge(s_y, i)
                act.copy(a_t[:, :], ps_a[:, :]).then_inc(s_at, 1)

            def keep_x1_t(i, p):
                act.wait_ge(s_np, i + 1)
                if since(i, 1):
                    act.wait_ge(s_g, i)
                act.copy(x1_t[:, :], ps_n[:, :]).then_inc(s_nt, 1)

            def exponential(i, p):
                act.wait_ge(s_shift, i + 1)
                act.activation(gates[:, :], gates[:, :], ACT.Exp).then_inc(s_e, 1)
            pipelined(act, NCH, [
                (exponential, 3),
                (keep_attention, 0),
                (keep_x1_t, 2),
                (lambda i, p: norm.root(act, i, eps[:, 0:1]), 1)])

        @block.vector
        def _(dve):
            dve.wait_ge(s_w, 16 * 3)
            dve.wait_ge(s_const, CONSTS)
            dve.tensor_copy(x1[:, :, TOKEN], token[:, :]).then_inc(s_token, 1)
            done = [0]

            def step(instruction):
                done[0] += 1
                instruction.then_inc(s_step, 1)
                dve.wait_ge(s_step, done[0])
            per_row = lambda a: a.rearrange("p (t o) -> p t o", o=1).to_broadcast([P, TPC, NE])
            per_expert = lambda a: a.rearrange("p (o e) -> p o e", o=1).to_broadcast([P, TPC, NE])

            def residual(i, p):
                dve.wait_ge(s_y, i + 1)
                if since(i, 1):
                    dve.wait_ge(norm.s_done, i * TPC)
                dve.tensor_tensor(res[:, :], ps_y[:, :], x_rows[:, p], ALU.add).then_inc(s_res, 1)
                dve.wait_ge(s_res, i + 1)
                norm.statistics(dve, i, res)

            def normalise(i, p):
                norm.apply(dve, i, lambda t: x1[:, i * TPC + t, 0:D], res)

            def shift_logits(i, p):
                dve.wait_ge(s_g, i + 1)
                step(dve.tensor_tensor(gates[:, :], ps_g[:, :], per_expert(bias_g[:, :]), ALU.add))
                step(dve.tensor_reduce(col[:, :], gates[:, :], AX.X, ALU.max))
                dve.tensor_tensor(gates[:, :], gates[:, :], per_row(col[:, :]), ALU.subtract).then_inc(s_shift, 1)

            def choose(i, p):
                mine = slice(i * TPC, i * TPC + TPC)
                dve.wait_ge(s_e, i + 1)
                step(dve.tensor_reduce(col[:, :], gates[:, :], AX.X, ALU.add))
                step(dve.reciprocal(col[:, :], col[:, :]))
                step(dve.tensor_tensor(gates[:, :], gates[:, :], per_row(col[:, :]), ALU.mult))
                for r in range(TOPK):
                    left = (gates, rest)[r]
                    step(dve.tensor_reduce(top[:, :], left[:, :], AX.X, ALU.max))
                    step(dve.tensor_copy(weight[:, r, mine], top[:, :]))
                    step(dve.tensor_tensor(same[:, :], left[:, :], per_row(top[:, :]), ALU.is_equal))
                    step(dve.tensor_tensor(same[:, :], same[:, :], per_expert(number[:, :]), ALU.mult))
                    step(dve.tensor_reduce(col[:, :], same[:, :], AX.X, ALU.max))
                    step(dve.tensor_tensor(hot[:, p, r], per_expert(number[:, :]), per_row(col[:, :]), ALU.is_equal))
                    if r == 0:
                        step(dve.tensor_copy(x1[:, mine, FIRST_EXPERT], col[:, :]))
                        step(dve.scalar_tensor_tensor(flat(rest[:, :]), flat(hot[:, p, r]), -2.0, flat(gates[:, :]), ALU.mult, ALU.add))
                dve.tensor_tensor(both[:, p], hot[:, p, 0], hot[:, p, 1], ALU.add).then_inc(s_hot, 1)

            def give_places(i, p):
                mine = slice(i * TPC, i * TPC + TPC)
                dve.wait_ge(s_count, i + 1)
                step(dve.tensor_tensor(place[:, :], ps_c[:, 0:TPC], per_expert(reached[:, :]), ALU.add))
                step(dve.tensor_tensor(reached[:, :], reached[:, :], ps_c[:, TPC], ALU.add))
                step(dve.tensor_tensor(picked[:, :], hot[:, p], place[:, :].rearrange("p (o t) e -> p o t e", o=1).to_broadcast([P, TOPK, TPC, NE]),
                                       ALU.mult))
                step(dve.tensor_reduce(chosen_place[:, :], picked[:, :], AX.X, ALU.add))
                dve.tensor_copy(places[:, :, mine], chosen_place[:, :]).then_inc(s_place, 1)

            pipelined(dve, NCH, [(normalise, 2), (residual, 1), (shift_logits, 3), (give_places, 4), (choose, 3)])

            dve.tensor_copy(pad_places[:, :], reached[0:1, :]).then_inc(s_pad, 1)
            step(dve.tensor_tensor(count[:, :], reached[:, :], starts[:, :], ALU.subtract))
            step(dve.tensor_scalar(tiles_i[:, :], count[:, :], float(P - 1), None, ALU.add))
            step(dve.tensor_scalar(tiles_i[:, :], tiles_i[:, :], P.bit_length() - 1, None, ALU.logical_shift_right))
            step(dve.tensor_copy(tiles[:, :], tiles_i[:, :]))
            step(dve.tensor_tensor_scan(ends[:, :], ones_f[:, :], tiles[:, :], 0.0, ALU.mult, ALU.add))
            every = [P, SLOT_TILES, NE]
            step(dve.tensor_tensor(passed[:, :], tile_no[:, :].rearrange("p (t o) -> p t o", o=1).to_broadcast(every),
                                   ends[:, :].rearrange("p (o e) -> p o e", o=1).to_broadcast(every), ALU.is_ge))
            step(dve.tensor_reduce(owner[:, :], passed[:, :], AX.X, ALU.add))
            step(dve.tensor_scalar(tile_expert[:, :], owner[0:1, :], float(NE - 1), None, ALU.min))
            step(dve.tensor_scalar(tile_number[:, :], owner[:, :], 1.0, None, ALU.add))
            step(dve.tensor_scalar(tiles[:, :], tiles[:, :], -1.0, float(REGION_TILES), ALU.mult, ALU.add))
            step(dve.tensor_tensor(passed[:, :], passed[:, :], tiles[:, :].rearrange("p (o e) -> p o e", o=1).to_broadcast(every), ALU.mult))
            step(dve.tensor_reduce(moved[:, :], passed[:, :], AX.X, ALU.add))
            step(dve.tensor_tensor(moved[:, :], moved[:, :], tile_no[:, :], ALU.add))
            step(dve.tensor_scalar(tile_in[:, :], moved[0:1, :], float(NE * REGION_TILES), None, ALU.min))

        @block.gpsimd
        def _(pool):
            identity(pool, ident[:, :], s_made, s_const)
            pool.memset(eps[:, :], LN_EPS).then_inc(s_const, 1)
            pool.memset(zeros[:, 0:TOKEN], 0.0).then_inc(s_const, 1)
            pool.memset(zeros[:, TOKEN:TOKEN + 1], NO_TOKEN).then_inc(s_const, 1)
            pool.memset(zeros[:, FIRST_EXPERT:ROW], 0.0).then_inc(s_const, 1)
            pool.iota(token[:, :], [[P, NT]], base=0, channel_multiplier=1, allow_small_or_imprecise_dtypes=True).then_inc(s_const, 1)
            pool.memset(ones[:, :], 1.0).then_inc(s_const, 1)
            pool.memset(ones_f[:, :], 1.0).then_inc(s_const, 1)
            pool.memset(before[:, :], 1.0).then_inc(s_made, 1)
            pool.wait_ge(s_made, 2)
            pool.affine_select(out=before[:, :], in_=before[:, :], compare_op=ALU.is_gt, fill=0.0, base=0,
                               pattern=[[1, P]], channel_multiplier=-1).then_inc(s_const, 1)
            inexact = dict(allow_small_or_imprecise_dtypes=True)
            pool.iota(number[:, :], [[1, NE]], base=1, channel_multiplier=0, **inexact).then_inc(s_const, 1)
            pool.iota(tile_no[:, :], [[1, SLOT_TILES]], base=0, channel_multiplier=0, **inexact).then_inc(s_const, 1)
            for tile in (starts, reached):
                pool.iota(tile[:, :], [[REGION_TILES * P, NE]], base=0, channel_multiplier=0, **inexact).then_inc(s_const, 1)

            def put(index, rows):
                pool.indirect_dma_start(out=sorted_rows, out_offset=bass.IndirectOffsetOnAxis(ap=index, axis=0),
                                        in_=rows, in_offset=None).then_inc(s_put, 16)
            pool.wait_ge(s_const, CONSTS)
            pool.dma_start(sorted_rows[NE * REGION_TILES * P:(NE * REGION_TILES + 1) * P], zeros[:, :]).then_inc(s_put, 16)
            pool.wait_ge(s_token, 1)
            for i in range(NCH):
                pool.wait_ge(s_place, i + 1)
                for t in range(i * TPC, i * TPC + TPC):
                    for r in range(TOPK):
                        put(places[:, r, t:t + 1], x1[:, t])
            pool.wait_ge(s_put, 16 * (1 + TOPK * NT))


def experts(nc, bf, x1, tile_expert, tile_in, tile_number, w1, w3, w2, bias1, bias3, bias2, sorted_rows, expert_rows):
    with ExitStack() as stack:
        n = Names(nc, stack, "exp")
        ident = n.sb("ident", [P, P])
        bias_f = n.sb("bias_f", [P, D])
        own_places = n.sb("own_places", [P, SLOT_TILES])
        second = n.sb("second", [P, 4])
        dest = n.sb("dest", [P, 4], U32)
        rows = n.sb("rows", [P, 4, ROW])
        rows_t = n.sb("rows_t", [P, 2, DK, P])
        left = n.sb("left", [P, 2, HID])
        right = n.sb("right", [P, 2, HID])
        product = n.sb("product", [P, 2, HID])
        hidden = n.sb("hidden", [P, 2, HID])
        hidden_t = n.sb("hidden_t", [P, 2, HK, P])
        result = n.sb("result", [P, 4, D])
        ps_x = n.ps("ps_x", [P, DK, P])
        ps_h = [[n.ps(f"ps_h{p}{i}", [P, HID]) for i in range(2)] for p in range(2)]
        ps_t = n.ps("ps_t", [P, HK, P])
        ps_y = [n.ps(f"ps_y{p}", [P, D]) for p in range(2)]

        s_made = n.sem("constants_begun")
        s_const = n.sem("constants")
        s_bf = n.sem("last_bias_loaded")
        s_x1 = n.sem("x1_biased")
        s_second = n.sem("second_expert_known")
        s_dest = n.sem("destinations_ready")
        s_seen = n.sem("result_seen")
        s_x = [n.sem(f"rows_loaded{i}") for i in range(4)]
        s_xp = n.sem("rows_turned")
        s_xt = n.sem("rows_t_ready")
        s_h = n.sem("hidden_projected")
        s_lr = n.sem("factors_ready")
        s_prod = n.sem("product_ready")
        s_act = n.sem("hidden_ready")
        s_hp = n.sem("hidden_turned")
        s_ht = n.sem("hidden_t_ready")
        s_y = n.sem("result_projected")
        s_r = n.sem("result_ready")
        s_out = [n.sem(f"result_stored{i}") for i in range(4)]
        block = stack.enter_context(nc.Block())

        rows_in = sorted_rows.rearrange("(s p) d -> s p d", p=P)

        def entry(eng, table, s, most):
            cell = table[0:1, s:s + 1] if isinstance(s, int) else table[0:1, bass.ds(s, 1)]
            return eng.value_load(cell, min_val=0, max_val=most)

        def expert(eng, s):
            return entry(eng, tile_expert, s, NE - 1)

        def of_expert(tile, e):
            return tile[:, bass.ds(e, 1)].rearrange("p o h -> p (o h)")

        @block.sync
        def _(sp):
            sp.dma_start(bias_f[:, :], bf.partition_broadcast(P)).then_inc(s_bf, 16)

            def load(s, p):
                if since(s, 4):
                    sp.wait_ge(s_xp, s - 3)
                    sp.wait_ge(s_dest, s - 3)
                sp.dma_start(rows[:, p], at(rows_in, entry(sp, tile_in, s, NE * REGION_TILES))).then_inc(s_x[p], 16)
            pipelined(sp, SLOT_TILES, [(load, 2)], body=4)

        @block.tensor
        def _(pe):
            pe.wait_ge(s_const, 1)

            def turn_in(s, p):
                pe.wait_ge(s_x[p], 16 * ((s >> 2) + 1))
                if since(s, 1):
                    pe.wait_ge(s_xt, s)
                for k in range(DK):
                    mm = pe.transpose(ps_x[:, k], rows[:, p, k * P:(k + 1) * P], ident[:, :])
                mm.then_inc(s_xp, 1)

            def project(s, p):
                p = p % 2
                e = expert(pe, s)
                pe.wait_ge(s_xt, s + 1)
                if since(s, 2):
                    pe.wait_ge(s_lr, 2 * (s - 1))
                for i, w in enumerate((w1, w3)):
                    for k in range(DK):
                        mm = pe.matmul(ps_h[p][i][:, :], rows_t[:, p, k], of_expert(w[:, k], e), start=(k == 0), stop=(k == DK - 1))
                    mm.then_inc(s_h, 1)

            def turn_hidden(s, p):
                pe.wait_ge(s_act, s + 1)
                if since(s, 1):
                    pe.wait_ge(s_ht, s)
                for k in range(HK):
                    mm = pe.transpose(ps_t[:, k], hidden[:, p % 2, k * P:(k + 1) * P], ident[:, :])
                mm.then_inc(s_hp, 1)

            def project_out(s, p):
                p = p % 2
                e = expert(pe, s)
                pe.wait_ge(s_ht, s + 1)
                if since(s, 2):
                    pe.wait_ge(s_r, s - 1)
                for k in range(HK):
                    mm = pe.matmul(ps_y[p][:, :], hidden_t[:, p, k], of_expert(w2[:, k], e), start=(k == 0), stop=(k == HK - 1))
                mm.then_inc(s_y, 1)
            pipelined(pe, SLOT_TILES, [(project, 1), (turn_in, 0), (project_out, 3), (turn_hidden, 2)], body=4)

        @block.vector
        def _(dve):
            dve.wait_ge(s_const, 2)

            def keep_rows(s, p):
                p = p % 2
                dve.wait_ge(s_xp, s + 1)
                if since(s, 2):
                    dve.wait_ge(s_h, 2 * (s - 1))
                dve.tensor_copy(rows_t[:, p], ps_x[:, :]).then_inc(s_xt, 1)

            def find_places(s, p):
                column = (lambda table: table[:, s:s + 1]) if isinstance(s, int) else (lambda table: table[:, bass.ds(s, 1)])
                dve.wait_ge(s_x[p], 16 * ((s >> 2) + 1))
                dve.tensor_scalar(second[:, p:p + 1], rows[:, p, FIRST_EXPERT:ROW], column(tile_number), float(T),
                                  ALU.not_equal, ALU.mult).then_inc(s_second, 1)
                dve.wait_ge(s_second, s + 1)
                if since(s, 4):
                    dve.wait_ge(s_out[p], 16 * (s >> 2))
                dve.scalar_tensor_tensor(dest[:, p:p + 1], rows[:, p, TOKEN:TOKEN + 1], second[:, p:p + 1], column(own_places),
                                         ALU.add, ALU.min).then_inc(s_dest, 1)

            def multiply(s, p):
                p = p % 2
                e = expert(dve, s)
                if since(s, 2):
                    dve.wait_ge(s_prod, s - 1)
                dve.wait_ge(s_h, 2 * s + 1)
                dve.tensor_tensor(left[:, p], ps_h[p][0][:, :], of_expert(bias1, e), ALU.add).then_inc(s_lr, 1)
                dve.wait_ge(s_h, 2 * s + 2)
                dve.tensor_tensor(right[:, p], ps_h[p][1][:, :], of_expert(bias3, e), ALU.add).then_inc(s_lr, 1)
                dve.wait_ge(s_lr, 2 * s + 2)
                if since(s, 2):
                    dve.wait_ge(s_act, s - 1)
                dve.tensor_tensor(product[:, p], left[:, p], right[:, p], ALU.mult).then_inc(s_prod, 1)

            def keep_result(s, p):
                e = expert(dve, s)
                dve.wait_ge(s_y, s + 1)
                if since(s, 4):
                    dve.wait_ge(s_out[p], 16 * (s >> 2))
                dve.tensor_tensor(result[:, p], ps_y[p % 2][:, :], of_expert(bias2, e), ALU.add).then_inc(s_r, 1)
            pipelined(dve, SLOT_TILES, [(multiply, 1), (keep_rows, 0), (keep_result, 3), (find_places, 2)], body=4)

        @block.scalar
        def _(act):
            def activate(s, p):
                p = p % 2
                act.wait_ge(s_prod, s + 1)
                if since(s, 2):
                    act.wait_ge(s_hp, s - 1)
                act.activation(hidden[:, p], product[:, p], ACT.Silu).then_inc(s_act, 1)

            def keep_hidden(s, p):
                p = p % 2
                act.wait_ge(s_hp, s + 1)
                if since(s, 2):
                    act.wait_ge(s_y, s - 1)
                act.copy(hidden_t[:, p], ps_t[:, :]).then_inc(s_ht, 1)
            pipelined(act, SLOT_TILES, [(activate, 1), (keep_hidden, 2)], body=4)

        @block.gpsimd
        def _(pool):
            identity(pool, ident[:, :], s_made, s_const)

            pool.iota(own_places[:, :], [[P, SLOT_TILES]], base=TOPK * T, channel_multiplier=1,
                      allow_small_or_imprecise_dtypes=True).then_inc(s_const, 1)
            pool.wait_ge(s_bf, 16)
            for c in range(NCH):
                x1_chunk = x1[:, c * TPC:(c + 1) * TPC, 0:D]
                pool.tensor_tensor(x1_chunk, x1_chunk, bias_f[:, :].rearrange("p (o d) -> p o d", o=1).to_broadcast([P, TPC, D]),
                                   ALU.add).then_inc(s_x1, 1)
            pool.wait_ge(s_x1, NCH)

            def store(s, p):
                pool.wait_ge(s_r, s + 1)
                pool.wait_ge(s_dest, s + 1)
                pool.sem_inc(s_seen, 1)
                pool.indirect_dma_start(out=expert_rows, out_offset=bass.IndirectOffsetOnAxis(ap=dest[:, p:p + 1], axis=0),
                                        in_=result[:, p], in_offset=None).then_inc(s_out[p], 16)
            pipelined(pool, SLOT_TILES, [(store, 2)], body=4)
            for p in range(4):
                pool.wait_ge(s_out[p], 16 * SLOT_TILES // 4)


def finish(nc, Wf, x1, weight, expert_rows, out):
    with ExitStack() as stack:
        n = Names(nc, stack, "fin")
        ident = n.sb("ident", [P, P])
        eps = n.sb("eps", [P, 1])
        wf = n.sb("wf", [P, DK, D])
        picked = n.sb("picked", [P, 2, TOPK, TPC, D])
        mixed = n.sb("mixed", [P, 2, TPC, D])
        mixed_t = n.sb("mixed_t", [P, 2, DK, CH])
        res = n.sb("res", [P, TPC, D])
        normed = n.sb("normed", [P, 2, TPC, D])
        norm = Norm(n)
        ps_m = n.ps("ps_m", [P, DK, CH])
        ps_y = [n.ps(f"ps_y{p}", [P, TPC, D]) for p in range(2)]

        s_made = n.sem("constants_begun")
        s_const = n.sem("constants")
        s_w = n.sem("weights_loaded")
        s_pick = [n.sem(f"rows_picked{i}") for i in range(2)]
        s_first = n.sem("first_weighted")
        s_mix = n.sem("rows_mixed")
        s_mp = n.sem("mixed_turned")
        s_mt = n.sem("mixed_t_ready")
        s_y = n.sem("projected")
        s_res = n.sem("residual_ready")
        s_out = [n.sem(f"rows_stored{i}") for i in range(2)]
        block = stack.enter_context(nc.Block())

        rows_out = out.rearrange("b (c t p) d -> (b c) p t d", p=P, t=TPC)
        rows_in = [expert_rows[r * T:(r + 1) * T].rearrange("(c t p) d -> c p t d", p=P, t=TPC) for r in range(TOPK)]

        @block.sync
        def _(sp):
            sp.dma_start(wf[:, :], Wf.rearrange("(k p) n -> p k n", p=P)).then_inc(s_w, 16)

            def load(i, p):
                if since(i, 2):
                    sp.wait_ge(s_mix, (i - 1) * TPC)
                for r in range(TOPK):
                    sp.dma_start(picked[:, p, r], at(rows_in[r], i)).then_inc(s_pick[p], 16)
            pipelined(sp, NCH, [(load, 0)])

        @block.gpsimd
        def _(pool):
            identity(pool, ident[:, :], s_made, s_const)
            pool.memset(eps[:, :], LN_EPS).then_inc(s_const, 1)

            def store(i, p):
                pool.wait_ge(norm.s_done, i * TPC + TPC)
                pool.dma_start(at(rows_out, i), normed[:, p]).then_inc(s_out[p], 16)
            pipelined(pool, NCH, [(store, 0)])
            for p in range(2):
                pool.wait_ge(s_out[p], 16 * NCH // 2)

        @block.tensor
        def _(pe):
            pe.wait_ge(s_const, 2)
            pe.wait_ge(s_w, 16)

            def turn(i, p):
                pe.wait_ge(s_mix, i * TPC + TPC)
                if since(i, 1):
                    pe.wait_ge(s_mt, i)
                turn_rows(pe, ps_m, mixed[:, p], ident[:, :]).then_inc(s_mp, 1)

            def project(i, p):
                pe.wait_ge(s_mt, i + 1)
                if since(i, 2):
                    pe.wait_ge(s_res, i - 1)
                multiply_rows(pe, ps_y[p], mixed_t[:, p], wf).then_inc(s_y, 1)
            pipelined(pe, NCH, [(turn, 0), (project, 1)])

        @block.scalar
        def _(act):
            act.wait_ge(s_const, 2)

            def keep_mixed(i, p):
                act.wait_ge(s_mp, i + 1)
                if since(i, 2):
                    act.wait_ge(s_y, i - 1)
                act.copy(mixed_t[:, p], ps_m[:, :]).then_inc(s_mt, 1)
            pipelined(act, NCH, [(keep_mixed, 0), (lambda i, p: norm.root(act, i, eps[:, 0:1]), 2)])

        @block.vector
        def _(dve):
            def mix(i, p):
                dve.wait_ge(s_pick[p], 16 * TOPK * ((i >> 1) + 1))
                if since(i, 2):
                    dve.wait_ge(s_mp, i - 1)
                gate = lambda r, t: weight[:, r, i * TPC + t:i * TPC + t + 1] if isinstance(i, int) else weight[:, r, bass.ds(i * TPC + t, 1)]
                for t in range(TPC):
                    dve.tensor_scalar(mixed[:, p, t], picked[:, p, 0, t], gate(0, t), None, ALU.mult).then_inc(s_first, 1)
                for t in range(TPC):
                    dve.wait_ge(s_first, i * TPC + (t + 1))
                    dve.scalar_tensor_tensor(mixed[:, p, t], picked[:, p, 1, t], gate(1, t), mixed[:, p, t],
                                             ALU.mult, ALU.add).then_inc(s_mix, 1)

            def residual(i, p):
                dve.wait_ge(s_y, i + 1)
                if since(i, 1):
                    dve.wait_ge(norm.s_done, i * TPC)
                x1_chunk = x1[:, i * TPC:i * TPC + TPC, 0:D] if isinstance(i, int) else x1[:, bass.ds(i * TPC, TPC), 0:D]
                dve.tensor_tensor(res[:, :], ps_y[p][:, :], x1_chunk, ALU.add).then_inc(s_res, 1)
                dve.wait_ge(s_res, i + 1)
                norm.statistics(dve, i, res)

            def normalise(i, p):
                if since(i, 2):
                    dve.wait_ge(s_out[p], 16 * (i >> 1))
                norm.apply(dve, i, lambda t: normed[:, p, t], res)
            pipelined(dve, NCH, [(mix, 0), (normalise, 3), (residual, 2)])


def program(nc, x, Wq, Wk, Wv, Wo, Wqp, Wkp, lambda_raw, W1, b1, W3, b3, W2, b2, Wg, bg, Wf, bf, out):
    scratch = lambda name, shape: nc.dram_tensor(name, shape, F32).ap()
    q_parts = scratch("q_parts", [NCH, 6, NQ, HD, QUAD, CH])
    k_parts = scratch("k_parts", [NCH, 6, NQ, HD, QUAD, CH])
    v_rows = scratch("v_rows", [T, H * VW])
    attn_rows = scratch("attn_rows", [T, D])
    sorted_rows = scratch("sorted_rows", [(NE * REGION_TILES + 1) * P, ROW])
    expert_rows = scratch("expert_rows", [TOPK * T + SLOT_TILES * P, D])
    prepare(nc, x, Wq, Wk, Wv, Wqp, Wkp, lambda_raw, q_parts, k_parts, v_rows)
    attend(nc, q_parts, k_parts, v_rows, attn_rows)
    with ExitStack() as stack:
        n = Names(nc, stack, "keep")
        x1 = n.sb("x1", [P, NT, ROW])
        weight = n.sb("weight", [P, TOPK, NT])
        tables = [n.sb("tile_expert", [1, SLOT_TILES], I32), n.sb("tile_in", [1, SLOT_TILES], I32),
                  n.sb("tile_number", [P, SLOT_TILES])]
        with ExitStack() as weights:
            m = Names(nc, weights, "keep")
            w1 = m.sb("w1", [P, DK, NE, HID])
            w3 = m.sb("w3", [P, DK, NE, HID])
            w2 = m.sb("w2", [P, HK, NE, D])
            bias1 = m.sb("bias1", [P, NE, HID])
            bias3 = m.sb("bias3", [P, NE, HID])
            bias2 = m.sb("bias2", [P, NE, D])
            route(nc, x, attn_rows, Wo, Wg, bg, W1, W3, W2, b1, b3, b2,
                  (x1, weight, *tables, w1, w3, w2, bias1, bias3, bias2), sorted_rows)
            experts(nc, bf, x1, *tables, w1, w3, w2, bias1, bias3, bias2, sorted_rows, expert_rows)
        finish(nc, Wf, x1, weight, expert_rows, out)


_INS = ['L0_attn_x', 'L0_attn_Wq', 'L0_attn_Wk', 'L0_attn_Wv', 'L0_attn_Wo', 'L0_attn_Wqp', 'L0_attn_Wkp',
        'L0_attn_lambda_raw', 'L0_ffn_W1', 'L0_ffn_b1', 'L0_ffn_W3', 'L0_ffn_b3', 'L0_ffn_W2', 'L0_ffn_b2',
        'L0_ffn_Wg', 'L0_ffn_bg', 'L0_ffn_Wf', 'L0_ffn_bf']


def kernel(**inputs):
    import numpy as _np
    import concourse.bacc as _bacc
    from concourse import mybir as _mybir
    from concourse.bass_utils import run_bass_kernel_spmd as _run

    nc = _bacc.Bacc("TRN2", target_bir_lowering=False, num_devices=1)
    arrays, args = {}, []
    for name in _INS:
        a = _np.ascontiguousarray(inputs[name])
        arrays[f"in_{name}_dram"] = a
        args.append(nc.dram_tensor(f"in_{name}_dram", a.shape, _mybir.dt.from_np(a.dtype), kind="ExternalInput").ap())
    args.append(nc.dram_tensor("out_0_dram", (B, S, D), F32, kind="ExternalOutput").ap())
    program(nc, *args)
    r = _run(nc, [arrays], core_ids=[0])
    return r.results[0]["out_0_dram"]
```
